# Optimizing a Trainium2 kernel written in Bass

```python
import numpy as np
import jax
import jax.numpy as jnp

def _softmax(x, axis=-1):
    return jax.nn.softmax(x, axis=axis)

def _gelu(x):
    return jax.nn.gelu(x, approximate=True)

def _silu(x):
    return jax.nn.silu(x)

def _sigmoid(x):
    return jax.nn.sigmoid(x)

def _layernorm(x, axis=-1, eps=1e-05):
    m = jnp.mean(x, axis=axis, keepdims=True)
    v = jnp.var(x, axis=axis, keepdims=True)
    return (x - m) / jnp.sqrt(v + eps)

def _scatter_add(tgt, idx, src, axis=0):
    return tgt.at[idx].add(src)

def _segment_sum(src, seg, n):
    return jax.ops.segment_sum(src, seg, n)
kernel_name = 'mk_adaln_ffn_d4_seqx_r8_bd9452'

def setup_inputs(seed: int=0):
    np.random.seed(seed)
    _w = jnp.asarray

    def _rec_inputs():
        import jax
        import jax.numpy as jnp
        _rk = jax.random.key(seed)
        x = 7.22e-05 + 1 * jax.random.normal(jax.random.fold_in(_rk, 1), (32, 32, 128), jnp.float32)
        _lenS = 32 - jax.random.randint(jax.random.fold_in(_rk, 7), (32,), 0, max(1, 32 // 4) + 1, jnp.int32)
        _lenS2 = 32 - jax.random.randint(jax.random.fold_in(_rk, 8), (32,), 0, max(1, 32 // 4) + 1, jnp.int32)
        cond_64 = -0.104238 + 1.01173 * jax.random.normal(jax.random.fold_in(_rk, 11), (32, 64), jnp.float32)
        fside_16xSxS_0 = -5.72187e-05 + 0.999849 * jax.random.normal(jax.random.fold_in(_rk, 12), (16, 32, 32), jnp.float32)
        _validS = jnp.arange(32)[None, :] < _lenS[:, None]
        _validS2 = jnp.arange(32)[None, :] < _lenS2[:, None]
        _causal = jnp.tril(jnp.ones((32, 32), dtype=bool))
        mask_BxS_bk0 = jnp.logical_not(jnp.broadcast_to(_validS[:, :], (32, 32)))
        mask_BxS_bf1 = jnp.ones((32, 32), dtype=bool)
        return (x, cond_64, fside_16xSxS_0, mask_BxS_bk0, mask_BxS_bf1)
    x, cond_64, fside_16xSxS_0, mask_BxS_bk0, mask_BxS_bf1 = _rec_inputs()

    def _L0_cond_setup():
        import jax, jax.numpy as jnp
        import numpy as np
        B, S, H = (4, 256, 128)
        E = 8
        M = 64
        K = 2
        N_SHARED = 2
        SM = M * N_SHARED
        G = 64
        GE_TEMP = 1.0
        ALPHA = 0.001
        SEQ_AUX = True
        NORM_TOPK = True
        COS_TEMP = 0.78
        CONS_ALPHA = 0.01
        LEAKY_SLOPE = 0.01
        EPS_COS = 1e-08

        def _leaky(x):
            return jnp.where(x >= 0, x, LEAKY_SLOPE * x)

        def _moe_forward(hidden_states, g, wt, wg, w_gate, w_up, w_down, sw_gate, sw_up, sw_down):
            b, s, h = hidden_states.shape
            x = hidden_states.reshape(-1, h)
            T = x.shape[0]
            logits_h = x @ wt.T
            logits_g = g @ wg.T
            logits_g = jnp.repeat(logits_g, s, axis=0)
            logits = (logits_h + logits_g / GE_TEMP) / (1.0 + 1.0 / GE_TEMP)
            scores = jax.nn.softmax(logits, axis=-1)
            topk_w, topk_idx = jax.lax.top_k(scores, K)
            if K > 1 and NORM_TOPK:
                topk_w = topk_w / (topk_w.sum(-1, keepdims=True) + 1e-20)
            onehot = jax.nn.one_hot(topk_idx.reshape(b, s * K), E, dtype=jnp.float32)
            ce = onehot.sum(1) / (s * K / E)
            aux_loss = (ce * scores.reshape(b, s, E).mean(1)).sum(1).mean() * ALPHA
            gp = _leaky(jnp.einsum('th,ehm->etm', x, w_gate))
            up = jnp.einsum('th,ehm->etm', x, w_up)
            y_all = jnp.einsum('etm,emh->eth', gp * up, w_down)
            y_sel = y_all[topk_idx, jnp.arange(T)[:, None], :]
            y = (y_sel * topk_w[..., None]).sum(1).reshape(b, s, h)
            p = _leaky(hidden_states @ sw_gate) * (hidden_states @ sw_up) @ sw_down
            y = y + p
            num = jnp.sum(y * p, -1)
            den = jnp.maximum(jnp.linalg.norm(y, axis=-1), EPS_COS) * jnp.maximum(jnp.linalg.norm(p, axis=-1), EPS_COS)
            closs = CONS_ALPHA * jnp.mean(num / den / (1.0 + COS_TEMP))
            return (y, aux_loss + closs)
        key = jax.random.key(seed)
        ks = jax.random.split(key, 12)
        sh = 1.0 / np.sqrt(H)
        sm = 1.0 / np.sqrt(M)
        ssm = 1.0 / np.sqrt(SM)
        sg = 1.0 / np.sqrt(G)
        return {'hidden_states': jax.random.normal(ks[0], (B, S, H), jnp.float32), 'g': jax.random.normal(ks[1], (B, G), jnp.float32), 'wt': jax.random.uniform(ks[2], (E, H), jnp.float32, -sh, sh), 'wg': jax.random.uniform(ks[3], (E, G), jnp.float32, -sg, sg), 'w_gate': jax.random.uniform(ks[4], (E, H, M), jnp.float32, -sh, sh), 'w_up': jax.random.uniform(ks[5], (E, H, M), jnp.float32, -sh, sh), 'w_down': jax.random.uniform(ks[6], (E, M, H), jnp.float32, -sm, sm), 'sw_gate': jax.random.uniform(ks[7], (H, SM), jnp.float32, -sh, sh), 'sw_up': jax.random.uniform(ks[8], (H, SM), jnp.float32, -sh, sh), 'sw_down': jax.random.uniform(ks[9], (SM, H), jnp.float32, -ssm, ssm)}
    _L0_cond_all = _L0_cond_setup()
    _L0_cond_in = {k: v for k, v in _L0_cond_all.items() if k in ('wt', 'wg', 'w_gate', 'w_up', 'w_down', 'sw_gate', 'sw_up', 'sw_down')}
    del _L0_cond_all

    def _L0_ffn_setup():
        import jax, jax.numpy as jnp
        import numpy as np
        D_MODEL = 128
        MLP_DIM = 512
        N_EXPERTS = 8
        B, T = (4, 128)
        key = jax.random.key(seed)
        ks = jax.random.split(key, 7)
        scale_in = (1.0 / D_MODEL) ** 0.5
        scale_out = (1.0 / MLP_DIM) ** 0.5
        bound_g = (1.0 / D_MODEL) ** 0.5
        w_gate = jax.random.uniform(ks[0], (D_MODEL, N_EXPERTS), minval=-bound_g, maxval=bound_g, dtype=jnp.float32)
        b_gate = jax.random.uniform(ks[1], (N_EXPERTS,), minval=-bound_g, maxval=bound_g, dtype=jnp.float32)
        W1 = jax.random.uniform(ks[2], (N_EXPERTS, D_MODEL, MLP_DIM), minval=-scale_in, maxval=scale_in, dtype=jnp.float32)
        b1 = jnp.zeros((N_EXPERTS, MLP_DIM), dtype=jnp.float32)
        W2 = jax.random.uniform(ks[3], (N_EXPERTS, MLP_DIM, D_MODEL), minval=-scale_out, maxval=scale_out, dtype=jnp.float32)
        b2 = jnp.zeros((N_EXPERTS, D_MODEL), dtype=jnp.float32)
        x = jax.random.normal(ks[4], (B, T, D_MODEL), dtype=jnp.float32)
        return {'x': x, 'w_gate': w_gate, 'b_gate': b_gate, 'W1': W1, 'b1': b1, 'W2': W2, 'b2': b2}
    _L0_ffn_all = _L0_ffn_setup()
    _L0_ffn_in = {k: v for k, v in _L0_ffn_all.items() if k in ('w_gate', 'b_gate', 'W1', 'b1', 'W2', 'b2')}
    del _L0_ffn_all

    def _L1_cond_setup():
        import jax, jax.numpy as jnp
        import numpy as np
        B, N, DIM, H, DH = (2, 256, 128, 16, 64)
        INNER = H * DH
        EPS = 1e-05

        def layernorm(x, g):
            mean = jnp.mean(x, axis=-1, keepdims=True)
            var = jnp.var(x, axis=-1, keepdims=True)
            return (x - mean) * jax.lax.rsqrt(var + EPS) * g
        key = jax.random.key(seed)
        ks = jax.random.split(key, 10)
        x = jax.random.normal(ks[0], (B, N, DIM), dtype=jnp.float32)
        attn_bias = jax.random.normal(ks[1], (H, N, N), dtype=jnp.float32)
        mask = jax.random.randint(ks[2], (B, N), 0, 2).astype(bool)
        g_in = jnp.ones((DIM,), dtype=jnp.float32)
        null_attn_bias = jax.random.normal(ks[3], (H,), dtype=jnp.float32)
        null_kv = jax.random.normal(ks[4], (2, DH), dtype=jnp.float32)
        Wq = jax.random.normal(ks[5], (DIM, INNER), dtype=jnp.float32) * 0.02
        Wkv = jax.random.normal(ks[6], (DIM, 2 * DH), dtype=jnp.float32) * 0.02
        Wo = jax.random.normal(ks[7], (INNER, DIM), dtype=jnp.float32) * 0.02
        g_out = jnp.ones((DIM,), dtype=jnp.float32)
        return {'x': x, 'attn_bias': attn_bias, 'mask': mask, 'g_in': g_in, 'null_attn_bias': null_attn_bias, 'null_kv': null_kv, 'Wq': Wq, 'Wkv': Wkv, 'Wo': Wo, 'g_out': g_out}
    _L1_cond_all = _L1_cond_setup()
    _L1_cond_in = {k: v for k, v in _L1_cond_all.items() if k in ('g_in', 'null_attn_bias', 'Wq', 'Wkv', 'Wo', 'g_out')}
    del _L1_cond_all

    def _L1_ffn_setup():
        import jax, jax.numpy as jnp
        import numpy as np
        NUM_EXPERTS = 8
        TOP_K = 2
        key = jax.random.key(seed)
        ks = jax.random.split(key, 6)
        B, S, D, F = (2, 256, 128, 512)
        E = NUM_EXPERTS
        sd = 1.0 / np.sqrt(D)
        sf = 1.0 / np.sqrt(F)
        return {'x': jax.random.normal(ks[0], (B, S, D), dtype=jnp.float32), 'gate_w': jax.random.normal(ks[1], (E, D), dtype=jnp.float32) * sd, 'w1': jax.random.uniform(ks[2], (F, E, D), dtype=jnp.float32, minval=-sd, maxval=sd), 'b1': jax.random.uniform(ks[3], (E, F), dtype=jnp.float32, minval=-sd, maxval=sd), 'w2': jax.random.uniform(ks[4], (D, E, F), dtype=jnp.float32, minval=-sf, maxval=sf), 'b2': jax.random.uniform(ks[5], (E, D), dtype=jnp.float32, minval=-sf, maxval=sf)}
    _L1_ffn_all = _L1_ffn_setup()
    _L1_ffn_in = {k: v for k, v in _L1_ffn_all.items() if k in ('gate_w', 'w1', 'b1', 'w2', 'b2')}
    del _L1_ffn_all

    def _L2_cond_setup():
        import jax, jax.numpy as jnp
        import numpy as np
        DIM = 128
        HEADS = 16
        DIM_HEAD = 64
        SCALE = 8.0

        def ln(x, g, eps=1e-05):
            mean = x.mean(axis=-1, keepdims=True)
            var = ((x - mean) ** 2).mean(axis=-1, keepdims=True)
            return (x - mean) * jax.lax.rsqrt(var + eps) * g

        def l2norm(t):
            n = jnp.maximum(jnp.linalg.norm(t, axis=-1, keepdims=True), 1e-12)
            return t / n

        def rel_pos_bias(n, w0, b0, g0, w1, b1, g1, w2, b2, dtype):
            pos = jnp.arange(-n + 1, n, dtype=dtype)[:, None]
            h = jax.nn.silu(ln(pos @ w0 + b0, g0))
            h = jax.nn.silu(ln(h @ w1 + b1, g1))
            h = h @ w2 + b2
            i = jnp.arange(n)
            idx = i[:, None] - i[None, :] + n - 1
            bias = h[idx]
            return jnp.transpose(bias, (2, 0, 1))
        key = jax.random.key(seed)
        ks = jax.random.split(key, 16)
        b, n = (2, 256)
        inner = HEADS * DIM_HEAD
        s = 0.02
        return {'x': jax.random.normal(ks[0], (b, n, DIM), jnp.float32), 'mask': jnp.ones((b, n), dtype=bool), 'g_norm': jnp.ones((DIM,), jnp.float32), 'Wq': jax.random.normal(ks[1], (DIM, inner), jnp.float32) * s, 'Wkv': jax.random.normal(ks[2], (DIM, 2 * DIM_HEAD), jnp.float32) * s, 'q_scale': jnp.ones((DIM_HEAD,), jnp.float32), 'k_scale': jnp.ones((DIM_HEAD,), jnp.float32), 'null_kv': jax.random.normal(ks[3], (2, DIM_HEAD), jnp.float32), 'null_attn_bias': jax.random.normal(ks[4], (HEADS,), jnp.float32), 'w0': jax.random.normal(ks[5], (1, DIM), jnp.float32) * s, 'b0': jnp.zeros((DIM,), jnp.float32), 'g0': jnp.ones((DIM,), jnp.float32), 'w1': jax.random.normal(ks[6], (DIM, DIM), jnp.float32) * s, 'b1': jnp.zeros((DIM,), jnp.float32), 'g1': jnp.ones((DIM,), jnp.float32), 'w2': jax.random.normal(ks[7], (DIM, HEADS), jnp.float32) * s, 'b2': jnp.zeros((HEADS,), jnp.float32), 'Wout': jax.random.normal(ks[8], (inner, DIM), jnp.float32) * s, 'g_out': jnp.ones((DIM,), jnp.float32)}
    _L2_cond_all = _L2_cond_setup()
    _L2_cond_in = {k: v for k, v in _L2_cond_all.items() if k in ('g_norm', 'Wq', 'Wkv', 'q_scale', 'k_scale', 'null_attn_bias', 'w0', 'b0', 'g0', 'w1', 'b1', 'g1', 'w2', 'b2', 'Wout', 'g_out')}
    del _L2_cond_all

    def _L2_ffn_setup():
        import jax, jax.numpy as jnp
        import numpy as np
        from jax import lax
        N_HEADS = 16
        TOP_K = 2
        N_EXPERTS = 8

        def layer_norm(x, w, b, eps=1e-05):
            mu = jnp.mean(x, axis=-1, keepdims=True)
            var = jnp.mean(jnp.square(x - mu), axis=-1, keepdims=True)
            return (x - mu) * lax.rsqrt(var + eps) * w + b

        def attention(x, w_qkv, b_qkv, w_o, b_o):
            B, T, D = x.shape
            dh = D // N_HEADS
            qkv = x @ w_qkv + b_qkv
            q, k, v = jnp.split(qkv, 3, axis=-1)
            q = q.reshape(B, T, N_HEADS, dh)
            k = k.reshape(B, T, N_HEADS, dh)
            v = v.reshape(B, T, N_HEADS, dh)
            scores = jnp.einsum('bqhd,bkhd->bhqk', q, k) / jnp.sqrt(jnp.float32(dh)).astype(x.dtype)
            probs = jax.nn.softmax(scores, axis=-1)
            ctx = jnp.einsum('bhqk,bkhd->bqhd', probs, v).reshape(B, T, D)
            return ctx @ w_o + b_o

        def moe_ff(x, w_gate, w1, b1, w2, b2):
            B, T, D = x.shape
            t = x.reshape(B * T, D)
            probs = jax.nn.softmax(t @ w_gate, axis=-1)
            tw, ti = lax.top_k(probs, TOP_K)
            tw = tw / jnp.sum(tw, axis=-1, keepdims=True)
            out = jnp.zeros_like(t)
            for e in range(N_EXPERTS):
                we = jnp.sum(jnp.where(ti == e, tw, 0.0), axis=-1)
                h = jax.nn.gelu(t @ w1[e] + b1[e]) @ w2[e] + b2[e]
                out = out + we[:, None] * h
            return out.reshape(B, T, D)
        key = jax.random.key(seed)
        ks = jax.random.split(key, 8)
        B, T, D, H, E = (4, 64, 128, 512, 8)
        s = lambda d: 1.0 / np.sqrt(d)
        return {'x': jax.random.normal(ks[0], (B, T, D), jnp.float32), 'ln1_w': jnp.ones((D,), jnp.float32), 'ln1_b': jnp.zeros((D,), jnp.float32), 'ln2_w': jnp.ones((D,), jnp.float32), 'ln2_b': jnp.zeros((D,), jnp.float32), 'w_qkv': jax.random.normal(ks[1], (D, 3 * D), jnp.float32) * s(D), 'b_qkv': jnp.zeros((3 * D,), jnp.float32), 'w_o': jax.random.normal(ks[2], (D, D), jnp.float32) * s(D), 'b_o': jnp.zeros((D,), jnp.float32), 'w_gate': jax.random.normal(ks[3], (D, E), jnp.float32) * s(D), 'w1': jax.random.normal(ks[4], (E, D, H), jnp.float32) * s(D), 'b1': jnp.zeros((E, H), jnp.float32), 'w2': jax.random.normal(ks[5], (E, H, D), jnp.float32) * s(H), 'b2': jnp.zeros((E, D), jnp.float32)}
    _L2_ffn_all = _L2_ffn_setup()
    _L2_ffn_in = {k: v for k, v in _L2_ffn_all.items() if k in ('ln1_w', 'ln1_b', 'ln2_w', 'ln2_b', 'w_qkv', 'b_qkv', 'w_o', 'b_o', 'w_gate', 'w1', 'b1', 'w2', 'b2')}
    del _L2_ffn_all

    def _L3_cond_setup():
        import jax, jax.numpy as jnp
        import numpy as np
        B, S, H = (4, 256, 128)
        E = 8
        M = 64
        K = 2
        N_SHARED = 2
        SM = M * N_SHARED
        G = 64
        GE_TEMP = 1.0
        ALPHA = 0.001
        SEQ_AUX = True
        NORM_TOPK = True
        COS_TEMP = 0.78
        CONS_ALPHA = 0.01
        LEAKY_SLOPE = 0.01
        EPS_COS = 1e-08

        def _leaky(x):
            return jnp.where(x >= 0, x, LEAKY_SLOPE * x)

        def _moe_forward(hidden_states, g, wt, wg, w_gate, w_up, w_down, sw_gate, sw_up, sw_down):
            b, s, h = hidden_states.shape
            x = hidden_states.reshape(-1, h)
            T = x.shape[0]
            logits_h = x @ wt.T
            logits_g = g @ wg.T
            logits_g = jnp.repeat(logits_g, s, axis=0)
            logits = (logits_h + logits_g / GE_TEMP) / (1.0 + 1.0 / GE_TEMP)
            scores = jax.nn.softmax(logits, axis=-1)
            topk_w, topk_idx = jax.lax.top_k(scores, K)
            if K > 1 and NORM_TOPK:
                topk_w = topk_w / (topk_w.sum(-1, keepdims=True) + 1e-20)
            onehot = jax.nn.one_hot(topk_idx.reshape(b, s * K), E, dtype=jnp.float32)
            ce = onehot.sum(1) / (s * K / E)
            aux_loss = (ce * scores.reshape(b, s, E).mean(1)).sum(1).mean() * ALPHA
            gp = _leaky(jnp.einsum('th,ehm->etm', x, w_gate))
            up = jnp.einsum('th,ehm->etm', x, w_up)
            y_all = jnp.einsum('etm,emh->eth', gp * up, w_down)
            y_sel = y_all[topk_idx, jnp.arange(T)[:, None], :]
            y = (y_sel * topk_w[..., None]).sum(1).reshape(b, s, h)
            p = _leaky(hidden_states @ sw_gate) * (hidden_states @ sw_up) @ sw_down
            y = y + p
            num = jnp.sum(y * p, -1)
            den = jnp.maximum(jnp.linalg.norm(y, axis=-1), EPS_COS) * jnp.maximum(jnp.linalg.norm(p, axis=-1), EPS_COS)
            closs = CONS_ALPHA * jnp.mean(num / den / (1.0 + COS_TEMP))
            return (y, aux_loss + closs)
        key = jax.random.key(seed)
        ks = jax.random.split(key, 12)
        sh = 1.0 / np.sqrt(H)
        sm = 1.0 / np.sqrt(M)
        ssm = 1.0 / np.sqrt(SM)
        sg = 1.0 / np.sqrt(G)
        return {'hidden_states': jax.random.normal(ks[0], (B, S, H), jnp.float32), 'g': jax.random.normal(ks[1], (B, G), jnp.float32), 'wt': jax.random.uniform(ks[2], (E, H), jnp.float32, -sh, sh), 'wg': jax.random.uniform(ks[3], (E, G), jnp.float32, -sg, sg), 'w_gate': jax.random.uniform(ks[4], (E, H, M), jnp.float32, -sh, sh), 'w_up': jax.random.uniform(ks[5], (E, H, M), jnp.float32, -sh, sh), 'w_down': jax.random.uniform(ks[6], (E, M, H), jnp.float32, -sm, sm), 'sw_gate': jax.random.uniform(ks[7], (H, SM), jnp.float32, -sh, sh), 'sw_up': jax.random.uniform(ks[8], (H, SM), jnp.float32, -sh, sh), 'sw_down': jax.random.uniform(ks[9], (SM, H), jnp.float32, -ssm, ssm)}
    _L3_cond_all = _L3_cond_setup()
    _L3_cond_in = {k: v for k, v in _L3_cond_all.items() if k in ('wt', 'wg', 'w_gate', 'w_up', 'w_down', 'sw_gate', 'sw_up', 'sw_down')}
    del _L3_cond_all

    def _L3_ffn_setup():
        import jax, jax.numpy as jnp
        import numpy as np
        D_MODEL, D_FF, N_EXPERTS, TOP_K = (128, 256, 8, 2)
        B, S = (2, 256)
        key = jax.random.key(seed)
        ks = jax.random.split(key, 6)
        sd = 1.0 / np.sqrt(D_MODEL)
        sf = 1.0 / np.sqrt(D_FF)
        return {'x': jax.random.normal(ks[0], (B, S, D_MODEL), jnp.float32), 'router_w': jax.random.normal(ks[1], (N_EXPERTS, D_MODEL), jnp.float32) * sd, 'gate_w': jax.random.normal(ks[2], (N_EXPERTS, D_MODEL, D_FF), jnp.float32) * sd, 'gate_b': jnp.zeros((N_EXPERTS, D_FF), jnp.float32), 'up_w': jax.random.normal(ks[3], (N_EXPERTS, D_MODEL, D_FF), jnp.float32) * sd, 'up_b': jnp.zeros((N_EXPERTS, D_FF), jnp.float32), 'down_w': jax.random.normal(ks[4], (N_EXPERTS, D_FF, D_MODEL), jnp.float32) * sf, 'down_b': jnp.zeros((N_EXPERTS, D_MODEL), jnp.float32)}
    _L3_ffn_all = _L3_ffn_setup()
    _L3_ffn_in = {k: v for k, v in _L3_ffn_all.items() if k in ('router_w', 'gate_w', 'gate_b', 'up_w', 'up_b', 'down_w', 'down_b')}
    del _L3_ffn_all
    return {'x': x, 'cond_64': cond_64, 'fside_16xSxS_0': fside_16xSxS_0, 'mask_BxS_bk0': mask_BxS_bk0, 'mask_BxS_bf1': mask_BxS_bf1, 'L0_cond_wt': _L0_cond_in['wt'], 'L0_cond_wg': _L0_cond_in['wg'], 'L0_cond_w_gate': _L0_cond_in['w_gate'], 'L0_cond_w_up': _L0_cond_in['w_up'], 'L0_cond_w_down': _L0_cond_in['w_down'], 'L0_cond_sw_gate': _L0_cond_in['sw_gate'], 'L0_cond_sw_up': _L0_cond_in['sw_up'], 'L0_cond_sw_down': _L0_cond_in['sw_down'], 'L0_ffn_w_gate': _L0_ffn_in['w_gate'], 'L0_ffn_b_gate': _L0_ffn_in['b_gate'], 'L0_ffn_W1': _L0_ffn_in['W1'], 'L0_ffn_b1': _L0_ffn_in['b1'], 'L0_ffn_W2': _L0_ffn_in['W2'], 'L0_ffn_b2': _L0_ffn_in['b2'], 'L1_cond_g_in': _L1_cond_in['g_in'], 'L1_cond_null_attn_bias': _L1_cond_in['null_attn_bias'], 'L1_cond_Wq': _L1_cond_in['Wq'], 'L1_cond_Wkv': _L1_cond_in['Wkv'], 'L1_cond_Wo': _L1_cond_in['Wo'], 'L1_cond_g_out': _L1_cond_in['g_out'], 'L1_ffn_gate_w': _L1_ffn_in['gate_w'], 'L1_ffn_w1': _L1_ffn_in['w1'], 'L1_ffn_b1': _L1_ffn_in['b1'], 'L1_ffn_w2': _L1_ffn_in['w2'], 'L1_ffn_b2': _L1_ffn_in['b2'], 'L2_cond_g_norm': _L2_cond_in['g_norm'], 'L2_cond_Wq': _L2_cond_in['Wq'], 'L2_cond_Wkv': _L2_cond_in['Wkv'], 'L2_cond_q_scale': _L2_cond_in['q_scale'], 'L2_cond_k_scale': _L2_cond_in['k_scale'], 'L2_cond_null_attn_bias': _L2_cond_in['null_attn_bias'], 'L2_cond_w0': _L2_cond_in['w0'], 'L2_cond_b0': _L2_cond_in['b0'], 'L2_cond_g0': _L2_cond_in['g0'], 'L2_cond_w1': _L2_cond_in['w1'], 'L2_cond_b1': _L2_cond_in['b1'], 'L2_cond_g1': _L2_cond_in['g1'], 'L2_cond_w2': _L2_cond_in['w2'], 'L2_cond_b2': _L2_cond_in['b2'], 'L2_cond_Wout': _L2_cond_in['Wout'], 'L2_cond_g_out': _L2_cond_in['g_out'], 'L2_ffn_ln1_w': _L2_ffn_in['ln1_w'], 'L2_ffn_ln1_b': _L2_ffn_in['ln1_b'], 'L2_ffn_ln2_w': _L2_ffn_in['ln2_w'], 'L2_ffn_ln2_b': _L2_ffn_in['ln2_b'], 'L2_ffn_w_qkv': _L2_ffn_in['w_qkv'], 'L2_ffn_b_qkv': _L2_ffn_in['b_qkv'], 'L2_ffn_w_o': _L2_ffn_in['w_o'], 'L2_ffn_b_o': _L2_ffn_in['b_o'], 'L2_ffn_w_gate': _L2_ffn_in['w_gate'], 'L2_ffn_w1': _L2_ffn_in['w1'], 'L2_ffn_b1': _L2_ffn_in['b1'], 'L2_ffn_w2': _L2_ffn_in['w2'], 'L2_ffn_b2': _L2_ffn_in['b2'], 'L3_cond_wt': _L3_cond_in['wt'], 'L3_cond_wg': _L3_cond_in['wg'], 'L3_cond_w_gate': _L3_cond_in['w_gate'], 'L3_cond_w_up': _L3_cond_in['w_up'], 'L3_cond_w_down': _L3_cond_in['w_down'], 'L3_cond_sw_gate': _L3_cond_in['sw_gate'], 'L3_cond_sw_up': _L3_cond_in['sw_up'], 'L3_cond_sw_down': _L3_cond_in['sw_down'], 'L3_ffn_router_w': _L3_ffn_in['router_w'], 'L3_ffn_gate_w': _L3_ffn_in['gate_w'], 'L3_ffn_gate_b': _L3_ffn_in['gate_b'], 'L3_ffn_up_w': _L3_ffn_in['up_w'], 'L3_ffn_up_b': _L3_ffn_in['up_b'], 'L3_ffn_down_w': _L3_ffn_in['down_w'], 'L3_ffn_down_b': _L3_ffn_in['down_b']}

def reference(x, cond_64, fside_16xSxS_0, mask_BxS_bk0, mask_BxS_bf1, L0_cond_wt, L0_cond_wg, L0_cond_w_gate, L0_cond_w_up, L0_cond_w_down, L0_cond_sw_gate, L0_cond_sw_up, L0_cond_sw_down, L0_ffn_w_gate, L0_ffn_b_gate, L0_ffn_W1, L0_ffn_b1, L0_ffn_W2, L0_ffn_b2, L1_cond_g_in, L1_cond_null_attn_bias, L1_cond_Wq, L1_cond_Wkv, L1_cond_Wo, L1_cond_g_out, L1_ffn_gate_w, L1_ffn_w1, L1_ffn_b1, L1_ffn_w2, L1_ffn_b2, L2_cond_g_norm, L2_cond_Wq, L2_cond_Wkv, L2_cond_q_scale, L2_cond_k_scale, L2_cond_null_attn_bias, L2_cond_w0, L2_cond_b0, L2_cond_g0, L2_cond_w1, L2_cond_b1, L2_cond_g1, L2_cond_w2, L2_cond_b2, L2_cond_Wout, L2_cond_g_out, L2_ffn_ln1_w, L2_ffn_ln1_b, L2_ffn_ln2_w, L2_ffn_ln2_b, L2_ffn_w_qkv, L2_ffn_b_qkv, L2_ffn_w_o, L2_ffn_b_o, L2_ffn_w_gate, L2_ffn_w1, L2_ffn_b1, L2_ffn_w2, L2_ffn_b2, L3_cond_wt, L3_cond_wg, L3_cond_w_gate, L3_cond_w_up, L3_cond_w_down, L3_cond_sw_gate, L3_cond_sw_up, L3_cond_sw_down, L3_ffn_router_w, L3_ffn_gate_w, L3_ffn_gate_b, L3_ffn_up_w, L3_ffn_up_b, L3_ffn_down_w, L3_ffn_down_b):
    import jax
    import jax.numpy as jnp

    def _L0_cond_ref(hidden_states, g, wt, wg, w_gate, w_up, w_down, sw_gate, sw_up, sw_down):
        import jax, jax.numpy as jnp
        import numpy as np
        B, S, H = (4, 256, 128)
        E = 8
        M = 64
        K = 2
        N_SHARED = 2
        SM = M * N_SHARED
        G = 64
        GE_TEMP = 1.0
        ALPHA = 0.001
        SEQ_AUX = True
        NORM_TOPK = True
        COS_TEMP = 0.78
        CONS_ALPHA = 0.01
        LEAKY_SLOPE = 0.01
        EPS_COS = 1e-08

        def _leaky(x):
            return jnp.where(x >= 0, x, LEAKY_SLOPE * x)

        def _moe_forward(hidden_states, g, wt, wg, w_gate, w_up, w_down, sw_gate, sw_up, sw_down):
            b, s, h = hidden_states.shape
            x = hidden_states.reshape(-1, h)
            T = x.shape[0]
            logits_h = x @ wt.T
            logits_g = g @ wg.T
            logits_g = jnp.repeat(logits_g, s, axis=0)
            logits = (logits_h + logits_g / GE_TEMP) / (1.0 + 1.0 / GE_TEMP)
            scores = jax.nn.softmax(logits, axis=-1)
            topk_w, topk_idx = jax.lax.top_k(scores, K)
            if K > 1 and NORM_TOPK:
                topk_w = topk_w / (topk_w.sum(-1, keepdims=True) + 1e-20)
            onehot = jax.nn.one_hot(topk_idx.reshape(b, s * K), E, dtype=jnp.float32)
            ce = onehot.sum(1) / (s * K / E)
            aux_loss = (ce * scores.reshape(b, s, E).mean(1)).sum(1).mean() * ALPHA
            gp = _leaky(jnp.einsum('th,ehm->etm', x, w_gate))
            up = jnp.einsum('th,ehm->etm', x, w_up)
            y_all = jnp.einsum('etm,emh->eth', gp * up, w_down)
            y_sel = y_all[topk_idx, jnp.arange(T)[:, None], :]
            y = (y_sel * topk_w[..., None]).sum(1).reshape(b, s, h)
            p = _leaky(hidden_states @ sw_gate) * (hidden_states @ sw_up) @ sw_down
            y = y + p
            num = jnp.sum(y * p, -1)
            den = jnp.maximum(jnp.linalg.norm(y, axis=-1), EPS_COS) * jnp.maximum(jnp.linalg.norm(p, axis=-1), EPS_COS)
            closs = CONS_ALPHA * jnp.mean(num / den / (1.0 + COS_TEMP))
            return (y, aux_loss + closs)
        y, _ = _moe_forward(hidden_states, g, wt, wg, w_gate, w_up, w_down, sw_gate, sw_up, sw_down)
        return y

    def _L0_ffn_ref(x, w_gate, b_gate, W1, b1, W2, b2):
        import jax, jax.numpy as jnp
        import numpy as np
        D_MODEL = 128
        MLP_DIM = 512
        N_EXPERTS = 8
        B, T = (4, 128)
        b, t, d = x.shape
        x_flat = x.reshape(b * t, d)
        logits = x_flat @ w_gate + b_gate
        probs = jax.nn.softmax(logits, axis=-1)
        route_p = jnp.max(probs, axis=-1)
        route_idx = jnp.argmax(probs, axis=-1)
        h = jnp.einsum('nd,edm->enm', x_flat, W1) + b1[:, None, :]
        h = jax.nn.relu(h)
        y = jnp.einsum('enm,emd->end', h, W2) + b2[:, None, :]
        n = b * t
        out = y[route_idx, jnp.arange(n)] * route_p[:, None]
        return out.reshape(b, t, d)

    def _L1_cond_ref(x, attn_bias, mask, g_in, null_attn_bias, null_kv, Wq, Wkv, Wo, g_out):
        import jax, jax.numpy as jnp
        import numpy as np
        B, N, DIM, H, DH = (2, 256, 128, 16, 64)
        INNER = H * DH
        EPS = 1e-05

        def layernorm(x, g):
            mean = jnp.mean(x, axis=-1, keepdims=True)
            var = jnp.var(x, axis=-1, keepdims=True)
            return (x - mean) * jax.lax.rsqrt(var + EPS) * g
        b, n, _ = x.shape
        scale = DH ** (-0.5)
        xn = layernorm(x, g_in)
        q = (xn @ Wq).reshape(b, n, H, DH).transpose(0, 2, 1, 3) * scale
        kv = xn @ Wkv
        k, v = (kv[..., :DH], kv[..., DH:])
        nk = jnp.broadcast_to(null_kv[0], (b, 1, DH))
        nv = jnp.broadcast_to(null_kv[1], (b, 1, DH))
        k = jnp.concatenate([nk, k], axis=1)
        v = jnp.concatenate([nv, v], axis=1)
        sim = jnp.einsum('bhid,bjd->bhij', q, k)
        null_col = jnp.broadcast_to(null_attn_bias[:, None, None], (H, n, 1))
        bias = jnp.concatenate([null_col, attn_bias], axis=-1)
        sim = sim + bias
        neg = -jnp.finfo(sim.dtype).max
        j = n + 1
        causal_mask = jnp.triu(jnp.ones((n, j), dtype=bool), k=j - n + 1)
        sim = jnp.where(causal_mask, neg, sim)
        mask_p = jnp.pad(mask, ((0, 0), (1, 0)), constant_values=True)
        sim = jnp.where(mask_p[:, None, None, :], sim, neg)
        attn = jax.nn.softmax(sim, axis=-1)
        out = jnp.einsum('bhij,bjd->bhid', attn, v)
        out = out.transpose(0, 2, 1, 3).reshape(b, n, INNER)
        out = out @ Wo
        return layernorm(out, g_out)

    def _L1_ffn_ref(x, gate_w, w1, b1, w2, b2):
        import jax, jax.numpy as jnp
        import numpy as np
        NUM_EXPERTS = 8
        TOP_K = 2
        logits = jnp.einsum('bsd,ed->bse', x, gate_w)
        probs = jax.nn.softmax(logits, axis=-1)
        topk_probs, topk_idx = jax.lax.top_k(probs, TOP_K)
        oh = jax.nn.one_hot(topk_idx, NUM_EXPERTS, dtype=x.dtype)
        h = jnp.einsum('bsd,fed,bske->bskf', x, w1, oh)
        h = h + jnp.take(b1, topk_idx, axis=0)
        h = jax.nn.gelu(h)
        y = jnp.einsum('bskf,def,bske->bskd', h, w2, oh)
        y = y + jnp.take(b2, topk_idx, axis=0)
        out = jnp.sum(y * topk_probs[..., None], axis=-2)
        return out

    def _L2_cond_ref(x, mask, g_norm, Wq, Wkv, q_scale, k_scale, null_kv, null_attn_bias, w0, b0, g0, w1, b1, g1, w2, b2, Wout, g_out):
        import jax, jax.numpy as jnp
        import numpy as np
        DIM = 128
        HEADS = 16
        DIM_HEAD = 64
        SCALE = 8.0

        def ln(x, g, eps=1e-05):
            mean = x.mean(axis=-1, keepdims=True)
            var = ((x - mean) ** 2).mean(axis=-1, keepdims=True)
            return (x - mean) * jax.lax.rsqrt(var + eps) * g

        def l2norm(t):
            n = jnp.maximum(jnp.linalg.norm(t, axis=-1, keepdims=True), 1e-12)
            return t / n

        def rel_pos_bias(n, w0, b0, g0, w1, b1, g1, w2, b2, dtype):
            pos = jnp.arange(-n + 1, n, dtype=dtype)[:, None]
            h = jax.nn.silu(ln(pos @ w0 + b0, g0))
            h = jax.nn.silu(ln(h @ w1 + b1, g1))
            h = h @ w2 + b2
            i = jnp.arange(n)
            idx = i[:, None] - i[None, :] + n - 1
            bias = h[idx]
            return jnp.transpose(bias, (2, 0, 1))
        b, n, _ = x.shape
        xn = ln(x, g_norm)
        q = (xn @ Wq).reshape(b, n, HEADS, DIM_HEAD).transpose(0, 2, 1, 3)
        kv = xn @ Wkv
        k, v = (kv[..., :DIM_HEAD], kv[..., DIM_HEAD:])
        nk = jnp.broadcast_to(null_kv[0], (b, 1, DIM_HEAD))
        nv = jnp.broadcast_to(null_kv[1], (b, 1, DIM_HEAD))
        k = jnp.concatenate([nk, k], axis=1)
        v = jnp.concatenate([nv, v], axis=1)
        q = l2norm(q) * q_scale
        k = l2norm(k) * k_scale
        sim = jnp.einsum('bhid,bjd->bhij', q, k) * SCALE
        bias = rel_pos_bias(n, w0, b0, g0, w1, b1, g1, w2, b2, q.dtype)
        null_bias = jnp.broadcast_to(null_attn_bias[:, None, None], (HEADS, n, 1))
        attn_bias = jnp.concatenate([null_bias, bias], axis=-1)
        sim = sim + attn_bias
        neg = -jnp.finfo(sim.dtype).max
        causal = jnp.triu(jnp.ones((n, n + 1), dtype=bool), k=2)
        sim = jnp.where(causal, neg, sim)
        m = jnp.pad(mask, ((0, 0), (1, 0)), constant_values=True)[:, None, None, :]
        sim = jnp.where(m, sim, neg)
        attn = jax.nn.softmax(sim, axis=-1)
        out = jnp.einsum('bhij,bjd->bhid', attn, v)
        out = out.transpose(0, 2, 1, 3).reshape(b, n, HEADS * DIM_HEAD)
        return ln(out @ Wout, g_out)

    def _L2_ffn_ref(x, ln1_w, ln1_b, ln2_w, ln2_b, w_qkv, b_qkv, w_o, b_o, w_gate, w1, b1, w2, b2):
        import jax, jax.numpy as jnp
        import numpy as np
        from jax import lax
        N_HEADS = 16
        TOP_K = 2
        N_EXPERTS = 8

        def layer_norm(x, w, b, eps=1e-05):
            mu = jnp.mean(x, axis=-1, keepdims=True)
            var = jnp.mean(jnp.square(x - mu), axis=-1, keepdims=True)
            return (x - mu) * lax.rsqrt(var + eps) * w + b

        def attention(x, w_qkv, b_qkv, w_o, b_o):
            B, T, D = x.shape
            dh = D // N_HEADS
            qkv = x @ w_qkv + b_qkv
            q, k, v = jnp.split(qkv, 3, axis=-1)
            q = q.reshape(B, T, N_HEADS, dh)
            k = k.reshape(B, T, N_HEADS, dh)
            v = v.reshape(B, T, N_HEADS, dh)
            scores = jnp.einsum('bqhd,bkhd->bhqk', q, k) / jnp.sqrt(jnp.float32(dh)).astype(x.dtype)
            probs = jax.nn.softmax(scores, axis=-1)
            ctx = jnp.einsum('bhqk,bkhd->bqhd', probs, v).reshape(B, T, D)
            return ctx @ w_o + b_o

        def moe_ff(x, w_gate, w1, b1, w2, b2):
            B, T, D = x.shape
            t = x.reshape(B * T, D)
            probs = jax.nn.softmax(t @ w_gate, axis=-1)
            tw, ti = lax.top_k(probs, TOP_K)
            tw = tw / jnp.sum(tw, axis=-1, keepdims=True)
            out = jnp.zeros_like(t)
            for e in range(N_EXPERTS):
                we = jnp.sum(jnp.where(ti == e, tw, 0.0), axis=-1)
                h = jax.nn.gelu(t @ w1[e] + b1[e]) @ w2[e] + b2[e]
                out = out + we[:, None] * h
            return out.reshape(B, T, D)
        h = x + attention(layer_norm(x, ln1_w, ln1_b), w_qkv, b_qkv, w_o, b_o)
        return h + moe_ff(layer_norm(h, ln2_w, ln2_b), w_gate, w1, b1, w2, b2)

    def _L3_cond_ref(hidden_states, g, wt, wg, w_gate, w_up, w_down, sw_gate, sw_up, sw_down):
        import jax, jax.numpy as jnp
        import numpy as np
        B, S, H = (4, 256, 128)
        E = 8
        M = 64
        K = 2
        N_SHARED = 2
        SM = M * N_SHARED
        G = 64
        GE_TEMP = 1.0
        ALPHA = 0.001
        SEQ_AUX = True
        NORM_TOPK = True
        COS_TEMP = 0.78
        CONS_ALPHA = 0.01
        LEAKY_SLOPE = 0.01
        EPS_COS = 1e-08

        def _leaky(x):
            return jnp.where(x >= 0, x, LEAKY_SLOPE * x)

        def _moe_forward(hidden_states, g, wt, wg, w_gate, w_up, w_down, sw_gate, sw_up, sw_down):
            b, s, h = hidden_states.shape
            x = hidden_states.reshape(-1, h)
            T = x.shape[0]
            logits_h = x @ wt.T
            logits_g = g @ wg.T
            logits_g = jnp.repeat(logits_g, s, axis=0)
            logits = (logits_h + logits_g / GE_TEMP) / (1.0 + 1.0 / GE_TEMP)
            scores = jax.nn.softmax(logits, axis=-1)
            topk_w, topk_idx = jax.lax.top_k(scores, K)
            if K > 1 and NORM_TOPK:
                topk_w = topk_w / (topk_w.sum(-1, keepdims=True) + 1e-20)
            onehot = jax.nn.one_hot(topk_idx.reshape(b, s * K), E, dtype=jnp.float32)
            ce = onehot.sum(1) / (s * K / E)
            aux_loss = (ce * scores.reshape(b, s, E).mean(1)).sum(1).mean() * ALPHA
            gp = _leaky(jnp.einsum('th,ehm->etm', x, w_gate))
            up = jnp.einsum('th,ehm->etm', x, w_up)
            y_all = jnp.einsum('etm,emh->eth', gp * up, w_down)
            y_sel = y_all[topk_idx, jnp.arange(T)[:, None], :]
            y = (y_sel * topk_w[..., None]).sum(1).reshape(b, s, h)
            p = _leaky(hidden_states @ sw_gate) * (hidden_states @ sw_up) @ sw_down
            y = y + p
            num = jnp.sum(y * p, -1)
            den = jnp.maximum(jnp.linalg.norm(y, axis=-1), EPS_COS) * jnp.maximum(jnp.linalg.norm(p, axis=-1), EPS_COS)
            closs = CONS_ALPHA * jnp.mean(num / den / (1.0 + COS_TEMP))
            return (y, aux_loss + closs)
        y, _ = _moe_forward(hidden_states, g, wt, wg, w_gate, w_up, w_down, sw_gate, sw_up, sw_down)
        return y

    def _L3_ffn_ref(x, router_w, gate_w, gate_b, up_w, up_b, down_w, down_b):
        import jax, jax.numpy as jnp
        import numpy as np
        D_MODEL, D_FF, N_EXPERTS, TOP_K = (128, 256, 8, 2)
        B, S = (2, 256)
        b, s, d = x.shape
        xf = x.reshape(b * s, d)
        n = xf.shape[0]
        router_logits = xf @ router_w.T
        probs = jax.nn.softmax(router_logits, axis=-1)
        topv, topi = jax.lax.top_k(probs, TOP_K)
        mask = jnp.zeros_like(probs).at[jnp.arange(n)[:, None], topi].set(1.0)
        probs = probs * mask
        probs = probs / (probs.sum(axis=-1, keepdims=True) + 1e-09)
        g = jnp.einsum('nd,edf->nef', xf, gate_w) + gate_b
        u = jnp.einsum('nd,edf->nef', xf, up_w) + up_b
        h = jax.nn.silu(g) * u
        expert_out = jnp.einsum('nef,efd->ned', h, down_w) + down_b
        y = jnp.einsum('ne,ned->nd', probs, expert_out)
        return y.reshape(b, s, d)
    x = x + _L0_ffn_ref(_L0_cond_ref(x, cond_64, L0_cond_wt, L0_cond_wg, L0_cond_w_gate, L0_cond_w_up, L0_cond_w_down, L0_cond_sw_gate, L0_cond_sw_up, L0_cond_sw_down), L0_ffn_w_gate, L0_ffn_b_gate, L0_ffn_W1, L0_ffn_b1, L0_ffn_W2, L0_ffn_b2)
    x = x + _L1_ffn_ref(_L1_cond_ref(x, fside_16xSxS_0, mask_BxS_bk0, L1_cond_g_in, L1_cond_null_attn_bias, cond_64, L1_cond_Wq, L1_cond_Wkv, L1_cond_Wo, L1_cond_g_out), L1_ffn_gate_w, L1_ffn_w1, L1_ffn_b1, L1_ffn_w2, L1_ffn_b2)
    x = x + _L2_ffn_ref(_L2_cond_ref(x, mask_BxS_bf1, L2_cond_g_norm, L2_cond_Wq, L2_cond_Wkv, L2_cond_q_scale, L2_cond_k_scale, cond_64, L2_cond_null_attn_bias, L2_cond_w0, L2_cond_b0, L2_cond_g0, L2_cond_w1, L2_cond_b1, L2_cond_g1, L2_cond_w2, L2_cond_b2, L2_cond_Wout, L2_cond_g_out), L2_ffn_ln1_w, L2_ffn_ln1_b, L2_ffn_ln2_w, L2_ffn_ln2_b, L2_ffn_w_qkv, L2_ffn_b_qkv, L2_ffn_w_o, L2_ffn_b_o, L2_ffn_w_gate, L2_ffn_w1, L2_ffn_b1, L2_ffn_w2, L2_ffn_b2)
    x = x + _L3_ffn_ref(_L3_cond_ref(x, cond_64, L3_cond_wt, L3_cond_wg, L3_cond_w_gate, L3_cond_w_up, L3_cond_w_down, L3_cond_sw_gate, L3_cond_sw_up, L3_cond_sw_down), L3_ffn_router_w, L3_ffn_gate_w, L3_ffn_gate_b, L3_ffn_up_w, L3_ffn_up_b, L3_ffn_down_w, L3_ffn_down_b)
    return x

_drawn_inputs = setup_inputs


def setup_inputs(seed=0):
    import zlib

    import numpy as np

    out = dict(_drawn_inputs(seed))
    spreads = {'L0_ffn_b1': (0.0, 0.513),
     'L0_ffn_b2': (0.0, 0.1),
     'L1_cond_g_in': (1.0, 0.6),
     'L1_cond_g_out': (1.0, 0.2),
     'L2_cond_g_norm': (1.0, 0.2),
     'L2_cond_q_scale': (1.0, 0.2),
     'L2_cond_k_scale': (1.0, 0.2),
     'L2_cond_b0': (0.0, 0.1),
     'L2_cond_g0': (1.0, 0.6),
     'L2_cond_b1': (0.0, 0.1),
     'L2_cond_g1': (1.0, 0.2),
     'L2_cond_b2': (0.0, 0.1),
     'L2_cond_g_out': (1.0, 0.2),
     'L2_ffn_ln1_w': (1.0, 0.2),
     'L2_ffn_ln1_b': (0.0, 0.1),
     'L2_ffn_ln2_w': (1.0, 0.2),
     'L2_ffn_ln2_b': (0.0, 0.1),
     'L2_ffn_b_qkv': (0.0, 0.1),
     'L2_ffn_b_o': (0.0, 0.1),
     'L2_ffn_b1': (0.0, 0.1),
     'L2_ffn_b2': (0.0, 0.1),
     'L3_ffn_gate_b': (0.0, 0.706),
     'L3_ffn_up_b': (0.0, 0.725),
     'L3_ffn_down_b': (0.0, 0.1)}
    factors = {'L0_ffn_W1': 3.593, 'L1_cond_Wq': 3.98}
    for name, (base, spread) in spreads.items():
        noise = np.random.default_rng([zlib.crc32(name.encode()), seed]).standard_normal(out[name].shape)
        drawn = base * np.exp(spread * noise) if base else spread * noise
        out[name] = jnp.asarray(drawn.astype(out[name].dtype))
    for name, factor in factors.items():
        out[name] = (out[name] * factor).astype(out[name].dtype)
    return out
```

```python
from contextlib import ExitStack

import numpy as np

import concourse.bass as bass
from concourse import mybir

ALU = mybir.AluOpType
ACT = mybir.ActivationFunctionType
F32 = mybir.dt.float32
F16 = mybir.dt.float16
U8 = mybir.dt.uint8
U32 = mybir.dt.uint32
AX_X = mybir.AxisListType.X

P = 128
BATCH = 32
SEQ = 32
TOK = BATCH * SEQ
TILES = TOK // P
HALF = 512
EXPERTS = 8
WSCALE = 64.0
MASKED = -1.0e30
KEYS = SEQ + 1
LN_EPS = 1e-5

FFN_KINDS = {
    0: dict(gated=False, chunks=4, func=ACT.Relu),
    1: dict(gated=False, chunks=4, func=ACT.Gelu_apprx_tanh),
    2: dict(gated=False, chunks=4, func=ACT.Gelu_apprx_tanh),
    3: dict(gated=True, chunks=2, func=ACT.Silu),
}
ROUTERS = {
    "cond0": dict(keep=2, norm=True, eps=1e-20, scale=0.5),
    "ffn0": dict(keep=1, norm=False, eps=0.0, scale=1.0),
    "ffn1": dict(keep=2, norm=False, eps=0.0, scale=1.0),
    "ffn2": dict(keep=2, norm=True, eps=0.0, scale=1.0),
    "cond3": dict(keep=2, norm=True, eps=1e-20, scale=0.5),
    "ffn3": dict(keep=2, norm=True, eps=1e-9, scale=1.0),
}
STAGES = ["cond0", "ffn0", "res0", "pre1", "att1", "post1", "ffn1", "res1", "pre2", "att2", "post2",
          "ln1", "self2", "ln2", "ffn2", "res2", "cond3", "ffn3", "res3"]


def expert_cols(kind):
    c = kind["chunks"]
    n_up = 2 if kind["gated"] else 1
    weights = n_up * c * P + c * P
    return weights, weights + 1 + n_up * c


COND_CHUNKS = 5
COND_COLS = COND_CHUNKS * 3 * P

SMALL = {}


def _small_layout():
    at = 0
    for name, n in [
        ("ident", P), ("iota", 8), ("eps", 1), ("headmask", 4), ("ones_pair", 2), ("ones_block", P), ("causal", 4 * KEYS),
        ("posm", 1),
        ("cond0_router", 8), ("cond3_router", 8), ("ffn0_router", 8), ("ffn1_router", 8),
        ("ffn2_router", 8), ("ffn3_router", 8),
        ("cond0_wg", 8), ("cond3_wg", 8), ("condT", BATCH), ("ffn0_brow", 8), ("ones_row", P),
        ("pre1_g", 1), ("post1_g", 1), ("pre2_g", 1), ("post2_g", 1), ("ln1_g", 1), ("ln1_b", 1), ("ln2_g", 1),
        ("ln2_b", 1), ("nk1", 1), ("nv1", 1), ("nv2", 1), ("qs2", 1), ("ks2", 1),
        ("bq", 1), ("bk", 1), ("bo", 1), ("relw1", P), ("relw2", 16), ("relb2", 1),
    ]:
        SMALL[name] = (at, n)
        at += n
    return at


N_SMALL = _small_layout()
ROWS = {}


def _row_layout():
    at = 0
    for name, n in [("relw0", P), ("relb0", P), ("relg0", P), ("relb1", P), ("relg1", P), ("nvrow", 64), ("bv", P)]:
        ROWS[name] = (at, n)
        at += n
    return at


N_ROWS = _row_layout()
N_ATT = TOK + P + 64 + 16 * P
N_SELF = 3 * P + 4 * P


class Chain:

    def __init__(self, eng, sem):
        self.eng, self.sem, self.n = eng, sem, 0

    def done(self, ins):
        ins.then_inc(self.sem, 1)
        self.n = self.n + 1

    def wait(self):
        self.eng.wait_ge(self.sem, self.n)

    def step(self, ins):
        self.done(ins)
        self.wait()


def ffn_steps(st):
    return 2 * COND_CHUNKS if st[:4] == "cond" else 2 * EXPERTS * FFN_KINDS[int(st[3])]["chunks"]


def family(st):
    return "moe" if st[:4] == "cond" or st[:3] == "ffn" else "att" if st[:3] == "att" else \
        "self" if st[:4] == "self" else "norm"


def signals_of(st):
    if family(st) == "moe":
        cond = st[:4] == "cond"
        steps, n = ffn_steps(st), 1 if cond else EXPERTS // 2
        wide = 8 if cond else 2 * EXPERTS
        second = 0 if cond else n
        outs = 0 if cond else 2 * EXPERTS
        return dict(logits=1, lg_sb=1, ex=1, w16=1, wT=1, wTsb=1, spread=wide, spread_sb=wide, split=1,
                    w_dma0=16 * n, w_dma1=16 * second, w_hi0=n, w_hi1=second, w_split0=n, w_split1=second,
                    up=steps, act=steps, hid=steps, down=steps, rep=1 if cond else 0, wtd=outs, acc=outs)
    if family(st) == "att":
        return dict(q=16, q_sb=16, k=2, kk=1, v=1, v_sb=1, sc=8, sub=16, rowmax=8, ex=8, p=16, pt=8, pt_sb=8, pv=16,
                    o=16, wo=2, bm=16, sq=1, ssq=1, k_sb=1, q2=16, ss=2, rq=1)
    if family(st) == "self":
        return dict(qkv=5, qk_sb=1, v_sb=1, sc=8, sub=8, ex=8, p=8, pt=8, pt_sb=8, pv=8, c=8, ct=8, ct_sb=8, wo=4)
    return dict(tr=1, stats=1, sq=1, norm=8, back=2)


class Signals:

    def __init__(self, sems, before, out):
        self.sems, self.before = dict(sems, out=out), dict(before, out=0)

    def __getitem__(self, name):
        return self.sems[name]

    def at(self, name, n):
        return self.sems[name], n + self.before[name]


def build_program(nc, dram, out, stages=None):
    stages = STAGES if stages is None else stages
    with ExitStack() as ctx:
        def sb(name, shape, dt=F32):
            return ctx.enter_context(nc.sbuf_tensor(name, shape, dt))

        def sem(name):
            return ctx.enter_context(nc.semaphore(name))

        small = sb("small", [P, N_SMALL])
        rows = sb("rows", [P, N_ROWS])
        sel16 = sb("sel16", [16, 12 * P], F16)
        ident16 = sb("ident16", [P, P], F16)
        resid = sb("resid", [P, TOK])
        cur = sb("cur", [P, TOK])
        nxt = sb("nxt", [P, TOK])
        keep_mask = sb("keep_mask", [P, BATCH * KEYS])
        keep = keep_mask[:, 0:TOK]
        mask_f = keep_mask[:, :]
        in_hi = sb("in_hi", [P, TOK], F16)
        in_lo = sb("in_lo", [P, TOK], F16)
        STAGE_COLS = 1032
        w_stage = sb("w_stage", [P, 2 * STAGE_COLS])
        w_hi = sb("w_hi", [P, 2 * 1024], F16)
        w_lo = sb("w_lo", [P, 2 * 1024], F16)
        w_bias = sb("w_bias", [P, 2 * 12])
        RING = 4
        h32 = sb("h32", [P, RING, HALF])
        h_hi = sb("h_hi", [P, RING, HALF], F16)
        h_lo = sb("h_lo", [P, RING, HALF], F16)
        gate_wtd = sb("gate_wtd", [P, 4 * HALF])
        gate32 = gate_wtd[:, 0:2 * HALF].rearrange("p (r n) -> p r n", r=2)
        wtd = gate_wtd[:, 2 * HALF:4 * HALF].rearrange("p (r n) -> p r n", r=2)
        big = sb("big", [P, 8 * TOK])
        q2 = sb("q2", [P, 4 * TOK])
        kbd = sb("kbd", [P, BATCH * 2 * KEYS])
        vbd = sb("vbd", [P, TILES * 256])
        oT = sb("oT", [P, 16 * 512])
        vself = oT[:, 8 * 512:16 * 512]
        bm = sb("bm", [P, TILES * 16 * KEYS])
        mask_u8 = sb("mask_u8", [P, 2 * TOK], U8)
        brow = sb("brow", [P, 2, 4, KEYS])
        att_w = sb("att_w", [P, N_ATT])
        self_w = sb("self_w", [P, N_SELF])
        p_sb, pT = h32[:, 0:2, :], h32[:, 2:4, :]
        s_sb = gate_wtd[:, 0:16 * KEYS]
        tok = sb("tok", [P, TILES, P])
        st6 = sb("st6", [P, TILES, 6])
        mv = sb("mv", [P, TILES, 2])
        rstd = sb("rstd", [P, TILES])
        sq8 = sb("sq8", [P, TILES])
        rq = sb("rq", [P, BATCH * 4])
        red = sb("red", [P, 2, 16])
        rt = kbd[:, 0:768].rearrange("p (k n) -> p k n", n=64)
        rt_idx = sb("rt_idx", [P, 64], U32)
        w16 = kbd[:, 768:832].bitcast(F16).rearrange("p (t e) -> p t e", t=TILES)
        wT16 = kbd[0:16, 832:832 + TOK // 2].bitcast(F16)
        rel = tok
        relT = oT[0:16, 0:TOK]
        psum = ctx.enter_context(nc.psum_tensor("psum", [P, 8, HALF], F32))

        def sm(name, lo=0, n=None, p=P):
            at, width = SMALL[name]
            n = width - lo if n is None else n
            return small[0:p, at + lo:at + lo + n]

        def rw(name, p=P):
            at, width = ROWS[name]
            return rows[0:p, at:at + width]

        ident = sm("ident")
        relb_dram = nc.dram_tensor("relb_scratch", [16, SEQ * SEQ], F32)

        c_small, c_rows, c_sel, c_x, c_attw1, c_attw2, c_selfw, c_mask, c_brow, c_relw, c_relr, c_nb = (
            sem(n) for n in ("c_small", "c_rows", "c_sel", "c_x", "c_attw1", "c_attw2", "c_selfw", "c_mask", "c_brow",
                             "c_relw", "c_relr", "c_nb"))
        out_done = sem("out_done")
        S, shared, count = {}, {}, {}
        for st in stages:
            stage_out = sem(f"{st}_out")
            if st[:3] == "res":
                S[st] = Signals({}, {}, stage_out)
                continue
            fam = family(st)
            if fam not in shared:
                shared[fam] = {n: sem(f"{fam}_{n}") for n in signals_of(st)}
                count[fam] = {n: int(n in ("wtd", "acc")) for n in signals_of(st)}
            S[st] = Signals(shared[fam], count[fam], stage_out)
            mine = {n: 0 if st == "att1" and n in ("sq", "ssq", "k_sb", "q2", "ss", "rq") else k
                    for n, k in signals_of(st).items()}
            count[fam] = {n: count[fam][n] + k for n, k in mine.items()}
        dve_chain, act_chain, pool_chain = sem("dve_chain"), sem("act_chain"), sem("pool_chain")
        rel_s = {n: sem(f"rel_{n}") for n in ("h0", "t0", "t0s", "m1", "h1", "t1", "t1s", "m2", "sb", "sq", "si")}
        use_rel = "att2" in stages

        prev = {}
        before = None
        for st in stages:
            prev[st] = before
            before = st
        OUTS = {}
        for st in stages:
            if st[:4] == "cond":
                OUTS[st] = 2
            elif st[:3] == "ffn":
                OUTS[st] = 1
            elif st[:3] == "att":
                OUTS[st] = 2
            elif st == "self2":
                OUTS[st] = 4
            elif st[:3] == "res":
                OUTS[st] = 1
            else:
                OUTS[st] = 2

        def ready(eng, st):
            if prev[st] is None:
                eng.wait_ge(c_x, 16)
            else:
                eng.wait_ge(S[prev[st]]["out"], OUTS[prev[st]])

        SRC, DST = {}, {}
        at = resid
        for st in stages:
            SRC[st] = at
            if st[:3] == "res":
                DST[st] = resid
            elif st == "self2":
                DST[st] = keep
            elif st == "post2":
                DST[st] = keep
            elif st[:3] == "ffn":
                DST[st] = nxt
            else:
                DST[st] = cur if at is not cur else nxt
            at = DST[st]
        LAST = stages[-1]

        block = ctx.enter_context(nc.Block())

        def weight_users():
            return [st for st in stages if st[:4] == "cond" or st[:3] == "ffn"]

        def free_staging(eng, st, slot):
            users = weight_users()
            k = users.index(st)
            if k:
                u = users[k - 1]
                if u[:3] == "ffn":
                    eng.wait_ge(*S[u].at(f"w_split{slot}", EXPERTS // 2))
                else:
                    eng.wait_ge(*S[u].at("w_split0", 1))

        @block.sync
        def _(sp):
            sp.dma_start(small[:, :], dram["small"]).then_inc(c_small, 16)
            sp.dma_start(resid[:, :], dram["xT"]).then_inc(c_x, 16)
            sp.dma_start(sel16[:, :], dram["sel16"]).then_inc(c_sel, 16)
            sp.dma_start(ident16[:, :], dram["ident16"]).then_inc(c_sel, 16)
            sp.dma_start(rows[:, :], dram["rows"].broadcast_to([P, N_ROWS])).then_inc(c_rows, 16)
            sp.dma_start(brow[:, :, :, :].rearrange("p l g k -> p (l g k)"), dram["brow"]).then_inc(c_brow, 16)
            sp.dma_start(mask_u8[:, :], dram["mask"].broadcast_to([P, 2 * TOK])).then_inc(c_mask, 16)
            sp.dma_start(self_w[:, :], dram["self_w"]).then_inc(c_selfw, 16)
            for st in weight_users():
                s = S[st]
                if st[:4] == "cond":
                    for slot in range(2):
                        free_staging(sp, st, slot)
                    sp.dma_start(w_stage[:, 0:COND_COLS], dram[f"{st}_w"]).then_inc(s["w_dma0"], 16)
                    continue
                cols = expert_cols(FFN_KINDS[int(st[3])])[1]
                src = dram[f"{st}_w"]
                for slot in range(2):
                    free_staging(sp, st, slot)
                    sp.dma_start(w_stage[:, slot * STAGE_COLS:slot * STAGE_COLS + cols],
                                 src[slot]).then_inc(s[f"w_dma{slot}"], 16)
                with sp.Fori(1, EXPERTS // 2) as i:
                    for slot in range(2):
                        sp.wait_ge(*s.at(f"w_split{slot}", i))
                        sp.dma_start(w_stage[:, slot * STAGE_COLS:slot * STAGE_COLS + cols],
                                     src[bass.ds(2 * i + slot, 1)].rearrange("a p c -> (a p) c"))\
                            .then_inc(s[f"w_dma{slot}"], 16)
            sp.wait_ge(S[LAST]["out"], OUTS[LAST])
            sp.dma_start(out, DST[LAST][:, :]).then_inc(out_done, 16)
            sp.wait_ge(out_done, 16)

        @block.gpsimd
        def _(pool):
            chain = Chain(pool, pool_chain)
            if "moe" in shared:
                pool.sem_inc(shared["moe"]["wtd"], 1)
                pool.sem_inc(shared["moe"]["acc"], 1)

            def attention_masks(layer):
                s = S[f"att{layer}"]
                if layer == 1:
                    pool.wait_ge(c_mask, 16)
                    pool.wait_ge(c_brow, 16)
                    pool.wait_ge(c_small, 16)
                if layer == 2:
                    pool.wait_ge(c_relr, 64)
                    if "att1" in stages:
                        pool.wait_ge(*S["att1"].at("sub", 2 * TILES))
                    else:
                        pool.wait_ge(c_mask, 16)
                        pool.wait_ge(c_brow, 16)
                        pool.wait_ge(c_small, 16)
                keys = mask_f[:, :].rearrange("p (b k) -> p b k", k=KEYS)
                chain.step(pool.memset(mask_f[:, :], 0.0))
                src = mask_u8[:, (layer - 1) * TOK:layer * TOK].rearrange("p (b k) -> p b k", k=SEQ)
                chain.step(pool.tensor_scalar(keys[:, :, 0:SEQ], src, -1.0, -MASKED, ALU.add, ALU.mult))
                chain.step(pool.tensor_tensor(brow[:, layer - 1, :, :], brow[:, layer - 1, :, :],
                                              sm("causal").rearrange("p (g k) -> p g k", k=KEYS), ALU.add))
                for t in range(TILES):
                    for g2 in range(2):
                        b = brow[:, layer - 1, 2 * g2:2 * g2 + 2, :].unsqueeze(1).broadcast_to([P, 4, 2, KEYS])
                        m = keys[:, 4 * t:4 * t + 4, :].unsqueeze(2).broadcast_to([P, 4, 2, KEYS])
                        o = bm[:, (2 * t + g2) * 8 * KEYS:(2 * t + g2 + 1) * 8 * KEYS]
                        pool.tensor_tensor(o.rearrange("p (b q k) -> p b q k", b=4, q=2), b, m, ALU.add)\
                            .then_inc(s["bm"], 1)

            def ffn(st):
                s = S[st]
                C = FFN_KINDS[int(st[3])]["chunks"]
                n = expert_cols(FFN_KINDS[int(st[3])])[0]
                acc = DST[st]

                def low_half(slot, i):
                    pool.wait_ge(*s.at(f"w_hi{slot}", i + 1))
                    base = slot * STAGE_COLS
                    pool.tensor_tensor(w_lo[:, slot * 1024:slot * 1024 + n], w_stage[:, base:base + n],
                                       w_hi[:, slot * 1024:slot * 1024 + n], ALU.subtract)\
                        .then_inc(s[f"w_split{slot}"], 1)

                def accumulate(y, pair):
                    half = y % 2
                    pool.wait_ge(*s.at("wtd", 4 * pair + y + 1))
                    a = acc[:, half * HALF:(half + 1) * HALF]
                    pool.tensor_tensor(a, a, wtd[:, half, :], ALU.add).then_inc(s["acc"], 1)
                    pool.wait_ge(*s.at("acc", 4 * pair + y + 1))

                low_half(0, 0)
                ready(pool, st)
                chain.step(pool.memset(acc[:, :], 0.0))
                with pool.Fori(0, EXPERTS // 2 - 1) as i:
                    low_half(1, i)
                    for y in range(2):
                        accumulate(y, i)
                    low_half(0, i + 1)
                    for y in range(2, 4):
                        accumulate(y, i)
                low_half(1, EXPERTS // 2 - 1)
                for y in range(4):
                    accumulate(y, EXPERTS // 2 - 1)

            def cond(st):
                s = S[st]
                pool.wait_ge(*s.at("w_hi0", 1))
                pool.tensor_tensor(w_lo[:, 0:COND_COLS], w_stage[:, 0:COND_COLS], w_hi[:, 0:COND_COLS], ALU.subtract)\
                    .then_inc(s["w_split0"], 1)

            for st in stages:
                if st == "att1":
                    attention_masks(1)
                if st == "att2":
                    attention_masks(2)
                if st[:3] == "ffn":
                    ffn(st)
                if st[:4] == "cond":
                    cond(st)

        @block.tensor
        def _(pe):
            mm = pe.matmul

            def mm3(out, w, x, start, stop):
                mm(out, w[0], x[0], start=start, stop=False)
                mm(out, w[0], x[1], start=False, stop=False)
                return mm(out, w[1], x[0], start=False, stop=stop)

            def router(st):
                s = S[st]
                src = SRC[st]
                lg = psum[:, 7, 0:64]
                for t in range(TILES):
                    o = lg[:, 8 * t:8 * t + 8]
                    extra = st[:4] == "cond" or st == "ffn0"
                    last = mm(o, src[:, t * P:(t + 1) * P], sm(f"{st}_router"), start=True, stop=not extra)
                    if st[:4] == "cond":
                        if t == 0:
                            pe.wait_ge(*s.at("rep", 1))
                        last = mm(o, nxt[0:64, t * P:(t + 1) * P], sm(f"{st}_wg", p=64), start=False, stop=True)
                    if st == "ffn0":
                        last = mm(o, sm("ones_row", p=1), sm("ffn0_brow", p=1), start=False, stop=True)
                last.then_inc(s["logits"], 1)

            def spread(st):
                s = S[st]
                n_sel = 4 if st[:4] == "cond" else EXPERTS
                off = EXPERTS if st[:4] == "cond" else 0
                pe.wait_ge(*s.at("w16", 1))
                wT = psum[0:16, 7, :].bitcast(F16)
                for t in range(TILES):
                    last = pe.transpose(wT[:, t * P:(t + 1) * P], w16[:, t, :], ident16[:, :])
                last.then_inc(s["wT"], 1)
                pe.wait_ge(*s.at("wTsb", 1))
                for k in range(2 * n_sel):
                    e, half = k // 2, k % 2
                    if k >= 2:
                        pe.wait_ge(*s.at("spread_sb", k - 1))
                    mm(psum[:, 6 + k % 2, :], sel16[:, (off + e) * P:(off + e + 1) * P],
                       wT16[:, half * HALF:(half + 1) * HALF], start=True, stop=True).then_inc(s["spread"], 1)

            def ffn(st):
                s = S[st]
                kind = FFN_KINDS[int(st[3])]
                C, gated = kind["chunks"], kind["gated"]
                n_up = 2 if gated else 1
                per = 4 * C
                LAG = 2
                router(st)
                spread(st)
                pe.wait_ge(*s.at("split", 1))
                with pe.Fori(0, EXPERTS // 2) as i:
                    pe.wait_ge(*s.at("hid", per * i))
                    for k in range(per + LAG):
                        if k < per:
                            slot, half, c = k // (2 * C), (k // C) % 2, k % C
                            if k % (2 * C) == 0:
                                pe.wait_ge(*s.at(f"w_split{slot}", i + 1))
                            x = (in_hi[:, half * HALF:(half + 1) * HALF], in_lo[:, half * HALF:(half + 1) * HALF])
                            if gated:
                                if k >= 2:
                                    pe.wait_ge(*s.at("hid", per * i + k - 1))
                                banks = [2 * (k % 2), 2 * (k % 2) + 1]
                            else:
                                if k >= 4:
                                    pe.wait_ge(*s.at("act", per * i + k - 3))
                                banks = [k % 4]
                            for u, bank in enumerate(banks):
                                w0 = slot * 1024 + (u * C + c) * P
                                last = mm3(psum[:, bank, :], (w_hi[:, w0:w0 + P], w_lo[:, w0:w0 + P]), x, True, True)
                            last.then_inc(s["up"], 1)
                        if k >= LAG:
                            j = k - LAG
                            slot, half, c = j // (2 * C), (j // C) % 2, j % C
                            yl = j // C
                            pe.wait_ge(*s.at("hid", per * i + j + 1))
                            if c == 0:
                                if yl >= 2:
                                    pe.wait_ge(*s.at("wtd", 4 * i + yl - 1))
                                else:
                                    pe.wait_ge(*s.at("wtd", 4 * i))
                            w0 = slot * 1024 + (n_up * C + c) * P
                            last = mm3(psum[:, 4 + half, :], (w_hi[:, w0:w0 + P], w_lo[:, w0:w0 + P]),
                                       (h_hi[:, j % RING, :], h_lo[:, j % RING, :]), c == 0, c == C - 1)
                            last.then_inc(s["down"], 1)

            def cond(st):
                s = S[st]
                router(st)
                pe.wait_ge(*s.at("split", 1))
                pe.wait_ge(*s.at("w_split0", 1))
                for k in range(2 * COND_CHUNKS + 1):
                    if k < 2 * COND_CHUNKS:
                        chunk, half = k // 2, k % 2
                        if k >= 2:
                            pe.wait_ge(*s.at("hid", k - 1))
                        x = (in_hi[:, half * HALF:(half + 1) * HALF], in_lo[:, half * HALF:(half + 1) * HALF])
                        for u in range(2):
                            w0 = (3 * chunk + u) * P
                            last = mm3(psum[:, 2 * (k % 2) + u, :], (w_hi[:, w0:w0 + P], w_lo[:, w0:w0 + P]), x,
                                       True, True)
                        last.then_inc(s["up"], 1)
                    if k == 1:
                        spread(st)
                    if k >= 1:
                        j = k - 1
                        chunk, half = j // 2, j % 2
                        pe.wait_ge(*s.at("hid", j + 1))
                        w0 = (3 * chunk + 2) * P
                        mm3(psum[:, 4 + half, :], (w_hi[:, w0:w0 + P], w_lo[:, w0:w0 + P]),
                            (h_hi[:, j % RING, :], h_lo[:, j % RING, :]), chunk == 0, chunk == COND_CHUNKS - 1)\
                            .then_inc(s["down"], 1)

            def layer_norm(st):
                s = S[st]
                src = SRC[st]
                for t in range(TILES):
                    last = pe.transpose(psum[:, t // 4, (t % 4) * P:(t % 4 + 1) * P], src[:, t * P:(t + 1) * P], ident)
                last.then_inc(s["tr"], 1)
                for t in range(TILES):
                    pe.wait_ge(*s.at("norm", t + 1))
                    last = pe.transpose(psum[:, 2 + t // 4, (t % 4) * P:(t % 4 + 1) * P], tok[:, t, :], ident)
                    if t % 4 == 3:
                        last.then_inc(s["back"], 1)

            def attention(st):
                s = S[st]
                layer = int(st[3])
                src = SRC[st]
                pe.wait_ge(c_attw1 if layer == 1 else c_attw2, 16)
                Wq, Wk, Wv = att_w[:, 0:TOK], att_w[:, TOK:TOK + P], att_w[:, TOK + P:TOK + P + 64]
                Wo = att_w[:, TOK + P + 64:].rearrange("p (h n) -> p h n", h=16)
                for half in range(2):
                    mm(psum[:, half, :], Wk, src[:, half * HALF:(half + 1) * HALF], start=True, stop=True)\
                        .then_inc(s["k"], 1)
                for t in range(TILES):
                    last = mm(psum[:, 2, t * 64:(t + 1) * 64], src[:, t * P:(t + 1) * P], Wv, start=True, stop=True)
                last.then_inc(s["v"], 1)
                if layer == 2:
                    pe.wait_ge(*s.at("sq", 1))
                    for k in range(3):
                        last = mm(psum[:, 5 + k, 0:352], sm("ones_block"), tok_flat[:, k * 352:(k + 1) * 352],
                                  start=True, stop=True)
                    last.then_inc(s["ssq"], 1)
                for k in range(16):
                    c, half = k // 2, k % 2
                    if k >= 2:
                        pe.wait_ge(*s.at("q_sb", k - 1))
                    mm(psum[:, 3 + k % 2, :], Wq[:, c * P:(c + 1) * P], src[:, half * HALF:(half + 1) * HALF],
                       start=True, stop=True).then_inc(s["q"], 1)
                    if layer == 2 and k % 8 == 7:
                        g2 = k // 8
                        pe.wait_ge(*s.at("q2", k + 1))
                        pe.wait_ge(*s.at("v_sb", 1))
                        for b in range(BATCH):
                            sq = q2[:, b * P:(b + 1) * P]
                            at = (g2 * BATCH + b) * 2
                            last = mm(psum[:, 2, at:at + 2], sq, sm("ones_pair"), start=True, stop=True)
                        last.then_inc(s["ss"], 1)
                pe.wait_ge(*s.at("q_sb", 16))
                pe.wait_ge(*s.at("kk", 1))
                pe.wait_ge(*s.at("v_sb", 1))

                def scores(t):
                    if t >= 1:
                        pe.wait_ge(*s.at("sub", 2 * t))
                    for g2 in range(2):
                        for b in range(4):
                            n = 4 * t + b
                            last = mm(psum[:, g2, b * 66:(b + 1) * 66],
                                      big[:, (g2 * BATCH + n) * P:(g2 * BATCH + n + 1) * P],
                                      kbd[:, n * 66:(n + 1) * 66], start=True, stop=True)
                    last.then_inc(s["sc"], 1)

                scores(0)
                for t in range(TILES):
                    if t + 1 < TILES:
                        scores(t + 1)
                    pe.wait_ge(*s.at("p", 2 * t + 2))
                    if t >= 2:
                        pe.wait_ge(*s.at("pt_sb", t - 1))
                    for g in range(4):
                        last = pe.transpose(psum[:, 6 + t % 2, g * P:(g + 1) * P], p_sb[:, t % 2, g * P:(g + 1) * P],
                                            ident)
                    last.then_inc(s["pt"], 1)
                    pe.wait_ge(*s.at("pt_sb", t + 1))
                    for bp in range(2):
                        if t >= 1:
                            pe.wait_ge(*s.at("o", 2 * (t - 1) + bp + 1))
                        v0 = t * 256 + bp * P
                        mm(psum[:, 3 + bp, :], vbd[:, v0:v0 + P], pT[:, t % 2, :], start=True, stop=True)\
                            .then_inc(s["pv"], 1)
                pe.wait_ge(*s.at("o", 16))
                o = oT[:, :].rearrange("p (m h i) -> p h m i", h=16, i=SEQ)
                for par in range(2):
                    r = slice(64 * par, 64 * par + 64)
                    for h in range(16):
                        last = mm(psum[:, par, :], Wo[r, h, :], o[r, h, :, :], start=h == 0, stop=h == 15)
                    last.then_inc(s["wo"], 1)

            def self_attention(st):
                s = S[st]
                src = SRC[st]
                pe.wait_ge(c_selfw, 16)
                for half in range(2):
                    for k in range(2):
                        mm(psum[:, 2 * k + half, :], self_w[:, k * P:(k + 1) * P], src[:, half * HALF:(half + 1) * HALF],
                           start=True, stop=True).then_inc(s["qkv"], 1)
                for t in range(TILES):
                    last = mm(psum[:, 4 + t // 4, (t % 4) * P:(t % 4 + 1) * P], src[:, t * P:(t + 1) * P],
                              self_w[:, 2 * P:3 * P], start=True, stop=True)
                last.then_inc(s["qkv"], 1)
                pe.wait_ge(*s.at("qk_sb", 1))
                pe.wait_ge(*s.at("v_sb", 1))
                km = q2[:, :].rearrange("p (g t) -> p g t", g=4)

                def scores(t):
                    if t >= 2:
                        pe.wait_ge(*s.at("sub", t - 1))
                    for b in range(4):
                        n = 4 * t + b
                        last = mm(psum[:, t % 2, b * P:(b + 1) * P], big[:, n * P:(n + 1) * P],
                                  km[:, :, n * SEQ:(n + 1) * SEQ], start=True, stop=True)
                    last.then_inc(s["sc"], 1)

                scores(0)
                for t in range(TILES):
                    if t + 1 < TILES:
                        scores(t + 1)
                    pe.wait_ge(*s.at("p", t + 1))
                    for g in range(4):
                        last = pe.transpose(psum[:, 2 + t % 2, g * P:(g + 1) * P], p_sb[:, t % 2, g * P:(g + 1) * P],
                                            ident)
                    last.then_inc(s["pt"], 1)
                    pe.wait_ge(*s.at("pt_sb", t + 1))
                    if t >= 2:
                        pe.wait_ge(*s.at("c", t - 1))
                    for g in range(4):
                        v0 = (t * 4 + g) * P
                        last = mm(psum[:, 4 + t % 2, g * P:(g + 1) * P], pT[:, t % 2, g * P:(g + 1) * P],
                                  vself[:, v0:v0 + P], start=True, stop=True)
                    last.then_inc(s["pv"], 1)
                    pe.wait_ge(*s.at("c", t + 1))
                    pe.transpose(psum[:, 6 + t % 2, 0:P], tok[:, t, :], ident).then_inc(s["ct"], 1)
                pe.wait_ge(*s.at("ct_sb", TILES))
                ctxT = oT[:, 0:TOK].rearrange("p (t h i) -> p h t i", h=4, i=SEQ)
                for b in range(4):
                    r = slice(32 * b, 32 * b + 32)
                    for h in range(4):
                        last = mm(psum[:, b, 0:256], self_w[r, (3 + h) * P:(4 + h) * P], ctxT[r, h, :, :],
                                  start=h == 0, stop=h == 3)
                    last.then_inc(s["wo"], 1)

            def relative_bias():
                pe.wait_ge(rel_s["h0"], 1)
                pe.transpose(psum[:, 0, 0:63], rel[0:63, 0, :], sm("ident", 0, 63, 63)).then_inc(rel_s["t0"], 1)
                pe.wait_ge(rel_s["t0s"], 1)
                mm(psum[0:63, 1, 0:P], rel[:, 1, 0:63], sm("relw1"), start=True, stop=True).then_inc(rel_s["m1"], 1)
                pe.wait_ge(rel_s["h1"], 1)
                pe.transpose(psum[:, 2, 0:63], rel[0:63, 2, :], sm("ident", 0, 63, 63)).then_inc(rel_s["t1"], 1)
                pe.wait_ge(rel_s["t1s"], 1)
                for part in range(2):
                    for i in range(16):
                        q = 16 * part + i
                        last = mm(psum[0:16, 3 + part, i * SEQ:(i + 1) * SEQ], sm("relw2"),
                                  rel[:, 3, 31 - q:63 - q], start=True, stop=True)
                last.then_inc(rel_s["m2"], 1)

            tok_flat = big[:, 0:3 * 352]
            pe.wait_ge(c_small, 16)
            pe.wait_ge(c_sel, 32)
            if use_rel:
                relative_bias()
            for st in stages:
                if st[:3] == "res":
                    continue
                ready(pe, st)
                if use_rel and st == stages[0]:
                    pe.wait_ge(rel_s["sb"], 2)
                if st[:4] == "cond":
                    cond(st)
                elif st[:3] == "ffn":
                    ffn(st)
                elif st[:3] == "att":
                    attention(st)
                elif st == "self2":
                    self_attention(st)
                else:
                    layer_norm(st)

        @block.vector
        def _(dve):
            chain = Chain(dve, dve_chain)
            stt, tt, ts = dve.scalar_tensor_tensor, dve.tensor_tensor, dve.tensor_scalar

            def router(st):
                s = S[st]
                r = ROUTERS[st]

                def r8(k):
                    return rt[:, k, :].rearrange("p (t e) -> p t e", e=8)

                lg, top, ex, m0, m1, em, fi = (r8(k) for k in range(7))
                dve.wait_ge(*s.at("logits", 1))
                chain.step(ts(rt[:, 0, :], psum[:, 7, 0:64], r["scale"], None, ALU.mult))
                for t in range(TILES):
                    chain.done(dve.max(top[:, t, :], lg[:, t, :]))
                chain.wait()
                top0 = top[:, :, 0:1].broadcast_to([P, 8, 8])
                tt(ex, lg, top0, ALU.subtract).then_inc(s["lg_sb"], 1)
                for t in range(TILES):
                    chain.done(dve.max_index(rt_idx[:, 8 * t:8 * t + 8], top[:, t, :], lg[:, t, :]))
                chain.wait()
                chain.step(dve.tensor_copy(rt[:, 6, :], rt_idx[:, :]))
                iota = sm("iota").unsqueeze(1).broadcast_to([P, 8, 8])
                chain.done(tt(m0, iota, fi[:, :, 0:1].broadcast_to([P, 8, 8]), ALU.is_equal))
                if r["keep"] == 2:
                    chain.step(tt(m1, iota, fi[:, :, 1:2].broadcast_to([P, 8, 8]), ALU.is_equal))
                    chain.step(tt(m0, m0, m1, ALU.add))
                chain.wait()
                dve.wait_ge(*s.at("ex", 1))
                chain.done(dve.reduce_sum(rt[:, 8, 0:8], r8(7), AX_X))
                chain.step(tt(em, r8(7), m0, ALU.mult))
                if r["norm"]:
                    chain.step(dve.reduce_sum(rt[:, 8, 8:16], em, AX_X))
                    chain.step(stt(rt[:, 8, 16:24], rt[:, 8, 0:8], r["eps"], rt[:, 8, 8:16], ALU.mult, ALU.add))
                    chain.step(dve.reciprocal(rt[:, 8, 24:32], rt[:, 8, 16:24]))
                else:
                    chain.step(dve.reciprocal(rt[:, 8, 24:32], rt[:, 8, 0:8]))
                chain.step(tt(r8(9), em, rt[:, 8, 24:32].unsqueeze(2).broadcast_to([P, 8, 8]), ALU.mult))
                chain.step(dve.tensor_copy(w16[:, :, 0:8], r8(9)))
                tt(w16[:, :, 8:16], r8(9), w16[:, :, 0:8], ALU.subtract).then_inc(s["w16"], 1)
                dve.wait_ge(*s.at("wT", 1))
                dve.tensor_copy(wT16[:, :], psum[0:16, 7, :].bitcast(F16)).then_inc(s["wTsb"], 1)

            def split_input(st):
                s = S[st]
                chain.step(dve.tensor_copy(in_hi[:, :], SRC[st][:, :]))
                tt(in_lo[:, :], SRC[st][:, :], in_hi[:, :], ALU.subtract).then_inc(s["split"], 1)

            def ffn(st):
                s = S[st]
                kind = FFN_KINDS[int(st[3])]
                C, gated = kind["chunks"], kind["gated"]
                per = 4 * C
                n_acts = C * (2 if gated else 1)
                split_input(st)
                router(st)
                dve.wait_ge(*s.at("spread_sb", 2 * EXPERTS))
                wide = big[:, :].rearrange("p (e t) -> p e t", e=8)
                base = chain.n
                links = per * (2 if gated else 1)
                with dve.Fori(0, EXPERTS // 2) as i:
                    chain.n = base + i * links
                    dve.wait_ge(*s.at("down", per * i))
                    dve.wait_ge(*s.at("acc", 4 * i))
                    DLAG = 3

                    def weigh(yl):
                        slot, half = yl // 2, yl % 2
                        dve.wait_ge(*s.at("down", per * i + C * (yl + 1)))
                        if yl >= 2:
                            dve.wait_ge(*s.at("acc", 4 * i + yl - 1))
                        w = wide[:, bass.ds(2 * i + slot, 1), half * HALF:(half + 1) * HALF]\
                            .rearrange("p a t -> p (a t)")
                        stt(wtd[:, half, :], psum[:, 4 + half, :], w_bias[:, slot * 12:slot * 12 + 1], w,
                            ALU.add, ALU.mult).then_inc(s["wtd"], 1)

                    for k in range(per + DLAG + 1):
                        if k < per:
                            slot, c = k // (2 * C), k % C
                            r = k % RING
                            dve.wait_ge(*s.at("act", per * i + k + 1))
                            if k >= RING:
                                dve.wait_ge(*s.at("down", per * i + k - RING + 1))
                            if gated:
                                ub = w_bias[:, slot * 12 + 1 + c:slot * 12 + 2 + c]
                                chain.step(stt(h32[:, r, :], psum[:, 2 * (k % 2) + 1, :], ub, gate32[:, k % 2, :],
                                               ALU.add, ALU.mult))
                                chain.step(ts(h_hi[:, r, :], h32[:, r, :], 1.0 / WSCALE, None, ALU.mult))
                                stt(h_lo[:, r, :], h32[:, r, :], 1.0 / WSCALE, h_hi[:, r, :], ALU.mult,
                                    ALU.subtract).then_inc(s["hid"], 1)
                            else:
                                chain.step(dve.tensor_copy(h_hi[:, r, :], h32[:, r, :]))
                                tt(h_lo[:, r, :], h32[:, r, :], h_hi[:, r, :], ALU.subtract).then_inc(s["hid"], 1)
                        if k >= DLAG and (k - DLAG) % C == C - 1 and (k - DLAG) < per:
                            weigh((k - DLAG) // C)
                chain.n = base + links * (EXPERTS // 2)
                dve.wait_ge(*s.at("acc", 2 * EXPERTS))
                dve.sem_inc(s["out"], 1)

            def cond(st):
                s = S[st]
                dve.tensor_copy(nxt[0:64, :].rearrange("p (b i) -> p b i", i=SEQ),
                                sm("condT", p=64).unsqueeze(2).broadcast_to([64, BATCH, SEQ])).then_inc(s["rep"], 1)
                split_input(st)
                router(st)
                wide = big[:, 0:4 * TOK].rearrange("p (e t) -> p e t", e=4)
                for k in range(2 * COND_CHUNKS):
                    chunk, half, r = k // 2, k % 2, k % RING
                    dve.wait_ge(*s.at("act", k + 1))
                    if k >= RING:
                        dve.wait_ge(*s.at("down", k - RING + 1))
                    g = gate32[:, k % 2, :]
                    chain.step(stt(h32[:, r, :], g, 0.01, g, ALU.mult, ALU.max))
                    chain.step(stt(h32[:, r, :], psum[:, 2 * (k % 2) + 1, :], 1.0 / WSCALE, h32[:, r, :],
                                   ALU.mult, ALU.mult))
                    if chunk:
                        dve.wait_ge(*s.at("spread_sb", 8))
                        chain.step(tt(h32[:, r, :], h32[:, r, :], wide[:, chunk - 1, half * HALF:(half + 1) * HALF],
                                      ALU.mult))
                    chain.step(dve.tensor_copy(h_hi[:, r, :], h32[:, r, :]))
                    tt(h_lo[:, r, :], h32[:, r, :], h_hi[:, r, :], ALU.subtract).then_inc(s["hid"], 1)

            def layer_norm(st):
                s = S[st]
                dve.wait_ge(*s.at("tr", 1))
                for t in range(TILES):
                    chain.done(dve.bn_stats(st6[:, t, :], psum[:, t // 4, (t % 4) * P:(t % 4 + 1) * P]))
                chain.wait()
                for t in range(TILES):
                    last = dve.bn_aggr(mv[:, t, :], st6[:, t, :])
                    chain.done(last)
                chain.wait()
                dve.sem_inc(s["stats"], 1)
                dve.wait_ge(*s.at("sq", 1))
                chain.step(dve.reciprocal(rstd[:, :], sq8[:, :]))
                for t in range(TILES):
                    ts(tok[:, t, :], psum[:, t // 4, (t % 4) * P:(t % 4 + 1) * P], mv[:, t, 0:1], rstd[:, t:t + 1],
                       ALU.subtract, ALU.mult).then_inc(s["norm"], 1)

            def attention(st):
                s = S[st]
                layer = int(st[3])
                kv = kbd[:, :].rearrange("p (b q k) -> p b q k", q=2, k=KEYS)
                chain.done(dve.memset(kbd[:, :], 0.0))
                chain.step(dve.memset(vbd[:, :], 0.0))
                nk = sm("nk1")
                dve.wait_ge(*s.at("k", 2))
                if layer == 1:
                    for p in range(2):
                        r = slice(64 * p, 64 * p + 64)
                        for half in range(2):
                            chain.done(dve.tensor_copy(
                                kv[r, 16 * half:16 * half + 16, p, 0:SEQ],
                                psum[r, half, :].rearrange("p (b k) -> p b k", k=SEQ)))
                        chain.done(dve.tensor_copy(kv[r, :, p, SEQ], nk[r, :].broadcast_to([64, BATCH])))
                    chain.wait()
                    dve.sem_inc(s["kk"], 1)
                else:
                    k33 = big[:, 2 * TOK:2 * TOK + BATCH * KEYS].rearrange("p (b k) -> p b k", k=KEYS)
                    flat = big[:, 2 * TOK:2 * TOK + BATCH * KEYS]
                    for half in range(2):
                        chain.done(dve.tensor_copy(k33[:, 16 * half:16 * half + 16, 0:SEQ],
                                                   psum[:, half, :].rearrange("p (b k) -> p b k", k=SEQ)))
                    chain.step(dve.tensor_copy(k33[:, :, SEQ], nk.broadcast_to([P, BATCH])))
                    tt(big[:, 0:3 * 352], flat, flat, ALU.mult).then_inc(s["sq"], 1)
                    dve.wait_ge(*s.at("k_sb", 1))
                    nrm = big[:, 4 * TOK:4 * TOK + 1056]
                    chain.step(ts(nrm, nrm, 1e-12, None, ALU.max))
                    chain.step(dve.reciprocal(nrm, nrm))
                    chain.step(tt(flat, flat, nrm, ALU.mult))
                    chain.step(ts(flat, flat, sm("qs2"), sm("ks2"), ALU.mult, ALU.mult))
                    for p in range(2):
                        r = slice(64 * p, 64 * p + 64)
                        chain.done(dve.tensor_copy(kv[r, :, p, :], k33[r, :, :]))
                    chain.wait()
                    dve.sem_inc(s["kk"], 1)
                dve.wait_ge(*s.at("v", 1))
                vb = vbd[:, :].rearrange("p (t b d) -> p t b d", b=4, d=64)
                for b in range(4):
                    r = slice(32 * b, 32 * b + 32)
                    chain.done(tt(vb[r, :, b, :], psum[r, 2, :].rearrange("p (t d) -> p t d", d=64),
                                  rw("nvrow")[r, :].unsqueeze(1).broadcast_to([32, TILES, 64]), ALU.subtract))
                chain.wait()
                dve.sem_inc(s["v_sb"], 1)
                if layer == 2:
                    dve.wait_ge(*s.at("rq", 1))
                    chain.step(ts(rq[:, :], rq[:, :], 1e-12, None, ALU.max))
                    chain.step(dve.reciprocal(rq[:, :], rq[:, :]))
                    chain.step(ts(rq[:, :], rq[:, :], 8.0, None, ALU.mult))
                rqv = rq[:, :].rearrange("p (g b q) -> p g b q", g=2, q=2)
                for t in range(TILES):
                    dve.wait_ge(*s.at("sc", t + 1))
                    for g2 in range(2):
                        if t == 0:
                            dve.wait_ge(*s.at("bm", 2 * TILES))
                        sl = s_sb[:, g2 * 8 * KEYS:(g2 + 1) * 8 * KEYS]
                        table = bm[:, (2 * t + g2) * 8 * KEYS:(2 * t + g2 + 1) * 8 * KEYS]
                        src = psum[:, g2, 0:8 * KEYS]
                        if layer == 2:
                            w = rqv[:, g2, 4 * t:4 * t + 4, :].rearrange("p b q -> p (b q)").unsqueeze(2)\
                                .broadcast_to([P, 8, KEYS])
                            chain.step(tt(sl.rearrange("p (a k) -> p a k", k=KEYS),
                                          src.rearrange("p (a k) -> p a k", k=KEYS), w, ALU.mult))
                            src = sl
                        ins = tt(sl, src, table, ALU.add)
                        ins.then_inc(s["sub"], 1)
                    dve.wait_ge(*s.at("sub", 2 * t + 2))
                    s3 = s_sb[:, :].rearrange("p (a k) -> p a k", k=KEYS)
                    chain.step(dve.reduce_max(red[:, 0, :], s3, AX_X))
                    tt(s3, s3, red[:, 0, :].unsqueeze(2).broadcast_to([P, 16, KEYS]), ALU.subtract)\
                        .then_inc(s["rowmax"], 1)
                    dve.wait_ge(*s.at("ex", t + 1))
                    chain.step(dve.reduce_sum(red[:, 1, :], s3, AX_X))
                    chain.step(dve.reciprocal(red[:, 1, :], red[:, 1, :]))
                    if t >= 2:
                        dve.wait_ge(*s.at("pt", t - 1))
                    for g2 in range(2):
                        o = p_sb[:, t % 2, g2 * 256:(g2 + 1) * 256].rearrange("p (q b k) -> p b q k", q=2, b=4)
                        e = s_sb[:, g2 * 8 * KEYS:(g2 + 1) * 8 * KEYS].rearrange("p (b q k) -> p b q k", b=4, q=2)
                        w = red[:, 1, 8 * g2:8 * g2 + 8].rearrange("p (b q) -> p b q", b=4).unsqueeze(3)\
                            .broadcast_to([P, 4, 2, SEQ])
                        tt(o, e[:, :, :, 0:SEQ], w, ALU.mult).then_inc(s["p"], 1)
                    dve.wait_ge(*s.at("p", 2 * t + 2))

            def self_attention(st):
                s = S[st]
                qm = big[:, 0:4 * TOK].rearrange("p (b h i) -> p h b i", h=4, i=SEQ)
                km = q2[:, :].rearrange("p (g t) -> p g t", g=4)
                chain.done(dve.memset(q2[:, :], 0.0))
                chain.step(dve.memset(vself, 0.0))
                dve.wait_ge(*s.at("qkv", 4))
                for half in range(2):
                    hs = slice(half * HALF, (half + 1) * HALF)
                    for h in range(4):
                        chain.done(ts(qm[:, h, 16 * half:16 * half + 16, :],
                                      psum[:, half, :].rearrange("p (b i) -> p b i", i=SEQ), sm("bq"), sm("headmask", h, 1),
                                      ALU.add, ALU.mult))
                    for g in range(4):
                        r = slice(32 * g, 32 * g + 32)
                        chain.done(ts(km[r, g, hs], psum[r, 2 + half, :], sm("bk")[r, :], None, ALU.add))
                chain.wait()
                dve.sem_inc(s["qk_sb"], 1)
                dve.wait_ge(*s.at("qkv", 5))
                vb = vself.rearrange("p (t g b d) -> p t g b d", g=4, b=4, d=32)
                bv = rw("bv").rearrange("p (g d) -> p g d", g=4)
                for b in range(4):
                    r = slice(32 * b, 32 * b + 32)
                    for half in range(2):
                        for g in range(4):
                            src = psum[r, 4 + half, :].rearrange("p (t g d) -> p t g d", g=4, d=32)[:, :, g, :]
                            chain.done(tt(vb[r, 4 * half:4 * half + 4, g, b, :], src,
                                          bv[r, g, :].unsqueeze(1).broadcast_to([32, 4, 32]), ALU.add))
                chain.wait()
                dve.sem_inc(s["v_sb"], 1)
                for t in range(TILES):
                    dve.wait_ge(*s.at("sc", t + 1))
                    s3 = s_sb[:, 0:512].rearrange("p (a k) -> p a k", k=SEQ)
                    src = psum[:, t % 2, :].rearrange("p (a k) -> p a k", k=SEQ)
                    chain.step(dve.reduce_max(red[:, 0, :], src, AX_X))
                    tt(s3, src, red[:, 0, :].unsqueeze(2).broadcast_to([P, 16, SEQ]), ALU.subtract)\
                        .then_inc(s["sub"], 1)
                    dve.wait_ge(*s.at("ex", t + 1))
                    chain.step(dve.reduce_sum(red[:, 1, :], s3, AX_X))
                    chain.step(dve.reciprocal(red[:, 1, :], red[:, 1, :]))
                    if t >= 2:
                        dve.wait_ge(*s.at("pt", t - 1))
                    o = p_sb[:, t % 2, :].rearrange("p (g b k) -> p b g k", g=4, b=4)
                    e = s_sb[:, 0:512].rearrange("p (b g k) -> p b g k", b=4, g=4)
                    w = red[:, 1, :].rearrange("p (b g) -> p b g", b=4).unsqueeze(3).broadcast_to([P, 4, 4, SEQ])
                    tt(o, e, w, ALU.mult).then_inc(s["p"], 1)
                    dve.wait_ge(*s.at("p", t + 1))
                    dve.wait_ge(*s.at("pv", t + 1))
                    for h in range(4):
                        r = slice(32 * h, 32 * h + 32)
                        c = psum[r, 4 + t % 2, :].rearrange("p (g b h d) -> p b g h d", g=4, b=4, h=4)[:, :, :, h, :]
                        chain.done(dve.tensor_copy(tok[r, t, :].rearrange("p (b g d) -> p b g d", b=4, g=4), c))
                    chain.wait()
                    dve.sem_inc(s["c"], 1)
                x = keep[:, :].rearrange("p (t b i) -> p t b i", b=4, i=SEQ)
                for b in range(4):
                    dve.wait_ge(*s.at("wo", b + 1))
                    stt(x[:, :, b, :], psum[:, b, 0:256].rearrange("p (t i) -> p t i", i=SEQ), sm("bo"),
                        x[:, :, b, :], ALU.add, ALU.add).then_inc(s["out"], 1)

            def relative_bias():
                n = 63
                a, m, q, r0 = rel[0:n, 4, :], mv[0:n, 0, :], sq8[0:n, 0:1], rstd[0:n, 0:1]
                for k, (g_name, b_name, dst) in enumerate([("relg0", "relb0", 0), ("relg1", "relb1", 2)]):
                    if k == 0:
                        chain.step(stt(a, rw("relw0", n), sm("posm", p=n), rw("relb0", n), ALU.mult, ALU.add))
                    else:
                        dve.wait_ge(rel_s["m1"], 1)
                        chain.step(tt(a, psum[0:n, 1, 0:P], rw("relb1", n), ALU.add))
                    chain.step(dve.bn_stats(st6[0:n, 0, :], a))
                    chain.step(dve.bn_aggr(m, st6[0:n, 0, :]))
                    dve.sem_inc(rel_s["sq"], 1)
                    dve.wait_ge(rel_s["sq"], 2 * k + 2)
                    chain.step(dve.reciprocal(r0, q))
                    chain.step(ts(a, a, m[:, 0:1], r0, ALU.subtract, ALU.mult))
                    tt(a, a, rw(g_name, n), ALU.mult).then_inc(rel_s["si"], 1)
                    if k == 0:
                        dve.wait_ge(rel_s["t0"], 1)
                        dve.tensor_copy(rel[:, 1, 0:n], psum[:, 0, 0:n]).then_inc(rel_s["t0s"], 1)
                    else:
                        dve.wait_ge(rel_s["t1"], 1)
                        dve.tensor_copy(rel[:, 3, 0:n], psum[:, 2, 0:n]).then_inc(rel_s["t1s"], 1)

            dve.wait_ge(c_small, 16)
            dve.wait_ge(c_rows, 16)
            if use_rel:
                relative_bias()
            for st in stages:
                ready(dve, st)
                s = S[st]
                if st[:3] == "res":
                    add = SRC[st]
                    if st == "res2":
                        chain.step(tt(resid[:, :], resid[:, :], keep[:, :], ALU.add))
                    tt(resid[:, :], resid[:, :], add[:, :], ALU.add).then_inc(s["out"], 1)
                elif st[:4] == "cond":
                    cond(st)
                elif st[:3] == "ffn":
                    ffn(st)
                elif st[:3] == "att":
                    attention(st)
                elif st == "self2":
                    self_attention(st)
                else:
                    layer_norm(st)

        @block.scalar
        def _(act):
            chain = Chain(act, act_chain)
            fn = act.activation

            def router(st):
                s = S[st]
                act.wait_ge(*s.at("lg_sb", 1))
                fn(rt[:, 7, :], rt[:, 2, :], ACT.Exp).then_inc(s["ex"], 1)

            def spread(st):
                s = S[st]
                n = 8 if st[:4] == "cond" else 2 * EXPERTS
                scale = 1.0 if st[:4] == "cond" else 1.0 / WSCALE
                for k in range(n):
                    act.wait_ge(*s.at("spread", k + 1))
                    fn(big[:, k * HALF:(k + 1) * HALF], psum[:, 6 + k % 2, :], ACT.Copy, scale=scale)\
                        .then_inc(s["spread_sb"], 1)

            def halves_free(st):
                users = weight_users()
                k = users.index(st)
                if k:
                    u = users[k - 1]
                    act.wait_ge(*S[u].at("down", ffn_steps(u)))
                    if u[:3] == "ffn":
                        act.wait_ge(*S[u].at("wtd", 2 * EXPERTS))

            def high_half(st, slot, i):
                s = S[st]
                kind = FFN_KINDS[int(st[3])]
                n, cols = expert_cols(kind)
                scaled = n + 1 + (kind["chunks"] if kind["gated"] else 0)
                base = slot * STAGE_COLS
                part = w_stage[:, base:base + scaled]
                act.wait_ge(*s.at(f"w_dma{slot}", 16 * (i + 1)))
                chain.step(fn(part, part, ACT.Copy, scale=WSCALE))
                chain.step(fn(w_bias[:, slot * 12:slot * 12 + cols - n], w_stage[:, base + n:base + cols], ACT.Copy))
                fn(w_hi[:, slot * 1024:slot * 1024 + n], w_stage[:, base:base + n], ACT.Copy)\
                    .then_inc(s[f"w_hi{slot}"], 1)

            def ffn(st):
                s = S[st]
                kind = FFN_KINDS[int(st[3])]
                C, gated = kind["chunks"], kind["gated"]
                per = 4 * C
                pairs = EXPERTS // 2

                def pair(i, last):
                    act.wait_ge(*s.at("hid", per * i))
                    for k in range(per):
                        slot, c = k // (2 * C), k % C
                        if k == C:
                            act.wait_ge(*s.at("down", per * i))
                            act.wait_ge(*s.at("wtd", 4 * i))
                            high_half(st, 1, i)
                        if k == 3 * C + gated and not last:
                            act.wait_ge(*s.at("down", per * i + 2 * C))
                            act.wait_ge(*s.at("wtd", 4 * i + 2))
                            high_half(st, 0, i + 1)
                        act.wait_ge(*s.at("up", per * i + k + 1))
                        at = slot * 12 + 1 + c + (C if gated else 0)
                        bias = w_bias[:, at:at + 1]
                        if gated:
                            if k >= 2:
                                act.wait_ge(*s.at("hid", per * i + k - 1))
                            dst, bank = gate32[:, k % 2, :], 2 * (k % 2)
                        else:
                            if k >= RING:
                                act.wait_ge(*s.at("hid", per * i + k - RING + 1))
                            dst, bank = h32[:, k % RING, :], k % 4
                        fn(dst, psum[:, bank, :], kind["func"], bias=bias, scale=1.0 / WSCALE).then_inc(s["act"], 1)

                router(st)
                spread(st)
                base_n = chain.n
                links = 2 * 2
                with act.Fori(0, pairs - 1) as i:
                    chain.n = base_n + i * links
                    pair(i, False)
                chain.n = base_n + (pairs - 1) * links
                pair(pairs - 1, True)

            def cond(st):
                s = S[st]
                router(st)
                for k in range(2 * COND_CHUNKS):
                    if k == 2:
                        spread(st)
                    act.wait_ge(*s.at("up", k + 1))
                    if k >= 2:
                        act.wait_ge(*s.at("hid", k - 1))
                    fn(gate32[:, k % 2, :], psum[:, 2 * (k % 2), :], ACT.Copy, scale=1.0 / WSCALE)\
                        .then_inc(s["act"], 1)
                for half in range(2):
                    act.wait_ge(*s.at("down", 2 * COND_CHUNKS - 1 + half))
                    fn(DST[st][:, half * HALF:(half + 1) * HALF], psum[:, 4 + half, :], ACT.Copy,
                       scale=1.0 / WSCALE).then_inc(s["out"], 1)

            def layer_norm(st):
                s = S[st]
                act.wait_ge(*s.at("stats", 1))
                fn(sq8[:, :], mv[:, :, 1], ACT.Sqrt, bias=sm("eps")).then_inc(s["sq"], 1)
                for half in range(2):
                    act.wait_ge(*s.at("back", half + 1))
                    kw = dict(bias=sm(f"{st}_b")) if st[:2] == "ln" else {}
                    fn(DST[st][:, half * HALF:(half + 1) * HALF], psum[:, 2 + half, :], ACT.Identity,
                       scale=sm(f"{st}_g"), **kw).then_inc(s["out"], 1)

            def attention(st):
                s = S[st]
                layer = int(st[3])
                q = big[:, :].rearrange("p (g b h i) -> p g h b i", g=2, h=4, i=SEQ)
                qq = q2[:, :].rearrange("p (b h i) -> p h b i", h=4, i=SEQ)
                if layer == 2:
                    act.wait_ge(*s.at("ssq", 1))
                    for k in range(3):
                        chain.done(fn(big[:, 4 * TOK + k * 352:4 * TOK + (k + 1) * 352], psum[:, 5 + k, 0:352], ACT.Sqrt))
                    chain.wait()
                    act.sem_inc(s["k_sb"], 1)
                    act.wait_ge(*s.at("kk", 1))
                for k in range(16):
                    c, half = k // 2, k % 2
                    act.wait_ge(*s.at("q", k + 1))
                    src = psum[:, 3 + k % 2, :].rearrange("p (b i) -> p b i", i=SEQ)
                    if layer == 2:
                        if k == 8:
                            act.wait_ge(*s.at("ss", 1))
                        fn(qq[:, c % 4, 16 * half:16 * half + 16, :], src, ACT.Square).then_inc(s["q2"], 1)
                    fn(q[:, c // 4, c % 4, 16 * half:16 * half + 16, :], src, ACT.Copy,
                       scale=0.125 if layer == 1 else 1.0).then_inc(s["q_sb"], 1)
                if layer == 2:
                    act.wait_ge(*s.at("ss", 2))
                    fn(rq[:, :], psum[:, 2, 0:128], ACT.Sqrt).then_inc(s["rq"], 1)
                for t in range(TILES):
                    act.wait_ge(*s.at("rowmax", t + 1))
                    fn(s_sb[:, :], s_sb[:, :], ACT.Exp).then_inc(s["ex"], 1)
                    act.wait_ge(*s.at("pt", t + 1))
                    if t >= 2:
                        act.wait_ge(*s.at("pv", 2 * t - 2))
                    fn(pT[:, t % 2, :], psum[:, 6 + t % 2, :], ACT.Copy).then_inc(s["pt_sb"], 1)
                    for bp in range(2):
                        act.wait_ge(*s.at("pv", 2 * t + bp + 1))
                        m = 2 * t + bp
                        fn(oT[:, m * 512:(m + 1) * 512], psum[:, 3 + bp, :], ACT.Identity, bias=sm("nv1"))\
                            .then_inc(s["o"], 1)
                y = DST[st][:, :].rearrange("p (m q i) -> p m q i", q=2, i=SEQ)
                for par in range(2):
                    act.wait_ge(*s.at("wo", par + 1))
                    fn(y[:, :, par, :], psum[:, par, :].rearrange("p (m i) -> p m i", i=SEQ), ACT.Copy)\
                        .then_inc(s["out"], 1)
                if layer == 1 and "att2" in stages:
                    act.wait_ge(*s.at("wo", 2))
                    act.dma_start(att_w[:, :], dram["att2_w"]).then_inc(c_attw2, 16)

            def self_attention(st):
                s = S[st]
                for t in range(TILES):
                    act.wait_ge(*s.at("sub", t + 1))
                    fn(s_sb[:, 0:512], s_sb[:, 0:512], ACT.Exp, scale=float(8.0 ** -0.5)).then_inc(s["ex"], 1)
                    act.wait_ge(*s.at("pt", t + 1))
                    if t >= 2:
                        act.wait_ge(*s.at("pv", t - 1))
                    fn(pT[:, t % 2, :], psum[:, 2 + t % 2, :], ACT.Copy).then_inc(s["pt_sb"], 1)
                    act.wait_ge(*s.at("ct", t + 1))
                    fn(oT[:, t * P:(t + 1) * P], psum[:, 6 + t % 2, 0:P], ACT.Copy).then_inc(s["ct_sb"], 1)

            def relative_bias():
                n = 63
                for k, dst in enumerate((0, 2)):
                    act.wait_ge(rel_s["sq"], 2 * k + 1)
                    fn(sq8[0:n, 0:1], mv[0:n, 0, 1:2], ACT.Sqrt, bias=sm("eps", p=n)).then_inc(rel_s["sq"], 1)
                    act.wait_ge(rel_s["si"], k + 1)
                    fn(rel[0:n, dst, :], rel[0:n, 4, :], ACT.Silu).then_inc(rel_s["h0" if k == 0 else "h1"], 1)
                act.wait_ge(rel_s["m2"], 1)
                for part in range(2):
                    fn(relT[:, part * HALF:(part + 1) * HALF], psum[0:16, 3 + part, :], ACT.Identity,
                       bias=sm("relb2", p=16)).then_inc(rel_s["sb"], 1)
                act.wait_ge(rel_s["sb"], 2)
                act.dma_start(relb_dram.ap(), relT[:, :]).then_inc(c_relw, 16)
                act.wait_ge(c_relw, 16)
                act.wait_ge(c_brow, 16)
                src = relb_dram.ap().rearrange("(h g) (i k) -> h i g k", h=4, i=SEQ)
                for h in range(4):
                    act.dma_start(brow[32 * h:32 * h + 32, 1, :, 0:SEQ], src[h]).then_inc(c_relr, 16)

            first_att = next((st for st in stages if st[:3] == "att"), None)
            if first_att:
                act.dma_start(att_w[:, :], dram[f"{first_att}_w"])\
                    .then_inc(c_attw1 if first_att == "att1" else c_attw2, 16)
            act.wait_ge(c_small, 16)
            if use_rel:
                relative_bias()
            for st in stages:
                if st[:3] == "res":
                    continue
                if family(st) == "moe":
                    halves_free(st)
                    if st[:4] == "cond":
                        act.wait_ge(*S[st].at("w_dma0", 16))
                        src = w_stage[:, 0:COND_COLS]
                        chain.step(fn(src, src, ACT.Copy, scale=WSCALE))
                        fn(w_hi[:, 0:COND_COLS], src, ACT.Copy).then_inc(S[st]["w_hi0"], 1)
                    else:
                        high_half(st, 0, 0)
                ready(act, st)
                if st[:4] == "cond":
                    cond(st)
                elif st[:3] == "ffn":
                    ffn(st)
                elif st[:3] == "att":
                    attention(st)
                elif st == "self2":
                    self_attention(st)
                else:
                    layer_norm(st)


def constants():
    c = {}
    c["ident"] = np.eye(P)
    c["iota"] = np.tile(np.arange(8.0), (P, 1))
    c["eps"] = np.full((P, 1), LN_EPS)
    c["headmask"] = ((np.arange(P)[:, None] % 32) // 8 == np.arange(4)[None, :])
    c["ones_pair"] = (np.arange(P)[:, None] // 64 == np.arange(2)[None, :])
    c["ones_block"] = (np.arange(P)[:, None] // 64 == np.arange(P)[None, :] // 64)
    future = np.arange(SEQ)[None, :] > (np.arange(P) % SEQ)[:, None]
    causal = np.zeros((P, 4, KEYS))
    causal[:, :, 0:SEQ] = np.where(future, MASKED, 0.0)[:, None, :]
    c["causal"] = causal.reshape(P, 4 * KEYS)
    pos = np.zeros((P, 1))
    pos[0:63, 0] = 31.0 - np.arange(63)
    c["posm"] = pos
    c["ones_row"] = np.ones((P, P))
    return c


def lay_out(i):
    f = np.float32

    def a(name):
        return np.asarray(i[name])

    def col(v):
        return v.reshape(-1, 1)

    def full(v, n=1):
        v = v.reshape(-1, n) if v.ndim == 1 else v
        o = np.zeros((P, v.shape[1]), f)
        o[0:v.shape[0]] = v
        return o

    s = constants()
    cond = a("cond_64")
    twice = lambda v: col(np.concatenate([v, v]))
    for layer in (0, 3):
        s[f"cond{layer}_router"] = a(f"L{layer}_cond_wt").T
        s[f"cond{layer}_wg"] = full(a(f"L{layer}_cond_wg").T)
    s["ffn0_router"] = a("L0_ffn_w_gate")
    s["ffn1_router"] = a("L1_ffn_gate_w").T
    s["ffn2_router"] = a("L2_ffn_w_gate")
    s["ffn3_router"] = a("L3_ffn_router_w").T
    s["condT"] = full(cond.T)
    s["ffn0_brow"] = np.tile(a("L0_ffn_b_gate"), (P, 1))
    s["pre1_g"], s["post1_g"] = col(a("L1_cond_g_in")), col(a("L1_cond_g_out"))
    s["pre2_g"], s["post2_g"] = col(a("L2_cond_g_norm")), col(a("L2_cond_g_out"))
    for n in (1, 2):
        s[f"ln{n}_g"], s[f"ln{n}_b"] = col(a(f"L2_ffn_ln{n}_w")), col(a(f"L2_ffn_ln{n}_b"))
    s["nk1"], s["nv1"], s["nv2"] = twice(cond[0]), twice(cond[1]), twice(cond[1])
    s["qs2"], s["ks2"] = twice(a("L2_cond_q_scale")), twice(a("L2_cond_k_scale"))
    bqkv = a("L2_ffn_b_qkv")
    s["bq"], s["bk"], s["bo"] = col(bqkv[0:P]), col(bqkv[P:2 * P]), col(a("L2_ffn_b_o"))
    s["relw1"] = a("L2_cond_w1")
    heads = np.array([8 * g2 + 2 * h4 + p for h4 in range(4) for g2 in range(2) for p in range(2)])
    s["relw2"] = a("L2_cond_w2")[:, heads]
    s["relb2"] = full(a("L2_cond_b2")[heads])
    small = np.zeros((P, N_SMALL), f)
    for name, (at, n) in SMALL.items():
        small[:, at:at + n] = s[name]

    r = {"relw0": a("L2_cond_w0").reshape(-1), "relb0": a("L2_cond_b0"), "relg0": a("L2_cond_g0"),
         "relb1": a("L2_cond_b1"), "relg1": a("L2_cond_g1"), "nvrow": cond[1], "bv": bqkv[2 * P:]}
    rows = np.concatenate([r[n] for n in ROWS]).reshape(1, N_ROWS)

    d = {"small": small, "rows": rows}
    d["xT"] = a("x").reshape(TOK, P).T
    d["ident16"] = np.eye(P, dtype=np.float16)
    sel = np.zeros((16, 12, P), np.float16)
    for e in range(EXPERTS):
        sel[[e, e + 8], e, :] = 1
        sel[[e, e + 8], 8 + e // 2, 64 * (e % 2):64 * (e % 2) + 64] = 1
    d["sel16"] = sel.reshape(16, 12 * P)
    d["mask"] = np.stack([a("mask_BxS_bk0"), a("mask_BxS_bf1")]).reshape(1, 2 * TOK)
    brow = np.zeros((4, SEQ, 2, 4, KEYS), f)
    hh = heads.reshape(4, 4)
    brow[:, :, 0, :, 0:SEQ] = a("fside_16xSxS_0")[hh].transpose(0, 2, 1, 3)
    for layer in (1, 2):
        brow[:, :, layer - 1, :, SEQ] = a(f"L{layer}_cond_null_attn_bias")[hh][:, None, :]
    d["brow"] = brow.reshape(P, 2 * 4 * KEYS)
    for layer in (0, 3):
        L = f"L{layer}_cond_"
        w = np.zeros((P, COND_CHUNKS, 3, P), f)
        w[:, 0, 0], w[:, 0, 1], w[:, 0, 2] = a(L + "sw_gate"), a(L + "sw_up"), a(L + "sw_down")
        w[:, 1:, 0] = a(L + "w_gate").transpose(1, 0, 2).reshape(P, 4, P)
        w[:, 1:, 1] = a(L + "w_up").transpose(1, 0, 2).reshape(P, 4, P)
        w[:, 1:, 2] = a(L + "w_down").reshape(4, P, P).transpose(1, 0, 2)
        d[f"cond{layer}_w"] = w.reshape(P, COND_COLS)

    def expert_blocks(ups, down, biases, bdown):
        F = down.shape[1]
        c = F // P
        parts = list(ups) + [down.reshape(EXPERTS, c, P, P).transpose(0, 2, 1, 3).reshape(EXPERTS, P, c * P)]
        parts.append(bdown[:, :, None])
        parts += [b.reshape(EXPERTS, c, P).transpose(0, 2, 1) for b in biases]
        return np.concatenate(parts, axis=2)

    d["ffn0_w"] = expert_blocks([a("L0_ffn_W1")], a("L0_ffn_W2"), [a("L0_ffn_b1")], a("L0_ffn_b2"))
    d["ffn1_w"] = expert_blocks([a("L1_ffn_w1").transpose(1, 2, 0)], a("L1_ffn_w2").transpose(1, 2, 0),
                                [a("L1_ffn_b1")], a("L1_ffn_b2"))
    d["ffn2_w"] = expert_blocks([a("L2_ffn_w1")], a("L2_ffn_w2"), [a("L2_ffn_b1")], a("L2_ffn_b2"))
    d["ffn3_w"] = expert_blocks([a("L3_ffn_gate_w"), a("L3_ffn_up_w")], a("L3_ffn_down_w"),
                                [a("L3_ffn_up_b"), a("L3_ffn_gate_b")], a("L3_ffn_down_b"))
    order = np.array([8 * g2 + 2 * h4 + p for g2 in range(2) for p in range(2) for h4 in range(4)])
    for layer, wo in ((1, "Wo"), (2, "Wout")):
        L = f"L{layer}_cond_"
        kv = a(L + "Wkv")
        o = a(L + wo).reshape(16, 64, P)[order].transpose(1, 0, 2).reshape(64, 16 * P)
        d[f"att{layer}_w"] = np.concatenate(
            [a(L + "Wq"), kv[:, 0:64], kv[:, 0:64], kv[:, 64:], np.concatenate([o, o])], axis=1)
    wo = a("L2_ffn_w_o").reshape(4, 4, 8, P).transpose(0, 2, 1, 3).reshape(32, 4 * P)
    d["self_w"] = np.concatenate([a("L2_ffn_w_qkv"), np.concatenate([wo] * 4)], axis=1)
    return {k: np.ascontiguousarray(v) for k, v in d.items()}


def make(nc, arrays, stages=None):
    dram = {}
    for name, v in arrays.items():
        dram[name] = nc.dram_tensor(f"in_{name}", v.shape, mybir.dt.from_np(v.dtype), kind="ExternalInput").ap()
    out = nc.dram_tensor("out_xT", (P, TOK), F32, kind="ExternalOutput").ap()
    build_program(nc, dram, out, stages)


def kernel(**inputs):
    import concourse.bacc as bacc
    from concourse.bass_utils import run_bass_kernel_spmd

    arrays = lay_out(inputs)
    nc = bacc.Bacc("TRN2", target_bir_lowering=False, num_devices=1)
    make(nc, arrays)
    r = run_bass_kernel_spmd(nc, [{f"in_{k}": v for k, v in arrays.items()}], core_ids=[0])
    return np.ascontiguousarray(np.asarray(r.results[0]["out_xT"]).T).reshape(BATCH, SEQ, P)
```

```python
from contextlib import ExitStack

import numpy as np

import concourse.bass as bass
from concourse import mybir

ALU = mybir.AluOpType
ACT = mybir.ActivationFunctionType
F32 = mybir.dt.float32
F16 = mybir.dt.float16
U8 = mybir.dt.uint8
U32 = mybir.dt.uint32
AX_X = mybir.AxisListType.X

P = 128
BATCH = 32
SEQ = 32
TOK = BATCH * SEQ
TILES = TOK // P
HALF = 512
EXPERTS = 8
WSCALE = 64.0
MASKED = -1.0e30
KEYS = SEQ + 1
LN_EPS = 1e-5

FFN_KINDS = {
    0: dict(gated=False, chunks=4, func=ACT.Relu),
    1: dict(gated=False, chunks=4, func=ACT.Gelu_apprx_tanh),
    2: dict(gated=False, chunks=4, func=ACT.Gelu_apprx_tanh),
    3: dict(gated=True, chunks=2, func=ACT.Silu),
}
ROUTERS = {
    "cond0": dict(keep=2, norm=True, eps=1e-20, scale=0.5),
    "ffn0": dict(keep=1, norm=False, eps=0.0, scale=1.0),
    "ffn1": dict(keep=2, norm=False, eps=0.0, scale=1.0),
    "ffn2": dict(keep=2, norm=True, eps=0.0, scale=1.0),
    "cond3": dict(keep=2, norm=True, eps=1e-20, scale=0.5),
    "ffn3": dict(keep=2, norm=True, eps=1e-9, scale=1.0),
}
STAGES = ["cond0", "ffn0", "res0", "pre1", "att1", "post1", "ffn1", "res1", "pre2", "att2", "post2",
          "ln1", "self2", "ln2", "ffn2", "res2", "cond3", "ffn3", "res3"]


def expert_cols(kind):
    c = kind["chunks"]
    n_up = 2 if kind["gated"] else 1
    weights = n_up * c * P + c * P
    return weights, weights + 1 + n_up * c


COND_CHUNKS = 5
COND_COLS = COND_CHUNKS * 3 * P
COND_PARTS = [(0, 2 * 3 * P), (2 * 3 * P, COND_COLS)]
COND_SPREAD = {3: (0, 3), 4: (3, 3), 5: (6, 2)}

SMALL = {}


def _small_layout():
    at = 0
    for name, n in [
        ("ident", P), ("iota", 8), ("eps", 1), ("headmask", 4), ("ones_pair", 2), ("ones_block", P), ("causal", 4 * KEYS),
        ("posm", 1),
        ("cond0_router", 8), ("cond3_router", 8), ("ffn0_router", 8), ("ffn1_router", 8),
        ("ffn2_router", 8), ("ffn3_router", 8),
        ("cond0_wg", 8), ("cond3_wg", 8), ("condT", BATCH), ("ffn0_brow", 8), ("ones_row", P),
        ("pre1_g", 1), ("post1_g", 1), ("pre2_g", 1), ("post2_g", 1), ("ln1_g", 1), ("ln1_b", 1), ("ln2_g", 1),
        ("ln2_b", 1), ("nk1", 1), ("nv1", 1), ("nv2", 1), ("qs2", 1), ("ks2", 1),
        ("bq", 1), ("bk", 1), ("bo", 1), ("relw1", P), ("relw2", 16), ("relb2", 1),
    ]:
        SMALL[name] = (at, n)
        at += n
    return at


N_SMALL = _small_layout()
ROWS = {}


def _row_layout():
    at = 0
    for name, n in [("relw0", P), ("relb0", P), ("relg0", P), ("relb1", P), ("relg1", P), ("nvrow", 64), ("bv", P)]:
        ROWS[name] = (at, n)
        at += n
    return at


N_ROWS = _row_layout()
N_ATT = TOK + P + 64 + 8 * P
Q_ORDER = [(half, g2, h4) for half in range(2) for g2 in range(2) for h4 in range(4)]
Q_BANKS = (3, 5, 6)
N_SELF = 3 * P + 4 * P


class Chain:

    def __init__(self, eng, sem):
        self.eng, self.sem, self.n = eng, sem, 0

    def done(self, ins):
        ins.then_inc(self.sem, 1)
        self.n = self.n + 1

    def wait(self):
        self.eng.wait_ge(self.sem, self.n)

    def step(self, ins):
        self.done(ins)
        self.wait()


AHEAD, AHEAD_OF = 4, ("wtd", "acc", "up", "act", "hid", "down", "prod", "high")
COND_LAG = 4
LAG = 3
WEIGH = 4


def splits(kind):
    if kind["gated"]:
        return [(0, 0, "down", 0), (1, 1, "up", 0), (4, 1, "down", 0), (5, 0, "up", 1)]
    return [(2, 1, "up", 0), (5, 1, "down", 0), (10, 0, "up", 1), (13, 0, "down", 1)]


def splits_at(kind, k, first=False, last=False):
    return [(slot, part, nxt) for step, slot, part, nxt in splits(kind)
            if step == k and not (last and nxt) and not (first and slot == 0 and not nxt)]


def weighed_at(kind, k):
    y, rest = divmod(k - WEIGH + 1, kind["chunks"])
    return y - 1 if rest == 0 and 1 <= y <= 4 else None


def part_cols(kind, part):
    up = (2 if kind["gated"] else 1) * kind["chunks"] * P
    return (0, up) if part == "up" else (up, up + kind["chunks"] * P)


def interleave(st):
    if FFN_KINDS[int(st[3])]["gated"]:
        return dict(mask=0, weights=0, copy=1, transpose=2, spread=3, pieces=4)
    return dict(mask=0, weights=1, copy=4, transpose=4, spread=6, pieces=2)


def ffn_steps(st):
    return 2 * COND_CHUNKS if st[:4] == "cond" else 2 * EXPERTS * FFN_KINDS[int(st[3])]["chunks"]


def family(st):
    return "moe" if st[:4] == "cond" or st[:3] == "ffn" else "att" if st[:3] == "att" else \
        "self" if st[:4] == "self" else "norm"


def signals_of(st):
    if family(st) == "moe":
        cond = st[:4] == "cond"
        gated = FFN_KINDS[int(st[3])]["gated"] if st[:3] == "ffn" else False
        steps, n = ffn_steps(st), 1 if cond else EXPERTS // 2
        wide = 8 if cond else 2 * EXPERTS
        second = 0 if cond else n
        outs = 0 if cond else 2 * EXPERTS
        return dict(logits=1, lg_sb=1, ex=1, w16=1, wT=1, wTsb=1, spread=wide, spread_sb=wide, split=1,
                    w_dma0=16 * n, w_dma1=16 * second, w_hi0=2 * n, w_hi1=2 * second, w_split0=2 * n,
                    w_split1=2 * second,
                    gate=steps if cond or gated else 0, up=steps, act=steps, hid=steps, down=steps, wtd=outs, acc=outs,
                    rep=1 if cond else 0, weighed=steps - 2 if cond else 0,
                    prod=steps if cond or gated else 0, high=steps if cond or gated else 0)
    if family(st) == "att":
        return dict(q=16, q_sb=16, k=2, kk=1, v=1, v_sb=1, sc=8, biased=16, rowmax=8, sub=8, ex=8, rsum=8, p=16,
                    pt=8, pt_sb=8, pv=16, o=32, wo=2, zeroed=1, bm=16, sq=1, ssq=1, k_sb=1, q2=16, ss=4, rq=2)
    if family(st) == "self":
        return dict(zeroed=1, qkv=5, q_sb=1, k_sb=1, v_sb=1, sc=8, sub=8, ex=8, rsum=8, p=8, pt=8, pt_sb=8, pv=8, c=8,
                    ct=8, ct_sb=8, wo=4)
    return dict(tr=2, stats=1, sq=1, inv=1, norm=4, norm_act=4, back=2)


class Signals:

    def __init__(self, sems, before, out):
        self.sems, self.before = dict(sems, out=out), dict(before, out=0)

    def __getitem__(self, name):
        return self.sems[name]

    def at(self, name, n):
        return self.sems[name], n + self.before[name]


def build_program(nc, dram, out, stages=None):
    stages = STAGES if stages is None else stages
    with ExitStack() as ctx:
        def sb(name, shape, dt=F32):
            return ctx.enter_context(nc.sbuf_tensor(name, shape, dt))

        def sem(name):
            return ctx.enter_context(nc.semaphore(name))

        small = sb("small", [P, N_SMALL])
        rows = sb("rows", [P, N_ROWS])
        sel16 = sb("sel16", [16, 12 * P], F16)
        ident16 = sb("ident16", [P, P], F16)
        resid = sb("resid", [P, TOK])
        cur = sb("cur", [P, TOK])
        nxt = sb("nxt", [P, TOK])
        keep_mask = sb("keep_mask", [P, BATCH * KEYS])
        keep = keep_mask[:, 0:TOK]
        mask_f = keep_mask[:, :]
        in_hi = sb("in_hi", [P, TOK], F16)
        in_lo = sb("in_lo", [P, TOK], F16)
        STAGE_COLS = 1032
        w_stage = sb("w_stage", [P, 2 * STAGE_COLS])
        w_hi = sb("w_hi", [P, 2 * 1024], F16)
        w_lo = sb("w_lo", [P, 2 * 1024], F16)
        w_bias = sb("w_bias", [P, 2 * 12])
        RING = 4
        h32 = sb("h32", [P, RING, HALF])
        h_hi = sb("h_hi", [P, RING, HALF], F16)
        h_lo = sb("h_lo", [P, RING, HALF], F16)
        gate_wtd = sb("gate_wtd", [P, 4 * HALF])
        gate32 = gate_wtd[:, 0:2 * HALF].rearrange("p (r n) -> p r n", r=2)
        wtd = gate_wtd[:, 2 * HALF:4 * HALF].rearrange("p (r n) -> p r n", r=2)
        big = sb("big", [P, 8 * TOK])
        q2 = sb("q2", [P, 4 * TOK])
        kbd = sb("kbd", [P, BATCH * 2 * KEYS])
        vbd = sb("vbd", [P, TILES * 256])
        oT = sb("oT", [P, 16 * 512])
        vself = oT[:, 8 * 512:16 * 512]
        bm = sb("bm", [P, TILES * 16 * KEYS])
        mask_u8 = sb("mask_u8", [P, 2 * TOK], U8)
        brow = sb("brow", [P, 2, 4, KEYS])
        att_w = sb("att_w", [P, N_ATT])
        self_w = sb("self_w", [P, N_SELF])
        p_sb, pT = h32[:, 0:2, :], h32[:, 2:4, :]
        s_sb = gate_wtd[:, 0:3 * 16 * KEYS].rearrange("p (r n) -> p r n", r=3)
        tok = sb("tok", [P, TILES, P])
        st6 = sb("st6", [P, TILES, 6])
        mv = sb("mv", [P, TILES, 2])
        rstd = sb("rstd", [P, TILES])
        sq8 = sb("sq8", [P, TILES])
        rq = sb("rq", [P, BATCH * 4])
        table_probe = sb("table_probe", [P, 1])
        nmr = sb("nmr", [P, TILES])
        red = sb("red", [P, 2, 2, 16])
        rt = kbd[:, 0:768].rearrange("p (k n) -> p k n", n=64)
        rt_idx = sb("rt_idx", [P, 64], U32)
        w16 = kbd[:, 768:832].bitcast(F16).rearrange("p (t e) -> p t e", t=TILES)
        wT16 = kbd[0:16, 832:832 + TOK // 2].bitcast(F16)
        rel = tok
        relT = oT[0:16, 0:TOK]
        psum = ctx.enter_context(nc.psum_tensor("psum", [P, 8, HALF], F32))

        def sm(name, lo=0, n=None, p=P):
            at, width = SMALL[name]
            n = width - lo if n is None else n
            return small[0:p, at + lo:at + lo + n]

        def rw(name, p=P):
            at, width = ROWS[name]
            return rows[0:p, at:at + width]

        ident = sm("ident")
        relb_dram = nc.dram_tensor("relb_scratch", [16, SEQ * SEQ], F32)

        c_small, c_rows, c_sel, c_x, c_attw1, c_attw2, c_selfw, c_mask, c_brow, c_relw, c_relr, c_nb = (
            sem(n) for n in ("c_small", "c_rows", "c_sel", "c_x", "c_attw1", "c_attw2", "c_selfw", "c_mask", "c_brow",
                             "c_relw", "c_relr", "c_nb"))
        out_done = sem("out_done")
        S, shared, count = {}, {}, {}
        for st in stages:
            stage_out = sem(f"{st}_out")
            if st[:3] == "res":
                S[st] = Signals({}, {}, stage_out)
                continue
            fam = family(st)
            if fam not in shared:
                shared[fam] = {n: sem(f"{fam}_{n}") for n in signals_of(st)}
                count[fam] = {n: AHEAD if n in AHEAD_OF else 0 for n in signals_of(st)}
            S[st] = Signals(shared[fam], count[fam], stage_out)
            mine = {n: 0 if st == "att1" and n in ("sq", "ssq", "k_sb", "q2", "ss", "rq") else k
                    for n, k in signals_of(st).items()}
            count[fam] = {n: count[fam][n] + k for n, k in mine.items()}
        dve_chain, act_chain, pool_chain = sem("dve_chain"), sem("act_chain"), sem("pool_chain")
        rel_s = {n: sem(f"rel_{n}") for n in ("h0", "t0", "t0s", "m1", "h1", "t1", "t1s", "m2", "sb", "sq", "si")}
        use_rel = "att2" in stages

        prev = {}
        before = None
        for st in stages:
            prev[st] = before
            before = st
        OUTS = {}
        for st in stages:
            if st[:4] == "cond":
                OUTS[st] = 2
            elif st[:3] == "ffn":
                OUTS[st] = 1
            elif st[:3] == "att":
                OUTS[st] = 2
            elif st == "self2":
                OUTS[st] = 4
            elif st[:3] == "res":
                OUTS[st] = 1
            else:
                OUTS[st] = 2

        def ready(eng, st):
            if prev[st] is None:
                eng.wait_ge(c_x, 16)
            else:
                eng.wait_ge(S[prev[st]]["out"], OUTS[prev[st]])

        SRC, DST = {}, {}
        at = resid
        for st in stages:
            SRC[st] = at
            if st[:3] == "res":
                DST[st] = resid
            elif st == "self2":
                DST[st] = keep
            elif st == "post2":
                DST[st] = keep
            elif st[:3] == "ffn":
                DST[st] = nxt
            else:
                DST[st] = cur if at is not cur else nxt
            at = DST[st]
        LAST = stages[-1]

        block = ctx.enter_context(nc.Block())

        def weight_users():
            return [st for st in stages if st[:4] == "cond" or st[:3] == "ffn"]

        def free_staging(eng, st, slot):
            users = weight_users()
            k = users.index(st)
            if k:
                u = users[k - 1]
                if u[:3] == "ffn":
                    eng.wait_ge(*S[u].at(f"w_split{slot}", EXPERTS))
                else:
                    eng.wait_ge(*S[u].at("w_split0", 2))

        @block.sync
        def _(sp):
            def load_conditioner(st):
                for slot in range(2):
                    free_staging(sp, st, slot)
                sp.dma_start(w_stage[:, 0:COND_COLS], dram[f"{st}_w"]).then_inc(S[st]["w_dma0"], 16)

            sp.dma_start(small[:, :], dram["small"]).then_inc(c_small, 16)
            sp.dma_start(rows[:, :], dram["rows"].broadcast_to([P, N_ROWS])).then_inc(c_rows, 16)
            sp.dma_start(resid[:, :], dram["xT"]).then_inc(c_x, 16)
            if stages[0][:4] == "cond":
                load_conditioner(stages[0])
            sp.dma_start(sel16[:, :], dram["sel16"]).then_inc(c_sel, 16)
            sp.dma_start(ident16[:, :], dram["ident16"]).then_inc(c_sel, 16)
            sp.dma_start(brow[:, :, :, :].rearrange("p l g k -> p (l g k)"), dram["brow"]).then_inc(c_brow, 16)
            sp.dma_start(mask_u8[:, :], dram["mask"].broadcast_to([P, 2 * TOK])).then_inc(c_mask, 16)
            sp.dma_start(self_w[:, :], dram["self_w"]).then_inc(c_selfw, 16)
            first_att = next((st for st in stages if st[:3] == "att"), None)
            if first_att:
                sp.dma_start(att_w[:, :], dram[f"{first_att}_w"])\
                    .then_inc(c_attw1 if first_att == "att1" else c_attw2, 16)
            if use_rel:
                sp.wait_ge(rel_s["sb"], 2)
                sp.dma_start(relb_dram.ap(), relT[:, :]).then_inc(c_relw, 16)
                sp.wait_ge(c_relw, 16)
                sp.wait_ge(c_brow, 16)
                table = relb_dram.ap().rearrange("(h g) (i k) -> h i g k", h=4, i=SEQ)
                for h in range(4):
                    sp.dma_start(brow[32 * h:32 * h + 32, 1, :, 0:SEQ], table[h]).then_inc(c_relr, 16)
            for st in weight_users():
                s = S[st]
                if st[:4] == "cond":
                    if st != stages[0]:
                        load_conditioner(st)
                    continue
                cols = expert_cols(FFN_KINDS[int(st[3])])[1]
                src = dram[f"{st}_w"]
                for slot in range(2):
                    free_staging(sp, st, slot)
                    sp.dma_start(w_stage[:, slot * STAGE_COLS:slot * STAGE_COLS + cols],
                                 src[slot]).then_inc(s[f"w_dma{slot}"], 16)
                with sp.Fori(1, EXPERTS // 2) as i:
                    for slot in range(2):
                        sp.wait_ge(*s.at(f"w_split{slot}", 2 * i))
                        sp.dma_start(w_stage[:, slot * STAGE_COLS:slot * STAGE_COLS + cols],
                                     src[bass.ds(2 * i + slot, 1)].rearrange("a p c -> (a p) c"))\
                            .then_inc(s[f"w_dma{slot}"], 16)
            sp.wait_ge(S[LAST]["out"], OUTS[LAST])
            sp.dma_start(out, DST[LAST][:, :]).then_inc(out_done, 16)
            sp.wait_ge(out_done, 16)

        @block.gpsimd
        def _(pool):
            chain = Chain(pool, pool_chain)
            if "moe" in shared:
                for n in AHEAD_OF:
                    pool.sem_inc(shared["moe"][n], AHEAD)

            def attention_masks(layer):
                s = S[f"att{layer}"]
                if layer == 2 and "att1" in stages:
                    pool.memset(kbd[:, :], 0.0).then_inc(s["zeroed"], 1)
                else:
                    chain.step(pool.memset(vbd[:, :], 0.0))
                    pool.memset(kbd[:, :], 0.0).then_inc(s["zeroed"], 1)
                if layer == 1:
                    pool.wait_ge(c_mask, 16)
                    pool.wait_ge(c_brow, 16)
                    pool.wait_ge(c_small, 16)
                if layer == 2:
                    pool.wait_ge(c_relr, 64)
                    if "att1" in stages:
                        pool.wait_ge(*S["att1"].at("biased", 2 * TILES))
                    else:
                        pool.wait_ge(c_mask, 16)
                        pool.wait_ge(c_brow, 16)
                        pool.wait_ge(c_small, 16)
                keys = mask_f[:, :].rearrange("p (b k) -> p b k", k=KEYS)
                chain.step(pool.memset(mask_f[:, :], 0.0))
                src = mask_u8[:, (layer - 1) * TOK:layer * TOK].rearrange("p (b k) -> p b k", k=SEQ)
                chain.step(pool.tensor_scalar(keys[:, :, 0:SEQ], src, -1.0, -MASKED, ALU.add, ALU.mult))
                chain.step(pool.tensor_tensor(brow[:, layer - 1, :, :], brow[:, layer - 1, :, :],
                                              sm("causal").rearrange("p (g k) -> p g k", k=KEYS), ALU.add))
                for t in range(TILES):
                    for g2 in range(2):
                        b = brow[:, layer - 1, 2 * g2:2 * g2 + 2, :].unsqueeze(1).broadcast_to([P, 4, 2, KEYS])
                        m = keys[:, 4 * t:4 * t + 4, :].unsqueeze(2).broadcast_to([P, 4, 2, KEYS])
                        o = bm[:, (2 * t + g2) * 8 * KEYS:(2 * t + g2 + 1) * 8 * KEYS]
                        pool.tensor_tensor(o.rearrange("p (b q k) -> p b q k", b=4, q=2), b, m, ALU.add)\
                            .then_inc(s["bm"], 1)

            def attention(st):
                s = S[st]
                if st == "att2":
                    slots = q2[:, :].rearrange("p (s b h i) -> p s h b i", s=2, h=4, i=SEQ)
                    queries = big[:, :].rearrange("p (g b h i) -> p g h b i", g=2, h=4, i=SEQ)
                    for k, (half, g2, h4) in enumerate(Q_ORDER):
                        pool.wait_ge(*s.at("q_sb", k + 1))
                        if k >= 8 and k % 4 == 0:
                            pool.wait_ge(*s.at("ss", k // 4 - 1))
                        q = queries[:, g2, h4, 16 * half:16 * half + 16, :]
                        pool.tensor_tensor(slots[:, (k // 4) % 2, h4, :, :], q, q, ALU.mult).then_inc(s["q2"], 1)
                for t in range(-1, TILES):
                    if t + 1 < TILES:
                        pool.wait_ge(*s.at("rowmax", t + 2))
                        s3 = s_sb[:, (t + 1) % 3, :].rearrange("p (a k) -> p a k", k=KEYS)
                        pool.tensor_tensor(s3, s3, red[:, 0, (t + 1) % 2, :].unsqueeze(2).broadcast_to([P, 16, KEYS]),
                                           ALU.subtract).then_inc(s["sub"], 1)
                    if t < 0:
                        continue
                    pool.wait_ge(*s.at("rsum", t + 1))
                    if t >= 2:
                        pool.wait_ge(*s.at("pt", t - 1))
                    for g2 in range(2):
                        o = p_sb[:, t % 2, g2 * 256:(g2 + 1) * 256].rearrange("p (q b k) -> p b q k", q=2, b=4)
                        e = s_sb[:, t % 3, g2 * 8 * KEYS:(g2 + 1) * 8 * KEYS].rearrange("p (b q k) -> p b q k", b=4, q=2)
                        w = red[:, 1, t % 2, 8 * g2:8 * g2 + 8].rearrange("p (b q) -> p b q", b=4).unsqueeze(3)\
                            .broadcast_to([P, 4, 2, SEQ])
                        pool.tensor_tensor(o, e[:, :, :, 0:SEQ], w, ALU.mult).then_inc(s["p"], 1)

            def self_attention(st):
                s = S[st]
                for t in range(TILES):
                    pool.wait_ge(*s.at("rsum", t + 1))
                    if t >= 2:
                        pool.wait_ge(*s.at("pt", t - 1))
                    o = p_sb[:, t % 2, :].rearrange("p (g b k) -> p b g k", g=4, b=4)
                    e = s_sb[:, t % 3, 0:512].rearrange("p (b g k) -> p b g k", b=4, g=4)
                    w = red[:, 1, t % 2, :].rearrange("p (b g) -> p b g", b=4).unsqueeze(3)\
                        .broadcast_to([P, 4, 4, SEQ])
                    pool.tensor_tensor(o, e, w, ALU.mult).then_inc(s["p"], 1)

            def ffn(st):
                s = S[st]
                kind = FFN_KINDS[int(st[3])]
                per = 4 * kind["chunks"]
                acc = DST[st]

                def low_half(slot, part, i):
                    pool.wait_ge(*s.at(f"w_hi{slot}", 2 * i + (1 if part == "up" else 2)))
                    lo, hi = part_cols(kind, part)
                    base, at = slot * STAGE_COLS, slot * 1024
                    pool.tensor_tensor(w_lo[:, at + lo:at + hi], w_stage[:, base + lo:base + hi],
                                       w_hi[:, at + lo:at + hi], ALU.subtract).then_inc(s[f"w_split{slot}"], 1)

                def accumulate(y, pair):
                    half = y % 2
                    pool.wait_ge(*s.at("wtd", 4 * pair + y + 1))
                    a = acc[:, half * HALF:(half + 1) * HALF]
                    pool.tensor_tensor(a, a, wtd[:, half, :], ALU.add).then_inc(s["acc"], 1)
                    pool.wait_ge(*s.at("acc", 4 * pair + y + 1))

                def pair(i, first=False, last=False):
                    for k in range(per):
                        for slot, part, nxt in splits_at(kind, k, first, last):
                            low_half(slot, part, i + nxt)
                        if weighed_at(kind, k) is not None:
                            accumulate(weighed_at(kind, k), i)
                        if not first and weighed_at(kind, per + k) is not None:
                            accumulate(weighed_at(kind, per + k), i - 1)

                low_half(0, "up", 0)
                low_half(0, "down", 0)
                ready(pool, st)
                chain.step(pool.memset(acc[:, :], 0.0))
                pair(0, first=True)
                with pool.Fori(1, EXPERTS // 2 - 1) as i:
                    pair(i)
                pair(EXPERTS // 2 - 1, last=True)
                for k in range(per, per + WEIGH):
                    if weighed_at(kind, k) is not None:
                        accumulate(weighed_at(kind, k), EXPERTS // 2 - 1)

            def cond(st):
                s = S[st]
                for k, (lo, hi) in enumerate(COND_PARTS):
                    pool.wait_ge(*s.at("w_hi0", k + 1))
                    pool.tensor_tensor(w_lo[:, lo:hi], w_stage[:, lo:hi], w_hi[:, lo:hi], ALU.subtract)\
                        .then_inc(s["w_split0"], 1)
                wide = big[:, 0:4 * TOK].rearrange("p (e t) -> p e t", e=4)
                for k in range(2, 2 * COND_CHUNKS):
                    chunk, half = k // 2, k % 2
                    pool.wait_ge(*s.at("prod", k + 1))
                    pool.wait_ge(*s.at("spread_sb", 2 * (chunk - 1) + half + 1))
                    h = h32[:, k % RING, :]
                    pool.tensor_tensor(h, h, wide[:, chunk - 1, half * HALF:(half + 1) * HALF], ALU.mult)\
                        .then_inc(s["weighed"], 1)

            for st in stages:
                if st[:3] == "att":
                    attention_masks(int(st[3]))
                    attention(st)
                if st == "self2":
                    s = S[st]
                    if "att2" in stages:
                        pool.wait_ge(*S["att2"].at("wo", 2))
                    chain.step(pool.memset(q2[:, :], 0.0))
                    pool.memset(vself, 0.0).then_inc(s["zeroed"], 1)
                    self_attention(st)
                if st[:3] == "ffn":
                    ffn(st)
                if st[:4] == "cond":
                    cond(st)

        @block.tensor
        def _(pe):
            mm = pe.matmul

            def mm3(out, w, x, start, stop):
                mm(out, w[0], x[0], start=start, stop=False)
                mm(out, w[0], x[1], start=False, stop=False)
                return mm(out, w[1], x[0], start=False, stop=stop)

            def router(st):
                s = S[st]
                src = SRC[st]
                lg = psum[:, 7, 0:64]
                for t in range(TILES):
                    o = lg[:, 8 * t:8 * t + 8]
                    extra = st[:4] == "cond" or st == "ffn0"
                    last = mm(o, src[:, t * P:(t + 1) * P], sm(f"{st}_router"), start=True, stop=not extra)
                    if st[:4] == "cond":
                        if t == 0:
                            pe.wait_ge(*s.at("rep", 1))
                        last = mm(o, nxt[0:64, t * P:(t + 1) * P], sm(f"{st}_wg", p=64), start=False, stop=True)
                    if st == "ffn0":
                        last = mm(o, sm("ones_row", p=1), sm("ffn0_brow", p=1), start=False, stop=True)
                last.then_inc(s["logits"], 1)

            def transpose_weights(st):
                s = S[st]
                pe.wait_ge(*s.at("w16", 1))
                wT = psum[0:16, 7, :].bitcast(F16)
                for t in range(TILES):
                    last = pe.transpose(wT[:, t * P:(t + 1) * P], w16[:, t, :], ident16[:, :])
                last.then_inc(s["wT"], 1)

            def spread(st, first, n):
                s = S[st]
                off = EXPERTS if st[:4] == "cond" else 0
                if first == 0:
                    pe.wait_ge(*s.at("wTsb", 1))
                for k in range(first, first + n):
                    e, half = k // 2, k % 2
                    if k >= 2:
                        pe.wait_ge(*s.at("spread_sb", k - 1))
                    mm(psum[:, 6 + k % 2, :], sel16[:, (off + e) * P:(off + e + 1) * P],
                       wT16[:, half * HALF:(half + 1) * HALF], start=True, stop=True).then_inc(s["spread"], 1)

            def ffn(st):
                s = S[st]
                kind = FFN_KINDS[int(st[3])]
                C, gated = kind["chunks"], kind["gated"]
                n_up = 2 if gated else 1
                per = 4 * C
                at = interleave(st)

                def up(i, k):
                    slot, half, c = k // (2 * C), (k // C) % 2, k % C
                    if k % (2 * C) == 0:
                        pe.wait_ge(*s.at(f"w_split{slot}", 2 * i + 1))
                    x = (in_hi[:, half * HALF:(half + 1) * HALF], in_lo[:, half * HALF:(half + 1) * HALF])
                    if gated:
                        pe.wait_ge(*s.at("prod", per * i + k - 1))
                        banks = [2 * (k % 2), 2 * (k % 2) + 1]
                    else:
                        pe.wait_ge(*s.at("act", per * i + k - 3))
                        banks = [k % 4]
                    for u, bank in enumerate(banks):
                        w0 = slot * 1024 + (u * C + c) * P
                        mm3(psum[:, bank, :], (w_hi[:, w0:w0 + P], w_lo[:, w0:w0 + P]), x, True, True)\
                            .then_inc(s["gate" if gated and u == 0 else "up"], 1)

                def down(i, j):
                    slot, half, c = j // (2 * C), (j // C) % 2, j % C
                    if j % (2 * C) == 0:
                        pe.wait_ge(*s.at(f"w_split{slot}", 2 * i + 2))
                    pe.wait_ge(*s.at("hid", per * i + j + 1))
                    if c == 0:
                        pe.wait_ge(*s.at("wtd", 4 * i + j // C - 1))
                    w0 = slot * 1024 + (n_up * C + c) * P
                    mm3(psum[:, 4 + half, :], (w_hi[:, w0:w0 + P], w_lo[:, w0:w0 + P]),
                        (h_hi[:, j % RING, :], h_lo[:, j % RING, :]), c == 0, c == C - 1).then_inc(s["down"], 1)

                router(st)
                pe.wait_ge(*s.at("split", 1))
                done = 0
                for k in range(per):
                    up(0, k)
                    if k == at["transpose"]:
                        transpose_weights(st)
                    if k >= at["spread"] and done < 2 * EXPERTS:
                        spread(st, done, at["pieces"])
                        done += at["pieces"]
                    if k >= LAG:
                        down(0, k - LAG)
                with pe.Fori(1, EXPERTS // 2) as i:
                    for k in range(per):
                        up(i, k)
                        if k >= LAG:
                            down(i, k - LAG)
                        else:
                            down(i - 1, per + k - LAG)
                for j in range(per - LAG, per):
                    down(EXPERTS // 2 - 1, j)

            def cond(st):
                s = S[st]
                router(st)
                pe.wait_ge(*s.at("split", 1))
                pe.wait_ge(*s.at("w_split0", 1))
                for k in range(2 * COND_CHUNKS + COND_LAG):
                    if k == 4:
                        pe.wait_ge(*s.at("w_split0", 2))
                    if k < 2 * COND_CHUNKS:
                        chunk, half = k // 2, k % 2
                        if k >= 2:
                            pe.wait_ge(*s.at("prod", k - 1))
                        x = (in_hi[:, half * HALF:(half + 1) * HALF], in_lo[:, half * HALF:(half + 1) * HALF])
                        for u in range(2):
                            w0 = (3 * chunk + u) * P
                            mm3(psum[:, 2 * (k % 2) + u, :], (w_hi[:, w0:w0 + P], w_lo[:, w0:w0 + P]), x,
                                True, True).then_inc(s[("gate", "up")[u]], 1)
                    if k == 2:
                        transpose_weights(st)
                    if k in COND_SPREAD:
                        spread(st, *COND_SPREAD[k])
                    if k >= COND_LAG:
                        j = k - COND_LAG
                        chunk, half = j // 2, j % 2
                        pe.wait_ge(*s.at("hid", j + 1))
                        w0 = (3 * chunk + 2) * P
                        mm3(psum[:, 4 + half, :], (w_hi[:, w0:w0 + P], w_lo[:, w0:w0 + P]),
                            (h_hi[:, j % RING, :], h_lo[:, j % RING, :]), chunk == 0, chunk == COND_CHUNKS - 1)\
                            .then_inc(s["down"], 1)

            def layer_norm(st):
                s = S[st]
                src = SRC[st]
                for t in range(TILES):
                    last = pe.transpose(psum[:, t // 4, (t % 4) * P:(t % 4 + 1) * P], src[:, t * P:(t + 1) * P], ident)
                    if t % 4 == 3:
                        last.then_inc(s["tr"], 1)
                for t in (0, 4, 1, 5, 2, 6, 3, 7):
                    pe.wait_ge(*s.at("norm" if t < 4 else "norm_act", t % 4 + 1))
                    last = pe.transpose(psum[:, 2 + t // 4, (t % 4) * P:(t % 4 + 1) * P], tok[:, t, :], ident)
                    if t % 4 == 3:
                        last.then_inc(s["back"], 1)

            def attention(st):
                s = S[st]
                layer = int(st[3])
                src = SRC[st]
                pe.wait_ge(c_attw1 if layer == 1 else c_attw2, 16)
                Wq, Wk, Wv = att_w[:, 0:TOK], att_w[:, TOK:TOK + P], att_w[:, TOK + P:TOK + P + 64]
                Wo = att_w[:, TOK + P + 64:].rearrange("p (c n) -> p c n", c=8)
                for half in range(2):
                    mm(psum[:, half, :], Wk, src[:, half * HALF:(half + 1) * HALF], start=True, stop=True)\
                        .then_inc(s["k"], 1)
                for t in range(TILES):
                    last = mm(psum[:, 2, t * 64:(t + 1) * 64], src[:, t * P:(t + 1) * P], Wv, start=True, stop=True)
                last.then_inc(s["v"], 1)
                def key_norms():
                    pe.wait_ge(*s.at("sq", 1))
                    for k in range(3):
                        last = mm(psum[:, (0, 1, 7)[k], 0:352], sm("ones_block"), k_square[:, k * 352:(k + 1) * 352],
                                  start=True, stop=True)
                    last.then_inc(s["ssq"], 1)

                def query_norms(group, first, n):
                    half, g2 = group // 2, group % 2
                    if first == 0:
                        pe.wait_ge(*s.at("q2", 4 * group + 4))
                        pe.wait_ge(*s.at("k_sb", 1))
                    for b in range(16 * half + first, 16 * half + first + n):
                        at, slot = (g2 * BATCH + b) * 2, (group % 2) * 16 + b % 16
                        last = mm(psum[:, (4, 7)[half], at:at + 2], q2[:, slot * P:(slot + 1) * P], sm("ones_pair"), start=True,
                                  stop=True)
                    if first + n == 16:
                        last.then_inc(s["ss"], 1)

                for k, (half, g2, h4) in enumerate(Q_ORDER):
                    c = 4 * g2 + h4
                    if k >= 3:
                        pe.wait_ge(*s.at("q_sb", k - 2))
                    mm(psum[:, Q_BANKS[k % 3], :], Wq[:, c * P:(c + 1) * P], src[:, half * HALF:(half + 1) * HALF],
                       start=True, stop=True).then_inc(s["q"], 1)
                    if layer == 2 and k == 4:
                        key_norms()
                    if layer == 2 and k >= 6:
                        group, quarter = divmod(k - 6, 4)
                        query_norms(group, 4 * quarter, 4)
                pe.wait_ge(*s.at("q_sb", 16))
                pe.wait_ge(*s.at("kk", 1))
                pe.wait_ge(*s.at("v_sb", 1))

                def scores(t):
                    if t >= 2:
                        pe.wait_ge(*s.at("biased", 2 * t - 2))
                    for g2 in range(2):
                        bank = (0, 1, 2, 5)[2 * (t % 2) + g2]
                        for b in range(4):
                            n = 4 * t + b
                            last = mm(psum[:, bank, b * 66:(b + 1) * 66],
                                      big[:, (g2 * BATCH + n) * P:(g2 * BATCH + n + 1) * P],
                                      kbd[:, n * 66:(n + 1) * 66], start=True, stop=True)
                    last.then_inc(s["sc"], 1)

                def transposes(t):
                    pe.wait_ge(*s.at("p", 2 * t + 2))
                    if t >= 2:
                        pe.wait_ge(*s.at("pt_sb", t - 1))
                    for g in range(4):
                        last = pe.transpose(psum[:, 6 + t % 2, g * P:(g + 1) * P], p_sb[:, t % 2, g * P:(g + 1) * P],
                                            ident)
                    last.then_inc(s["pt"], 1)

                def contexts(t):
                    pe.wait_ge(*s.at("pt_sb", t + 1))
                    if t >= 1:
                        pe.wait_ge(*s.at("o", 4 * t))
                    for bp in range(2):
                        v0 = t * 256 + bp * P
                        mm(psum[:, 3 + bp, :], vbd[:, v0:v0 + P], pT[:, t % 2, :], start=True, stop=True)\
                            .then_inc(s["pv"], 1)

                o = oT[:, :].rearrange("p (n c i) -> p c n i", c=8, i=SEQ)

                def project(half, pairs):
                    for c in pairs:
                        last = mm(psum[:, half, :], Wo[:, c, :], o[:, c, 16 * half:16 * half + 16, :],
                                  start=c == 0, stop=c == 7)
                    if c == 7:
                        last.then_inc(s["wo"], 1)

                scores(0)
                scores(1)
                if layer == 2:
                    query_norms(2, 8, 8)
                    query_norms(3, 0, 16)
                for t in range(TILES + 1):
                    if t + 2 < TILES:
                        scores(t + 2)
                    if t < TILES:
                        transposes(t)
                    if t >= 1:
                        contexts(t - 1)
                    if t == 6:
                        pe.wait_ge(*s.at("biased", 14))
                    if t >= 6:
                        project(0, ((0, 1, 2), (3, 4, 5), (6, 7))[t - 6])
                pe.wait_ge(*s.at("o", 4 * TILES))
                project(1, range(8))

            def self_attention(st):
                s = S[st]
                src = SRC[st]
                pe.wait_ge(c_selfw, 16)
                for half in range(2):
                    for k in range(2):
                        mm(psum[:, 2 * k + half, :], self_w[:, k * P:(k + 1) * P], src[:, half * HALF:(half + 1) * HALF],
                           start=True, stop=True).then_inc(s["qkv"], 1)
                for t in range(TILES):
                    last = mm(psum[:, 4 + t // 4, (t % 4) * P:(t % 4 + 1) * P], src[:, t * P:(t + 1) * P],
                              self_w[:, 2 * P:3 * P], start=True, stop=True)
                last.then_inc(s["qkv"], 1)
                pe.wait_ge(*s.at("q_sb", 1))
                pe.wait_ge(*s.at("k_sb", 1))
                km = q2[:, :].rearrange("p (g t) -> p g t", g=4)

                def scores(t):
                    if t >= 2:
                        pe.wait_ge(*s.at("sub", t - 1))
                    for b in range(4):
                        n = 4 * t + b
                        last = mm(psum[:, t % 2, b * P:(b + 1) * P], big[:, n * P:(n + 1) * P],
                                  km[:, :, n * SEQ:(n + 1) * SEQ], start=True, stop=True)
                    last.then_inc(s["sc"], 1)

                def transposes(t):
                    pe.wait_ge(*s.at("p", t + 1))
                    if t >= 2:
                        pe.wait_ge(*s.at("pt_sb", t - 1))
                    for g in range(4):
                        last = pe.transpose(psum[:, 2 + t % 2, g * P:(g + 1) * P], p_sb[:, t % 2, g * P:(g + 1) * P],
                                            ident)
                    last.then_inc(s["pt"], 1)

                def contexts(t):
                    pe.wait_ge(*s.at("pt_sb", t + 1))
                    if t == 0:
                        pe.wait_ge(*s.at("v_sb", 1))
                    if t >= 2:
                        pe.wait_ge(*s.at("c", t - 1))
                    for g in range(4):
                        v0 = (t * 4 + g) * P
                        last = mm(psum[:, 4 + t % 2, g * P:(g + 1) * P], pT[:, t % 2, g * P:(g + 1) * P],
                                  vself[:, v0:v0 + P], start=True, stop=True)
                    last.then_inc(s["pv"], 1)

                def context_transpose(t):
                    pe.wait_ge(*s.at("c", t + 1))
                    if t >= 2:
                        pe.wait_ge(*s.at("ct_sb", t - 1))
                    pe.transpose(psum[:, 6 + t % 2, 0:P], tok[:, t, :], ident).then_inc(s["ct"], 1)

                scores(0)
                scores(1)
                for t in range(TILES + 2):
                    if t + 2 < TILES:
                        scores(t + 2)
                    if t < TILES:
                        transposes(t)
                    if 1 <= t <= TILES:
                        contexts(t - 1)
                    if t >= 2:
                        context_transpose(t - 2)
                pe.wait_ge(*s.at("ct_sb", TILES))
                ctxT = oT[:, 0:TOK].rearrange("p (t h i) -> p h t i", h=4, i=SEQ)
                for b in range(4):
                    r = slice(32 * b, 32 * b + 32)
                    for h in range(4):
                        last = mm(psum[:, b, 0:256], self_w[r, (3 + h) * P:(4 + h) * P], ctxT[r, h, :, :],
                                  start=h == 0, stop=h == 3)
                    last.then_inc(s["wo"], 1)

            def relative_bias():
                pe.wait_ge(rel_s["h0"], 1)
                pe.transpose(psum[:, 0, 0:63], rel[0:63, 0, :], sm("ident", 0, 63, 63)).then_inc(rel_s["t0"], 1)
                pe.wait_ge(rel_s["t0s"], 1)
                mm(psum[0:63, 1, 0:P], rel[:, 1, 0:63], sm("relw1"), start=True, stop=True).then_inc(rel_s["m1"], 1)
                pe.wait_ge(rel_s["h1"], 1)
                pe.transpose(psum[:, 2, 0:63], rel[0:63, 2, :], sm("ident", 0, 63, 63)).then_inc(rel_s["t1"], 1)
                pe.wait_ge(rel_s["t1s"], 1)
                for part in range(2):
                    for i in range(16):
                        q = 16 * part + i
                        last = mm(psum[0:16, 3 + part, i * SEQ:(i + 1) * SEQ], sm("relw2"),
                                  rel[:, 3, 31 - q:63 - q], start=True, stop=True)
                last.then_inc(rel_s["m2"], 1)

            k_square = oT[:, 2 * TOK:2 * TOK + BATCH * KEYS]
            pe.wait_ge(c_small, 16)
            pe.wait_ge(c_sel, 32)
            if use_rel:
                relative_bias()
            for st in stages:
                if st[:3] == "res":
                    continue
                ready(pe, st)
                if use_rel and st == stages[0]:
                    pe.wait_ge(rel_s["sb"], 2)
                if st[:4] == "cond":
                    cond(st)
                elif st[:3] == "ffn":
                    ffn(st)
                elif st[:3] == "att":
                    attention(st)
                elif st == "self2":
                    self_attention(st)
                else:
                    layer_norm(st)

        @block.vector
        def _(dve):
            chain = Chain(dve, dve_chain)
            stt, tt, ts = dve.scalar_tensor_tensor, dve.tensor_tensor, dve.tensor_scalar

            def r8(k):
                return rt[:, k, :].rearrange("p (t e) -> p t e", e=8)

            def router_top(st):
                s = S[st]
                dve.wait_ge(*s.at("logits", 1))
                chain.step(ts(rt[:, 0, :], psum[:, 7, 0:64], ROUTERS[st]["scale"], None, ALU.mult))
                for t in range(TILES):
                    chain.done(dve.max(r8(1)[:, t, :], r8(0)[:, t, :]))
                chain.wait()
                tt(r8(2), r8(0), r8(1)[:, :, 0:1].broadcast_to([P, 8, 8]), ALU.subtract).then_inc(s["lg_sb"], 1)

            def router_mask(st):
                lg, top, m0, m1, fi = r8(0), r8(1), r8(3), r8(4), r8(6)
                for t in range(TILES):
                    chain.done(dve.max_index(rt_idx[:, 8 * t:8 * t + 8], top[:, t, :], lg[:, t, :]))
                chain.wait()
                chain.step(dve.tensor_copy(rt[:, 6, :], rt_idx[:, :]))
                iota = sm("iota").unsqueeze(1).broadcast_to([P, 8, 8])
                chain.done(tt(m0, iota, fi[:, :, 0:1].broadcast_to([P, 8, 8]), ALU.is_equal))
                if ROUTERS[st]["keep"] == 2:
                    chain.step(tt(m1, iota, fi[:, :, 1:2].broadcast_to([P, 8, 8]), ALU.is_equal))
                    chain.step(tt(m0, m0, m1, ALU.add))
                chain.wait()

            def router_weights(st):
                s, r = S[st], ROUTERS[st]
                ex, m0, em = r8(7), r8(3), r8(5)
                dve.wait_ge(*s.at("ex", 1))
                chain.done(dve.reduce_sum(rt[:, 8, 0:8], ex, AX_X))
                chain.step(tt(em, ex, m0, ALU.mult))
                if r["norm"]:
                    chain.step(dve.reduce_sum(rt[:, 8, 8:16], em, AX_X))
                    chain.step(stt(rt[:, 8, 16:24], rt[:, 8, 0:8], r["eps"], rt[:, 8, 8:16], ALU.mult, ALU.add))
                    chain.step(dve.reciprocal(rt[:, 8, 24:32], rt[:, 8, 16:24]))
                else:
                    chain.step(dve.reciprocal(rt[:, 8, 24:32], rt[:, 8, 0:8]))
                chain.step(tt(r8(9), em, rt[:, 8, 24:32].unsqueeze(2).broadcast_to([P, 8, 8]), ALU.mult))
                chain.step(dve.tensor_copy(w16[:, :, 0:8], r8(9)))
                tt(w16[:, :, 8:16], r8(9), w16[:, :, 0:8], ALU.subtract).then_inc(s["w16"], 1)

            def router_copy(st):
                s = S[st]
                dve.wait_ge(*s.at("wT", 1))
                dve.tensor_copy(wT16[:, :], psum[0:16, 7, :].bitcast(F16)).then_inc(s["wTsb"], 1)

            def split_input(st):
                s = S[st]
                chain.step(dve.tensor_copy(in_hi[:, :], SRC[st][:, :]))
                tt(in_lo[:, :], SRC[st][:, :], in_hi[:, :], ALU.subtract).then_inc(s["split"], 1)

            def ffn(st):
                s = S[st]
                kind = FFN_KINDS[int(st[3])]
                C, gated = kind["chunks"], kind["gated"]
                per = 4 * C
                at = interleave(st)
                wide = big[:, :].rearrange("p (e t) -> p e t", e=8)
                links = 0 if gated else per

                def hidden(i, k):
                    r = k % RING
                    dve.wait_ge(*s.at("act", per * i + k + 1))
                    dve.wait_ge(*s.at("down", per * i + k - RING + 1))
                    chain.step(dve.tensor_copy(h_hi[:, r, :], h32[:, r, :]))
                    tt(h_lo[:, r, :], h32[:, r, :], h_hi[:, r, :], ALU.subtract).then_inc(s["hid"], 1)

                def product(i, k):
                    slot, c, r = k // (2 * C), k % C, k % RING
                    dve.wait_ge(*s.at("act", per * i + k + 1))
                    dve.wait_ge(*s.at("up", per * i + k + 1))
                    dve.wait_ge(*s.at("hid", per * i + k - RING + 1))
                    ub = w_bias[:, slot * 12 + 1 + c:slot * 12 + 2 + c]
                    stt(h32[:, r, :], psum[:, 2 * (k % 2) + 1, :], ub, gate32[:, k % 2, :],
                        ALU.add, ALU.mult).then_inc(s["prod"], 1)

                def low_of_product(i, k):
                    r = k % RING
                    dve.wait_ge(*s.at("high", per * i + k + 1))
                    stt(h_lo[:, r, :], h32[:, r, :], 1.0 / WSCALE, h_hi[:, r, :], ALU.mult,
                        ALU.subtract).then_inc(s["hid"], 1)

                def weigh(i, y):
                    slot, half = y // 2, y % 2
                    dve.wait_ge(*s.at("down", per * i + C * (y + 1)))
                    dve.wait_ge(*s.at("acc", 4 * i + y - 1))
                    w = wide[:, bass.ds(2 * i + slot, 1), half * HALF:(half + 1) * HALF].rearrange("p a t -> p (a t)")
                    stt(wtd[:, half, :], psum[:, 4 + half, :], w_bias[:, slot * 12:slot * 12 + 1], w,
                        ALU.add, ALU.mult).then_inc(s["wtd"], 1)

                def step(i, k, first=False):
                    if gated:
                        product(i, k)
                        if not first or k:
                            low_of_product(i, k - 1)
                    else:
                        hidden(i, k)
                    if first and k == at["mask"]:
                        router_mask(st)
                    if first and k == at["weights"]:
                        router_weights(st)
                    if first and k == at["copy"]:
                        router_copy(st)
                    y = weighed_at(kind, k)
                    if y is not None:
                        if first:
                            dve.wait_ge(*s.at("spread_sb", y + 1))
                        weigh(i, y)
                    y = weighed_at(kind, per + k)
                    if y is not None and not first:
                        weigh(i - 1, y)

                split_input(st)
                router_top(st)
                for k in range(per):
                    step(0, k, first=True)
                dve.wait_ge(*s.at("spread_sb", 2 * EXPERTS))
                base = chain.n
                with dve.Fori(1, EXPERTS // 2) as i:
                    chain.n = base + (i - 1) * links
                    for k in range(per):
                        step(i, k)
                chain.n = base + links * (EXPERTS // 2 - 1)
                if gated:
                    low_of_product(EXPERTS // 2 - 1, per - 1)
                for k in range(per, per + WEIGH):
                    if weighed_at(kind, k) is not None:
                        weigh(EXPERTS // 2 - 1, weighed_at(kind, k))
                dve.wait_ge(*s.at("acc", 2 * EXPERTS))
                dve.sem_inc(s["out"], 1)

            def cond_input(st):
                s = S[st]
                dve.tensor_copy(nxt[0:64, :].rearrange("p (b i) -> p b i", i=SEQ),
                                sm("condT", p=64).unsqueeze(2).broadcast_to([64, BATCH, SEQ])).then_inc(s["rep"], 1)
                split_input(st)

            def cond(st, prepared):
                s = S[st]
                if not prepared:
                    cond_input(st)
                router_top(st)
                for k in range(2 * COND_CHUNKS + 2):
                    if k < 2 * COND_CHUNKS:
                        r = k % RING
                        dve.wait_ge(*s.at("act", k + 1))
                        if k >= RING:
                            dve.wait_ge(*s.at("hid", k - RING + 1))
                        g = gate32[:, k % 2, :]
                        chain.step(stt(h32[:, r, :], g, 0.01, g, ALU.mult, ALU.max))
                        dve.wait_ge(*s.at("up", k + 1))
                        stt(h32[:, r, :], psum[:, 2 * (k % 2) + 1, :], 1.0 / WSCALE, h32[:, r, :],
                            ALU.mult, ALU.mult).then_inc(s["prod"], 1)
                    if k == 0:
                        router_mask(st)
                        router_weights(st)
                    if k == 2:
                        router_copy(st)
                    if k >= 2:
                        r = (k - 2) % RING
                        dve.wait_ge(*s.at("high", k - 1))
                        tt(h_lo[:, r, :], h32[:, r, :], h_hi[:, r, :], ALU.subtract).then_inc(s["hid"], 1)

            def layer_norm(st):
                s = S[st]
                for t in range(TILES):
                    if t % 4 == 0:
                        dve.wait_ge(*s.at("tr", t // 4 + 1))
                    chain.done(dve.bn_stats(st6[:, t, :], psum[:, t // 4, (t % 4) * P:(t % 4 + 1) * P]))
                chain.wait()
                for t in range(TILES):
                    last = dve.bn_aggr(mv[:, t, :], st6[:, t, :])
                    chain.done(last)
                chain.wait()
                dve.sem_inc(s["stats"], 1)
                dve.wait_ge(*s.at("sq", 1))
                chain.step(dve.reciprocal(rstd[:, :], sq8[:, :]))
                stt(nmr[:, :], mv[:, :, 0], -1.0, rstd[:, :], ALU.mult, ALU.mult).then_inc(s["inv"], 1)
                for t in range(TILES // 2):
                    ts(tok[:, t, :], psum[:, t // 4, (t % 4) * P:(t % 4 + 1) * P], mv[:, t, 0:1], rstd[:, t:t + 1],
                       ALU.subtract, ALU.mult).then_inc(s["norm"], 1)
                dve.wait_ge(*s.at("back", 2))
                beta = sm(f"{st}_b") if st[:2] == "ln" else None
                ts(DST[st][:, HALF:TOK], psum[:, 3, :], sm(f"{st}_g"), beta, ALU.mult,
                   *([ALU.add] if beta is not None else [])).then_inc(s["out"], 1)

            def attention(st):
                s = S[st]
                layer = int(st[3])
                kv = kbd[:, :].rearrange("p (b q k) -> p b q k", q=2, k=KEYS)
                nk = sm("nk1")
                dve.wait_ge(*s.at("zeroed", 1))
                dve.wait_ge(*s.at("k", 2))
                if layer == 1:
                    for p in range(2):
                        r = slice(64 * p, 64 * p + 64)
                        for half in range(2):
                            chain.done(dve.tensor_copy(
                                kv[r, 16 * half:16 * half + 16, p, 0:SEQ],
                                psum[r, half, :].rearrange("p (b k) -> p b k", k=SEQ)))
                        chain.done(dve.tensor_copy(kv[r, :, p, SEQ], nk[r, :].broadcast_to([64, BATCH])))
                    chain.wait()
                    dve.sem_inc(s["kk"], 1)
                else:
                    flat = oT[:, 0:BATCH * KEYS]
                    k33 = flat.rearrange("p (b k) -> p b k", k=KEYS)
                    for half in range(2):
                        chain.done(dve.tensor_copy(k33[:, 16 * half:16 * half + 16, 0:SEQ],
                                                   psum[:, half, :].rearrange("p (b k) -> p b k", k=SEQ)))
                    chain.step(dve.tensor_copy(k33[:, :, SEQ], nk.broadcast_to([P, BATCH])))
                    tt(oT[:, 2 * TOK:2 * TOK + BATCH * KEYS], flat, flat, ALU.mult).then_inc(s["sq"], 1)
                    dve.wait_ge(*s.at("k_sb", 1))
                    nrm = oT[:, 4 * TOK:4 * TOK + BATCH * KEYS]
                    chain.step(ts(nrm, nrm, 1e-12, None, ALU.max))
                    chain.step(dve.reciprocal(nrm, nrm))
                    chain.step(tt(flat, flat, nrm, ALU.mult))
                    chain.step(ts(flat, flat, sm("qs2"), sm("ks2"), ALU.mult, ALU.mult))
                    for p in range(2):
                        r = slice(64 * p, 64 * p + 64)
                        chain.done(dve.tensor_copy(kv[r, :, p, :], k33[r, :, :]))
                    chain.wait()
                    dve.sem_inc(s["kk"], 1)
                dve.wait_ge(*s.at("v", 1))
                vb = vbd[:, :].rearrange("p (t b d) -> p t b d", b=4, d=64)
                for b in range(4):
                    r = slice(32 * b, 32 * b + 32)
                    chain.done(tt(vb[r, :, b, :], psum[r, 2, :].rearrange("p (t d) -> p t d", d=64),
                                  rw("nvrow")[r, :].unsqueeze(1).broadcast_to([32, TILES, 64]), ALU.subtract))
                chain.wait()
                dve.sem_inc(s["v_sb"], 1)
                rqv = rq[:, :].rearrange("p (g b q) -> p g b q", g=2, q=2)

                def query_scales(half):
                    dve.wait_ge(*s.at("rq", half + 1))
                    r = rq[:, :].rearrange("p (g h x) -> p g h x", g=2, h=2)[:, :, half, :]
                    chain.step(ts(r, r, 1e-12, None, ALU.max))
                    chain.step(dve.reciprocal(r, r))
                    chain.step(ts(r, r, 8.0, None, ALU.mult))

                dve.wait_ge(*s.at("bm", 2 * TILES))
                for t in range(-1, TILES):
                    if t + 1 < TILES:
                        n = t + 1
                        if layer == 2 and n % 4 == 0:
                            query_scales(n // 4)
                        dve.wait_ge(*s.at("sc", n + 1))
                        if n >= 3:
                            dve.wait_ge(*s.at("p", 2 * (n - 3) + 2))
                        for g2 in range(2):
                            sl = s_sb[:, n % 3, g2 * 8 * KEYS:(g2 + 1) * 8 * KEYS]
                            table = bm[:, (2 * n + g2) * 8 * KEYS:(2 * n + g2 + 1) * 8 * KEYS]
                            src = psum[:, (0, 1, 2, 5)[2 * (n % 2) + g2], 0:8 * KEYS]
                            if layer == 2:
                                w = rqv[:, g2, 4 * n:4 * n + 4, :].rearrange("p b q -> p (b q)").unsqueeze(2)\
                                    .broadcast_to([P, 8, KEYS])
                                chain.step(tt(sl.rearrange("p (a k) -> p a k", k=KEYS),
                                              src.rearrange("p (a k) -> p a k", k=KEYS), w, ALU.mult))
                                src = sl
                            tt(sl, src, table, ALU.add).then_inc(s["biased"], 1)
                        dve.wait_ge(*s.at("biased", 2 * n + 2))
                        s3 = s_sb[:, n % 3, :].rearrange("p (a k) -> p a k", k=KEYS)
                        dve.reduce_max(red[:, 0, n % 2, :], s3, AX_X).then_inc(s["rowmax"], 1)
                    if 0 <= t < TILES:
                        dve.wait_ge(*s.at("ex", t + 1))
                        if t >= 2:
                            dve.wait_ge(*s.at("p", 2 * (t - 2) + 2))
                        s3 = s_sb[:, t % 3, :].rearrange("p (a k) -> p a k", k=KEYS)
                        total = red[:, 1, t % 2, :]
                        chain.step(dve.reduce_sum(total, s3, AX_X))
                        dve.reciprocal(total, total).then_inc(s["rsum"], 1)

            def self_attention(st):
                s = S[st]
                qm = big[:, 0:4 * TOK].rearrange("p (b h i) -> p h b i", h=4, i=SEQ)
                dve.wait_ge(*s.at("qkv", 4))
                for half in range(2):
                    for h in range(4):
                        chain.done(ts(qm[:, h, 16 * half:16 * half + 16, :],
                                      psum[:, half, :].rearrange("p (b i) -> p b i", i=SEQ), sm("bq"), sm("headmask", h, 1),
                                      ALU.add, ALU.mult))
                chain.wait()
                dve.sem_inc(s["q_sb"], 1)
                dve.wait_ge(*s.at("qkv", 5))
                dve.wait_ge(*s.at("zeroed", 1))
                vb = vself.rearrange("p (t g b d) -> p t g b d", g=4, b=4, d=32)
                bv = rw("bv").rearrange("p (g d) -> p g d", g=4)
                for half in range(2):
                    for b in range(4):
                        r = slice(32 * b, 32 * b + 32)
                        src = psum[r, 4 + half, :].rearrange("p (t g d) -> p t g d", g=4, d=32)
                        chain.done(tt(vb[r, 4 * half:4 * half + 4, :, b, :], src,
                                      bv[r, :, :].unsqueeze(1).broadcast_to([32, 4, 4, 32]), ALU.add))
                chain.wait()
                dve.sem_inc(s["v_sb"], 1)
                for t in range(-1, TILES + 1):
                    if t + 1 < TILES:
                        n = t + 1
                        dve.wait_ge(*s.at("sc", n + 1))
                        if n >= 3:
                            dve.wait_ge(*s.at("p", n - 2))
                        s3 = s_sb[:, n % 3, 0:512].rearrange("p (a k) -> p a k", k=SEQ)
                        src = psum[:, n % 2, :].rearrange("p (a k) -> p a k", k=SEQ)
                        chain.step(dve.reduce_max(red[:, 0, n % 2, :], src, AX_X))
                        tt(s3, src, red[:, 0, n % 2, :].unsqueeze(2).broadcast_to([P, 16, SEQ]), ALU.subtract)\
                            .then_inc(s["sub"], 1)
                    if 0 <= t < TILES:
                        dve.wait_ge(*s.at("ex", t + 1))
                        if t >= 2:
                            dve.wait_ge(*s.at("p", t - 1))
                        s3 = s_sb[:, t % 3, 0:512].rearrange("p (a k) -> p a k", k=SEQ)
                        total = red[:, 1, t % 2, :]
                        chain.step(dve.reduce_sum(total, s3, AX_X))
                        dve.reciprocal(total, total).then_inc(s["rsum"], 1)
                    if t >= 1:
                        m = t - 1
                        dve.wait_ge(*s.at("pv", m + 1))
                        for h in range(4):
                            r = slice(32 * h, 32 * h + 32)
                            c = psum[r, 4 + m % 2, :].rearrange("p (g b h d) -> p b g h d", g=4, b=4, h=4)[:, :, :, h, :]
                            chain.done(dve.tensor_copy(tok[r, m, :].rearrange("p (b g d) -> p b g d", b=4, g=4), c))
                        chain.wait()
                        dve.sem_inc(s["c"], 1)
                x = keep[:, :].rearrange("p (t b i) -> p t b i", b=4, i=SEQ)
                for b in range(4):
                    dve.wait_ge(*s.at("wo", b + 1))
                    stt(x[:, :, b, :], psum[:, b, 0:256].rearrange("p (t i) -> p t i", i=SEQ), sm("bo"),
                        x[:, :, b, :], ALU.add, ALU.add).then_inc(s["out"], 1)

            def relative_layer(k):
                n = 63
                a, m, q, r0 = rel[0:n, 4, :], mv[0:n, 0, :], sq8[0:n, 0:1], rstd[0:n, 0:1]
                g_name, b_name = (("relg0", "relb0"), ("relg1", "relb1"))[k]
                if k == 0:
                    chain.step(stt(a, rw("relw0", n), sm("posm", p=n), rw("relb0", n), ALU.mult, ALU.add))
                else:
                    dve.wait_ge(rel_s["m1"], 1)
                    chain.step(tt(a, psum[0:n, 1, 0:P], rw("relb1", n), ALU.add))
                chain.step(dve.bn_stats(st6[0:n, 0, :], a))
                chain.step(dve.bn_aggr(m, st6[0:n, 0, :]))
                dve.sem_inc(rel_s["sq"], 1)
                dve.wait_ge(rel_s["sq"], 2 * k + 2)
                chain.step(dve.reciprocal(r0, q))
                chain.step(ts(a, a, m[:, 0:1], r0, ALU.subtract, ALU.mult))
                tt(a, a, rw(g_name, n), ALU.mult).then_inc(rel_s["si"], 1)
                if k == 0:
                    dve.wait_ge(rel_s["t0"], 1)
                    dve.tensor_copy(rel[:, 1, 0:n], psum[:, 0, 0:n]).then_inc(rel_s["t0s"], 1)
                else:
                    dve.wait_ge(rel_s["t1"], 1)
                    dve.tensor_copy(rel[:, 3, 0:n], psum[:, 2, 0:n]).then_inc(rel_s["t1s"], 1)

            dve.wait_ge(c_small, 16)
            dve.wait_ge(c_rows, 16)
            prepared = use_rel and stages[0][:4] == "cond"
            if use_rel:
                relative_layer(0)
                if prepared:
                    ready(dve, stages[0])
                    cond_input(stages[0])
                relative_layer(1)
            for st in stages:
                ready(dve, st)
                s = S[st]
                if st[:3] == "res":
                    add = SRC[st]
                    if st == "res2":
                        chain.step(tt(resid[:, :], resid[:, :], keep[:, :], ALU.add))
                    tt(resid[:, :], resid[:, :], add[:, :], ALU.add).then_inc(s["out"], 1)
                elif st[:4] == "cond":
                    cond(st, prepared and st == stages[0])
                elif st[:3] == "ffn":
                    ffn(st)
                elif st[:3] == "att":
                    attention(st)
                elif st == "self2":
                    self_attention(st)
                else:
                    layer_norm(st)

        @block.scalar
        def _(act):
            chain = Chain(act, act_chain)
            fn = act.activation

            def preload(func):
                chain.step(fn(table_probe[:, :], sm("eps"), func))

            def router(st):
                s = S[st]
                preload(ACT.Exp)
                act.wait_ge(*s.at("lg_sb", 1))
                fn(rt[:, 7, :], rt[:, 2, :], ACT.Exp).then_inc(s["ex"], 1)

            def spread(st, first, n):
                s = S[st]
                scale = 1.0 if st[:4] == "cond" else 1.0 / WSCALE
                for k in range(first, first + n):
                    act.wait_ge(*s.at("spread", k + 1))
                    fn(big[:, k * HALF:(k + 1) * HALF], psum[:, 6 + k % 2, :], ACT.Copy, scale=scale)\
                        .then_inc(s["spread_sb"], 1)

            def halves_free(st):
                users = weight_users()
                k = users.index(st)
                if k:
                    u = users[k - 1]
                    act.wait_ge(*S[u].at("down", ffn_steps(u)))
                    if u[:3] == "ffn":
                        act.wait_ge(*S[u].at("wtd", 2 * EXPERTS))

            def high_half(st, slot, part, i):
                s = S[st]
                kind = FFN_KINDS[int(st[3])]
                n, cols = expert_cols(kind)
                base, bias = slot * STAGE_COLS, slot * 12
                lo, hi = part_cols(kind, part)
                if part == "up":
                    act.wait_ge(*s.at(f"w_dma{slot}", 16 * (i + 1)))
                    if kind["gated"]:
                        c = kind["chunks"]
                        chain.done(fn(w_bias[:, bias + 1:bias + 1 + c], w_stage[:, base + n + 1:base + n + 1 + c],
                                      ACT.Copy, scale=WSCALE))
                        chain.done(fn(w_bias[:, bias + 1 + c:bias + 1 + 2 * c],
                                      w_stage[:, base + n + 1 + c:base + n + 1 + 2 * c], ACT.Copy))
                    else:
                        chain.done(fn(w_bias[:, bias + 1:bias + cols - n], w_stage[:, base + n + 1:base + cols],
                                      ACT.Copy))
                else:
                    chain.done(fn(w_bias[:, bias:bias + 1], w_stage[:, base + n:base + n + 1], ACT.Copy, scale=WSCALE))
                chain.step(fn(w_stage[:, base + lo:base + hi], w_stage[:, base + lo:base + hi], ACT.Copy, scale=WSCALE))
                fn(w_hi[:, slot * 1024 + lo:slot * 1024 + hi], w_stage[:, base + lo:base + hi], ACT.Copy)\
                    .then_inc(s[f"w_hi{slot}"], 1)

            def ffn(st):
                s = S[st]
                kind = FFN_KINDS[int(st[3])]
                C, gated = kind["chunks"], kind["gated"]
                per = 4 * C
                pairs = EXPERTS // 2

                def split_part(slot, part, i, nxt):
                    if part == "up":
                        act.wait_ge(*s.at("up", per * i + 2 * C * nxt))
                        act.wait_ge(*s.at("act", per * i + 2 * C * nxt))
                        if gated:
                            act.wait_ge(*s.at("prod", per * i + 2 * C * nxt))
                    else:
                        ahead = nxt if slot == 0 and nxt else slot - 1
                        act.wait_ge(*s.at("down", per * i + 2 * C * ahead))
                        act.wait_ge(*s.at("wtd", 4 * i + 2 * ahead))
                    high_half(st, slot, part, i + nxt)

                def high_of_product(i, k):
                    r = k % RING
                    act.wait_ge(*s.at("prod", per * i + k + 1))
                    act.wait_ge(*s.at("down", per * i + k - RING + 1))
                    fn(h_hi[:, r, :], h32[:, r, :], ACT.Copy, scale=1.0 / WSCALE).then_inc(s["high"], 1)

                def pair(i, first=False, last=False):
                    done = 0
                    for k in range(per):
                        slot, c = k // (2 * C), k % C
                        for split_slot, part, nxt in splits_at(kind, k, first, last):
                            split_part(split_slot, part, i, nxt)
                        act.wait_ge(*s.at("gate" if gated else "up", per * i + k + 1))
                        b = slot * 12 + 1 + c + (C if gated else 0)
                        if gated:
                            act.wait_ge(*s.at("prod", per * i + k - 1))
                            dst, bank = gate32[:, k % 2, :], 2 * (k % 2)
                        else:
                            act.wait_ge(*s.at("hid", per * i + k - RING + 1))
                            dst, bank = h32[:, k % RING, :], k % 4
                        fn(dst, psum[:, bank, :], kind["func"], bias=w_bias[:, b:b + 1], scale=1.0 / WSCALE)\
                            .then_inc(s["act"], 1)
                        if first and k >= at["spread"] and done < 2 * EXPERTS:
                            spread(st, done, at["pieces"])
                            done += at["pieces"]
                        if gated and (not first or k):
                            high_of_product(i, k - 1)

                at = interleave(st)
                links = sum(3 if gated and part == "up" else 2 for _, _, part, _ in splits(kind))
                router(st)
                pair(0, first=True)
                base_n = chain.n
                with act.Fori(1, pairs - 1) as i:
                    chain.n = base_n + (i - 1) * links
                    pair(i)
                chain.n = base_n + (pairs - 2) * links
                pair(pairs - 1, last=True)
                if gated:
                    high_of_product(pairs - 1, per - 1)

            def cond(st):
                s = S[st]
                router(st)
                for k in range(2 * COND_CHUNKS + 2):
                    if k < 2 * COND_CHUNKS:
                        act.wait_ge(*s.at("gate", k + 1))
                        if k >= 2:
                            act.wait_ge(*s.at("prod", k - 1))
                        fn(gate32[:, k % 2, :], psum[:, 2 * (k % 2), :], ACT.Copy, scale=1.0 / WSCALE)\
                            .then_inc(s["act"], 1)
                    if k in COND_SPREAD:
                        spread(st, *COND_SPREAD[k])
                    if k >= 2:
                        j = k - 2
                        if j < 2:
                            act.wait_ge(*s.at("prod", j + 1))
                        else:
                            act.wait_ge(*s.at("weighed", j - 1))
                        if j >= RING:
                            act.wait_ge(*s.at("down", j - RING + 1))
                        fn(h_hi[:, j % RING, :], h32[:, j % RING, :], ACT.Copy).then_inc(s["high"], 1)
                for half in range(2):
                    act.wait_ge(*s.at("down", 2 * COND_CHUNKS - 1 + half))
                    fn(DST[st][:, half * HALF:(half + 1) * HALF], psum[:, 4 + half, :], ACT.Copy,
                       scale=1.0 / WSCALE).then_inc(s["out"], 1)

            def layer_norm(st):
                s = S[st]
                preload(ACT.Sqrt)
                act.wait_ge(*s.at("stats", 1))
                fn(sq8[:, :], mv[:, :, 1], ACT.Sqrt, bias=sm("eps")).then_inc(s["sq"], 1)
                act.wait_ge(*s.at("inv", 1))
                for t in range(TILES // 2, TILES):
                    fn(tok[:, t, :], psum[:, t // 4, (t % 4) * P:(t % 4 + 1) * P], ACT.Identity,
                       bias=nmr[:, t:t + 1], scale=rstd[:, t:t + 1]).then_inc(s["norm_act"], 1)
                act.wait_ge(*s.at("back", 1))
                kw = dict(bias=sm(f"{st}_b")) if st[:2] == "ln" else {}
                fn(DST[st][:, 0:HALF], psum[:, 2, :], ACT.Identity, scale=sm(f"{st}_g"), **kw).then_inc(s["out"], 1)

            def attention(st):
                s = S[st]
                layer = int(st[3])
                q = big[:, :].rearrange("p (g b h i) -> p g h b i", g=2, h=4, i=SEQ)

                def query_roots(half):
                    act.wait_ge(*s.at("ss", 2 * half + 2))
                    r = rq[:, :].rearrange("p (g h x) -> p g h x", g=2, h=2)[:, :, half, :]
                    b = psum[:, (4, 7)[half], 0:128].rearrange("p (g h x) -> p g h x", g=2, h=2)[:, :, half, :]
                    fn(r, b, ACT.Sqrt).then_inc(s["rq"], 1)

                for k, (half, g2, h4) in enumerate(Q_ORDER):
                    act.wait_ge(*s.at("q", k + 1))
                    fn(q[:, g2, h4, 16 * half:16 * half + 16, :],
                       psum[:, Q_BANKS[k % 3], :].rearrange("p (b i) -> p b i", i=SEQ), ACT.Copy,
                       scale=0.125 if layer == 1 else 1.0).then_inc(s["q_sb"], 1)
                    if layer == 2 and k == 6:
                        act.wait_ge(*s.at("ssq", 1))
                        for n in range(3):
                            chain.done(fn(oT[:, 4 * TOK + n * 352:4 * TOK + (n + 1) * 352],
                                          psum[:, (0, 1, 7)[n], 0:352], ACT.Sqrt))
                        chain.wait()
                        act.sem_inc(s["k_sb"], 1)
                if layer == 2:
                    query_roots(0)
                    query_roots(1)
                preload(ACT.Exp)
                for t in range(-1, TILES + 1):
                    if t + 1 < TILES:
                        act.wait_ge(*s.at("sub", t + 2))
                        e = s_sb[:, (t + 1) % 3, :]
                        fn(e, e, ACT.Exp).then_inc(s["ex"], 1)
                    if 0 <= t < TILES:
                        act.wait_ge(*s.at("pt", t + 1))
                        if t >= 2:
                            act.wait_ge(*s.at("pv", 2 * t - 2))
                        fn(pT[:, t % 2, :], psum[:, 6 + t % 2, :], ACT.Copy).then_inc(s["pt_sb"], 1)
                    if t >= 1:
                        act.wait_ge(*s.at("pv", 2 * t))
                        o = oT[:, :].rearrange("p (t m b g x) -> p t m b g x", t=TILES, m=2, b=2, g=2)
                        for b in range(2):
                            for par in range(2):
                                r, to = slice(64 * b, 64 * b + 64), slice(64 * par, 64 * par + 64)
                                src = psum[r, 3:5, :].rearrange("p m (g q x) -> p m g q x", g=2, q=2)[:, :, :, par, :]
                                fn(o[to, t - 1, :, b, :, :], src, ACT.Identity, bias=sm("nv1")[r, :])\
                                    .then_inc(s["o"], 1)
                for half in range(2):
                    act.wait_ge(*s.at("wo", half + 1))
                    fn(DST[st][:, half * HALF:(half + 1) * HALF], psum[:, half, :], ACT.Copy).then_inc(s["out"], 1)
                if layer == 1 and "att2" in stages:
                    act.wait_ge(*s.at("wo", 2))
                    act.dma_start(att_w[:, :], dram["att2_w"]).then_inc(c_attw2, 16)

            def self_attention(st):
                s = S[st]
                km = q2[:, :].rearrange("p (g t) -> p g t", g=4)
                act.wait_ge(*s.at("zeroed", 1))
                act.wait_ge(*s.at("qkv", 4))
                for half in range(2):
                    for g in range(4):
                        r = slice(32 * g, 32 * g + 32)
                        chain.done(fn(km[r, g, half * HALF:(half + 1) * HALF], psum[r, 2 + half, :], ACT.Identity,
                                      bias=sm("bk")[r, :]))
                chain.wait()
                act.sem_inc(s["k_sb"], 1)
                preload(ACT.Exp)
                for t in range(-1, TILES + 2):
                    if t + 1 < TILES:
                        act.wait_ge(*s.at("sub", t + 2))
                        e = s_sb[:, (t + 1) % 3, 0:512]
                        fn(e, e, ACT.Exp, scale=float(8.0 ** -0.5)).then_inc(s["ex"], 1)
                    if 0 <= t < TILES:
                        act.wait_ge(*s.at("pt", t + 1))
                        if t >= 2:
                            act.wait_ge(*s.at("pv", t - 1))
                        fn(pT[:, t % 2, :], psum[:, 2 + t % 2, :], ACT.Copy).then_inc(s["pt_sb"], 1)
                    if t >= 2:
                        m = t - 2
                        act.wait_ge(*s.at("ct", m + 1))
                        fn(oT[:, m * P:(m + 1) * P], psum[:, 6 + m % 2, 0:P], ACT.Copy).then_inc(s["ct_sb"], 1)

            def relative_layer(k):
                n = 63
                preload(ACT.Sqrt)
                act.wait_ge(rel_s["sq"], 2 * k + 1)
                fn(sq8[0:n, 0:1], mv[0:n, 0, 1:2], ACT.Sqrt, bias=sm("eps", p=n)).then_inc(rel_s["sq"], 1)
                preload(ACT.Silu)
                act.wait_ge(rel_s["si"], k + 1)
                fn(rel[0:n, 2 * k, :], rel[0:n, 4, :], ACT.Silu).then_inc(rel_s["h1" if k else "h0"], 1)

            def relative_table():
                act.wait_ge(rel_s["m2"], 1)
                for part in range(2):
                    fn(relT[:, part * HALF:(part + 1) * HALF], psum[0:16, 3 + part, :], ACT.Identity,
                       bias=sm("relb2", p=16)).then_inc(rel_s["sb"], 1)

            def first_split(st, k):
                if st[:4] == "cond":
                    act.wait_ge(*S[st].at("w_dma0", 16))
                    lo, hi = COND_PARTS[k]
                    chain.step(fn(w_stage[:, lo:hi], w_stage[:, lo:hi], ACT.Copy, scale=WSCALE))
                    fn(w_hi[:, lo:hi], w_stage[:, lo:hi], ACT.Copy).then_inc(S[st]["w_hi0"], 1)
                else:
                    high_half(st, 0, ("up", "down")[k], 0)

            act.wait_ge(c_small, 16)
            if use_rel:
                relative_layer(0)
                if family(stages[0]) != "moe":
                    relative_layer(1)
                    relative_table()
            for st in stages:
                if st[:3] == "res":
                    continue
                if family(st) == "moe":
                    halves_free(st)
                    with_rel = use_rel and st == stages[0]
                    first_split(st, 0)
                    if with_rel:
                        relative_layer(1)
                    first_split(st, 1)
                    if with_rel:
                        relative_table()
                ready(act, st)
                if st[:4] == "cond":
                    cond(st)
                elif st[:3] == "ffn":
                    ffn(st)
                elif st[:3] == "att":
                    attention(st)
                elif st == "self2":
                    self_attention(st)
                else:
                    layer_norm(st)


def constants():
    c = {}
    c["ident"] = np.eye(P)
    c["iota"] = np.tile(np.arange(8.0), (P, 1))
    c["eps"] = np.full((P, 1), LN_EPS)
    c["headmask"] = ((np.arange(P)[:, None] % 32) // 8 == np.arange(4)[None, :])
    c["ones_pair"] = (np.arange(P)[:, None] // 64 == np.arange(2)[None, :])
    c["ones_block"] = (np.arange(P)[:, None] // 64 == np.arange(P)[None, :] // 64)
    future = np.arange(SEQ)[None, :] > (np.arange(P) % SEQ)[:, None]
    causal = np.zeros((P, 4, KEYS))
    causal[:, :, 0:SEQ] = np.where(future, MASKED, 0.0)[:, None, :]
    c["causal"] = causal.reshape(P, 4 * KEYS)
    pos = np.zeros((P, 1))
    pos[0:63, 0] = 31.0 - np.arange(63)
    c["posm"] = pos
    c["ones_row"] = np.ones((P, P))
    return c


def lay_out(i):
    f = np.float32

    def a(name):
        return np.asarray(i[name])

    def col(v):
        return v.reshape(-1, 1)

    def full(v, n=1):
        v = v.reshape(-1, n) if v.ndim == 1 else v
        o = np.zeros((P, v.shape[1]), f)
        o[0:v.shape[0]] = v
        return o

    s = constants()
    cond = a("cond_64")
    twice = lambda v: col(np.concatenate([v, v]))
    for layer in (0, 3):
        s[f"cond{layer}_router"] = a(f"L{layer}_cond_wt").T
        s[f"cond{layer}_wg"] = full(a(f"L{layer}_cond_wg").T)
    s["ffn0_router"] = a("L0_ffn_w_gate")
    s["ffn1_router"] = a("L1_ffn_gate_w").T
    s["ffn2_router"] = a("L2_ffn_w_gate")
    s["ffn3_router"] = a("L3_ffn_router_w").T
    s["condT"] = full(cond.T)
    s["ffn0_brow"] = np.tile(a("L0_ffn_b_gate"), (P, 1))
    s["pre1_g"], s["post1_g"] = col(a("L1_cond_g_in")), col(a("L1_cond_g_out"))
    s["pre2_g"], s["post2_g"] = col(a("L2_cond_g_norm")), col(a("L2_cond_g_out"))
    for n in (1, 2):
        s[f"ln{n}_g"], s[f"ln{n}_b"] = col(a(f"L2_ffn_ln{n}_w")), col(a(f"L2_ffn_ln{n}_b"))
    s["nk1"], s["nv1"], s["nv2"] = twice(cond[0]), twice(cond[1]), twice(cond[1])
    s["qs2"], s["ks2"] = twice(a("L2_cond_q_scale")), twice(a("L2_cond_k_scale"))
    bqkv = a("L2_ffn_b_qkv")
    s["bq"], s["bk"], s["bo"] = col(bqkv[0:P]), col(bqkv[P:2 * P]), col(a("L2_ffn_b_o"))
    s["relw1"] = a("L2_cond_w1")
    heads = np.array([8 * g2 + 2 * h4 + p for h4 in range(4) for g2 in range(2) for p in range(2)])
    s["relw2"] = a("L2_cond_w2")[:, heads]
    s["relb2"] = full(a("L2_cond_b2")[heads])
    small = np.zeros((P, N_SMALL), f)
    for name, (at, n) in SMALL.items():
        small[:, at:at + n] = s[name]

    r = {"relw0": a("L2_cond_w0").reshape(-1), "relb0": a("L2_cond_b0"), "relg0": a("L2_cond_g0"),
         "relb1": a("L2_cond_b1"), "relg1": a("L2_cond_g1"), "nvrow": cond[1], "bv": bqkv[2 * P:]}
    rows = np.concatenate([r[n] for n in ROWS]).reshape(1, N_ROWS)

    d = {"small": small, "rows": rows}
    d["xT"] = a("x").reshape(TOK, P).T
    d["ident16"] = np.eye(P, dtype=np.float16)
    sel = np.zeros((16, 12, P), np.float16)
    for e in range(EXPERTS):
        sel[[e, e + 8], e, :] = 1
        sel[[e, e + 8], 8 + e // 2, 64 * (e % 2):64 * (e % 2) + 64] = 1
    d["sel16"] = sel.reshape(16, 12 * P)
    d["mask"] = np.stack([a("mask_BxS_bk0"), a("mask_BxS_bf1")]).reshape(1, 2 * TOK)
    brow = np.zeros((4, SEQ, 2, 4, KEYS), f)
    hh = heads.reshape(4, 4)
    brow[:, :, 0, :, 0:SEQ] = a("fside_16xSxS_0")[hh].transpose(0, 2, 1, 3)
    for layer in (1, 2):
        brow[:, :, layer - 1, :, SEQ] = a(f"L{layer}_cond_null_attn_bias")[hh][:, None, :]
    d["brow"] = brow.reshape(P, 2 * 4 * KEYS)
    for layer in (0, 3):
        L = f"L{layer}_cond_"
        w = np.zeros((P, COND_CHUNKS, 3, P), f)
        w[:, 0, 0], w[:, 0, 1], w[:, 0, 2] = a(L + "sw_gate"), a(L + "sw_up"), a(L + "sw_down")
        w[:, 1:, 0] = a(L + "w_gate").transpose(1, 0, 2).reshape(P, 4, P)
        w[:, 1:, 1] = a(L + "w_up").transpose(1, 0, 2).reshape(P, 4, P)
        w[:, 1:, 2] = a(L + "w_down").reshape(4, P, P).transpose(1, 0, 2)
        d[f"cond{layer}_w"] = w.reshape(P, COND_COLS)

    def expert_blocks(ups, down, biases, bdown):
        F = down.shape[1]
        c = F // P
        parts = list(ups) + [down.reshape(EXPERTS, c, P, P).transpose(0, 2, 1, 3).reshape(EXPERTS, P, c * P)]
        parts.append(bdown[:, :, None])
        parts += [b.reshape(EXPERTS, c, P).transpose(0, 2, 1) for b in biases]
        return np.concatenate(parts, axis=2)

    d["ffn0_w"] = expert_blocks([a("L0_ffn_W1")], a("L0_ffn_W2"), [a("L0_ffn_b1")], a("L0_ffn_b2"))
    d["ffn1_w"] = expert_blocks([a("L1_ffn_w1").transpose(1, 2, 0)], a("L1_ffn_w2").transpose(1, 2, 0),
                                [a("L1_ffn_b1")], a("L1_ffn_b2"))
    d["ffn2_w"] = expert_blocks([a("L2_ffn_w1")], a("L2_ffn_w2"), [a("L2_ffn_b1")], a("L2_ffn_b2"))
    d["ffn3_w"] = expert_blocks([a("L3_ffn_gate_w"), a("L3_ffn_up_w")], a("L3_ffn_down_w"),
                                [a("L3_ffn_up_b"), a("L3_ffn_gate_b")], a("L3_ffn_down_b"))
    for layer, wo in ((1, "Wo"), (2, "Wout")):
        L = f"L{layer}_cond_"
        kv = a(L + "Wkv")
        o = a(L + wo).reshape(8, P, P).transpose(1, 0, 2).reshape(P, 8 * P)
        d[f"att{layer}_w"] = np.concatenate(
            [a(L + "Wq"), kv[:, 0:64], kv[:, 0:64], kv[:, 64:], o], axis=1)
    wo = a("L2_ffn_w_o").reshape(4, 4, 8, P).transpose(0, 2, 1, 3).reshape(32, 4 * P)
    d["self_w"] = np.concatenate([a("L2_ffn_w_qkv"), np.concatenate([wo] * 4)], axis=1)
    return {k: np.ascontiguousarray(v) for k, v in d.items()}


def make(nc, arrays, stages=None):
    dram = {}
    for name, v in arrays.items():
        dram[name] = nc.dram_tensor(f"in_{name}", v.shape, mybir.dt.from_np(v.dtype), kind="ExternalInput").ap()
    out = nc.dram_tensor("out_xT", (P, TOK), F32, kind="ExternalOutput").ap()
    build_program(nc, dram, out, stages)


def kernel(**inputs):
    import concourse.bacc as bacc
    from concourse.bass_utils import run_bass_kernel_spmd

    arrays = lay_out(inputs)
    nc = bacc.Bacc("TRN2", target_bir_lowering=False, num_devices=1)
    make(nc, arrays)
    r = run_bass_kernel_spmd(nc, [{f"in_{k}": v for k, v in arrays.items()}], core_ids=[0])
    return np.ascontiguousarray(np.asarray(r.results[0]["out_xT"]).T).reshape(BATCH, SEQ, P)
```

```python
from contextlib import ExitStack

import numpy as np

import concourse.bass as bass
from concourse import mybir

ALU = mybir.AluOpType
ACT = mybir.ActivationFunctionType
F32 = mybir.dt.float32
F16 = mybir.dt.float16
U8 = mybir.dt.uint8
U32 = mybir.dt.uint32
AX_X = mybir.AxisListType.X

P = 128
BATCH = 32
SEQ = 32
TOK = BATCH * SEQ
TILES = TOK // P
HALF = 512
EXPERTS = 8
WSCALE = 64.0
MASKED = -1.0e30
KEYS = SEQ + 1
LN_EPS = 1e-5

FFN_KINDS = {
    0: dict(gated=False, chunks=4, func=ACT.Relu),
    1: dict(gated=False, chunks=4, func=ACT.Gelu_apprx_tanh),
    2: dict(gated=False, chunks=4, func=ACT.Gelu_apprx_tanh),
    3: dict(gated=True, chunks=2, func=ACT.Silu),
}
ROUTERS = {
    "cond0": dict(keep=2, norm=True, eps=1e-20, scale=0.5),
    "ffn0": dict(keep=1, norm=False, eps=0.0, scale=1.0),
    "ffn1": dict(keep=2, norm=False, eps=0.0, scale=1.0),
    "ffn2": dict(keep=2, norm=True, eps=0.0, scale=1.0),
    "cond3": dict(keep=2, norm=True, eps=1e-20, scale=0.5),
    "ffn3": dict(keep=2, norm=True, eps=1e-9, scale=1.0),
}
STAGES = ["cond0", "ffn0", "res0", "pre1", "att1", "post1", "ffn1", "res1", "pre2", "att2", "post2",
          "ln1", "self2", "ln2", "ffn2", "res2", "cond3", "ffn3", "res3"]


def expert_cols(kind):
    c = kind["chunks"]
    n_up = 2 if kind["gated"] else 1
    weights = n_up * c * P + c * P
    return weights, weights + 1 + n_up * c


COND_CHUNKS = 5
COND_COLS = COND_CHUNKS * 3 * P
COND_PARTS = [(0, 2 * 3 * P), (2 * 3 * P, COND_COLS)]
COND_SPREAD = {3: (0, 3), 4: (3, 6), 5: (6, 8)}

HEADSEL = 3 * SEQ + 2

SMALL = {}


def _small_layout():
    at = 0
    for name, n in [
        ("ident", P), ("iota", 8), ("eps", 1), ("headmask", 4), ("headsel", HEADSEL + P), ("ones_block", P),
        ("causal", 4 * KEYS),
        ("posm", 1),
        ("cond0_router", 8), ("cond3_router", 8), ("ffn0_router", 8), ("ffn1_router", 8),
        ("ffn2_router", 8), ("ffn3_router", 8),
        ("cond0_wg", 8), ("cond3_wg", 8), ("condT", BATCH), ("ffn0_brow", 8), ("ones_row", P),
        ("pre1_g", 1), ("post1_g", 1), ("pre2_g", 1), ("post2_g", 1), ("ln1_g", 1), ("ln1_b", 1), ("ln2_g", 1),
        ("ln2_b", 1), ("null_key", 1), ("null_value", 1), ("qs2", 1), ("ks2", 1),
        ("bq", 1), ("bk", 1), ("bo", 1), ("relw1", P), ("relw2", 16), ("relb2", 1),
    ]:
        SMALL[name] = (at, n)
        at += n
    return at


N_SMALL = _small_layout()
ROWS = {}


def _row_layout():
    at = 0
    for name, n in [("relw0", P), ("relb0", P), ("relg0", P), ("relb1", P), ("relg1", P),
                    ("null_value_row", 64), ("bv", P)]:
        ROWS[name] = (at, n)
        at += n
    return at


N_ROWS = _row_layout()
N_ATT = TOK + P + 64 + 8 * P
Q_ORDER = [(half, g2, h4) for half in range(2) for g2 in range(2) for h4 in range(4)]
Q_BANKS = (3, 5, 6)
N_SELF = 3 * P + 4 * P


class Chain:

    def __init__(self, eng, sem):
        self.eng, self.sem, self.n = eng, sem, 0

    def done(self, ins):
        ins.then_inc(self.sem, 1)
        self.n = self.n + 1

    def wait(self):
        self.eng.wait_ge(self.sem, self.n)

    def step(self, ins):
        self.done(ins)
        self.wait()


AHEAD, AHEAD_OF = 4, ("wtd", "acc", "up", "act", "hid", "down", "prod", "high")
TABLE_STEP = 1
COND_LAG = 4
LAG = 3
WEIGH = 4


def splits(kind):
    if kind["gated"]:
        return [(0, 0, "down", 0), (1, 1, "up", 0), (4, 1, "down", 0), (5, 0, "up", 1)]
    return [(2, 1, "up", 0), (5, 1, "down", 0), (10, 0, "up", 1), (13, 0, "down", 1)]


def splits_at(kind, k, first=False, last=False):
    return [(slot, part, nxt) for step, slot, part, nxt in splits(kind)
            if step == k and not (last and nxt) and not (first and slot == 0 and not nxt)]


def weighed_at(kind, k):
    y, rest = divmod(k - WEIGH + 1, kind["chunks"])
    return y - 1 if rest == 0 and 1 <= y <= 4 else None


def part_cols(kind, part):
    up = (2 if kind["gated"] else 1) * kind["chunks"] * P
    return (0, up) if part == "up" else (up, up + kind["chunks"] * P)


def interleave(st):
    if FFN_KINDS[int(st[3])]["gated"]:
        return dict(copy=1, transpose=1, spread=2, pieces=3)
    return dict(copy=2, transpose=2, spread=4, pieces=2)


def ffn_steps(st):
    return 2 * COND_CHUNKS if st[:4] == "cond" else 2 * EXPERTS * FFN_KINDS[int(st[3])]["chunks"]


def family(st):
    return "moe" if st[:4] == "cond" or st[:3] == "ffn" else "att" if st[:3] == "att" else \
        "self" if st[:4] == "self" else "norm"


def signals_of(st):
    if family(st) == "moe":
        cond = st[:4] == "cond"
        gated = FFN_KINDS[int(st[3])]["gated"] if st[:3] == "ffn" else False
        steps, n = ffn_steps(st), 1 if cond else EXPERTS // 2
        wide = 8 if cond else 2 * EXPERTS
        second = 0 if cond else n
        outs = 0 if cond else 2 * EXPERTS
        sums = max(outs - 1, 0)
        return dict(logits=1, lg_sb=1, ex=1, w16=1, wT=1, wTsb=1, spread=wide, spread_sb=wide, split=1,
                    w_dma0=16 * n, w_dma1=16 * second, w_hi0=2 * n, w_hi1=2 * second, w_split0=2 * n,
                    w_split1=2 * second,
                    gate=steps if cond or gated else 0, up=steps, act=steps, hid=steps, down=steps, wtd=outs, acc=sums,
                    rep=1 if cond else 0, weighed=steps - 2 if cond else 0,
                    prod=steps if cond or gated else 0, high=steps if cond or gated else 0)
    if family(st) == "att":
        return dict(split=1, wq_hi=1, wq_split=1, q=16, q_sb=16, k=2, kk=1, v=1, v_sb=1, sc=8, biased=16, rowmax=8,
                    sub=8, ex=8, rsum=8, p=16,
                    pt=8, pt_sb=8, pv=16, o=32, wo=2, zeroed=1, bm=16, sq=1, ssq=1, k_sb=1, q2=16,
                     ss=16, ss_rows=2, rq=2)
    if family(st) == "self":
                    return dict(zeroed=1, qkv=5, q_sb=1, k_sb=1, v_sb=2, sc=8, sub=8, ex=8, rsum=8, p=8, pt=8, pt_sb=8, pv=8, c=8,
                    ct=8, ct_sb=8, wo=4)
    return dict(tr=2, stats=1, sq=1, inv=1, norm=4, norm_act=4, back=2)


class Signals:

    def __init__(self, sems, before, out):
        self.sems, self.before = dict(sems, out=out), dict(before, out=0)

    def __getitem__(self, name):
        return self.sems[name]

    def at(self, name, n):
        return self.sems[name], n + self.before[name]


def build_program(nc, dram, out, stages=None):
    stages = STAGES if stages is None else stages
    with ExitStack() as ctx:
        def sb(name, shape, dt=F32):
            return ctx.enter_context(nc.sbuf_tensor(name, shape, dt))

        def sem(name):
            return ctx.enter_context(nc.semaphore(name))

        small = sb("small", [P, N_SMALL])
        rows = sb("rows", [P, N_ROWS])
        sel16 = sb("sel16", [16, 12 * P], F16)
        ident16 = sb("ident16", [P, P], F16)
        resid = sb("resid", [P, TOK])
        cur = sb("cur", [P, TOK])
        nxt = sb("nxt", [P, TOK])
        keep_mask = sb("keep_mask", [P, BATCH * KEYS])
        keep = keep_mask[:, 0:TOK]
        mask_f = keep_mask[:, :]
        in_hi = sb("in_hi", [P, TOK], F16)
        in_lo = sb("in_lo", [P, TOK], F16)
        STAGE_COLS = 1032
        w_stage = sb("w_stage", [P, 2 * STAGE_COLS])
        w_hi = sb("w_hi", [P, 2 * 1024], F16)
        w_lo = sb("w_lo", [P, 2 * 1024], F16)
        w_bias = sb("w_bias", [P, 2 * 12])
        RING = 4
        h32 = sb("h32", [P, RING, HALF])
        h_hi = sb("h_hi", [P, RING, HALF], F16)
        h_lo = sb("h_lo", [P, RING, HALF], F16)
        gate_wtd = sb("gate_wtd", [P, 4 * HALF])
        gate32 = gate_wtd[:, 0:2 * HALF].rearrange("p (r n) -> p r n", r=2)
        wtd = gate_wtd[:, 2 * HALF:4 * HALF].rearrange("p (r n) -> p r n", r=2)
        big = sb("big", [P, 8 * TOK])
        q2 = sb("q2", [P, 4 * TOK])
        kbd = sb("kbd", [P, BATCH * 2 * KEYS])
        vbd = sb("vbd", [P, TILES * 256])
        oT = sb("oT", [P, 16 * 512])
        vself = oT[:, 8 * 512:16 * 512]
        bm = sb("bm", [P, TILES * 16 * KEYS])
        mask_u8 = sb("mask_u8", [P, 2 * TOK], U8)
        brow = sb("brow", [P, 2, 4, KEYS])
        att_w = sb("att_w", [P, N_ATT])
        self_w = sb("self_w", [P, N_SELF])
        p_sb, pT = h32[:, 0:2, :], h32[:, 2:4, :]
        s_sb = gate_wtd[:, 0:3 * 16 * KEYS].rearrange("p (r n) -> p r n", r=3)
        tok = sb("tok", [P, TILES, P])
        st6 = sb("st6", [P, TILES, 6])
        mv = sb("mv", [P, TILES, 2])
        rstd = sb("rstd", [P, TILES])
        sq8 = sb("sq8", [P, TILES])
        rq = sb("rq", [P, BATCH * 4])
        table_probe = sb("table_probe", [P, 1])
        nmr = sb("nmr", [P, TILES])
        red = sb("red", [P, 2, 2, 16])
        rt = kbd[:, 0:768].rearrange("p (k n) -> p k n", n=64)
        rt_idx = sb("rt_idx", [P, 64], U32)
        w16 = kbd[:, 768:832].bitcast(F16).rearrange("p (t e) -> p t e", t=TILES)
        wT16 = kbd[0:16, 832:832 + TOK // 2].bitcast(F16)
        rel = tok
        relT = oT[0:16, 0:TOK]
        psum = ctx.enter_context(nc.psum_tensor("psum", [P, 8, HALF], F32))

        def sm(name, lo=0, n=None, p=P):
            at, width = SMALL[name]
            n = width - lo if n is None else n
            return small[0:p, at + lo:at + lo + n]

        def rw(name, p=P):
            at, width = ROWS[name]
            return rows[0:p, at:at + width]

        ident = sm("ident")
        relb_dram = nc.dram_tensor("relb_scratch", [16, SEQ * SEQ], F32)

        c_small, c_rows, c_sel, c_x, c_attw1, c_attw2, c_selfw, c_mask, c_brow, c_relw, c_relr = (
            sem(n) for n in ("c_small", "c_rows", "c_sel", "c_x", "c_attw1", "c_attw2", "c_selfw", "c_mask", "c_brow",
                             "c_relw", "c_relr"))
        out_done = sem("out_done")
        S, shared, count = {}, {}, {}
        for st in stages:
            stage_out = sem(f"{st}_out")
            if st[:3] == "res":
                S[st] = Signals({}, {}, stage_out)
                continue
            fam = family(st)
            if fam not in shared:
                shared[fam] = {n: sem(f"{fam}_{n}") for n in signals_of(st)}
                count[fam] = {n: AHEAD if n in AHEAD_OF else 0 for n in signals_of(st)}
            S[st] = Signals(shared[fam], count[fam], stage_out)
            mine = {n: 0 if st == "att1" and n in ("sq", "ssq", "k_sb", "q2", "ss", "ss_rows", "rq") else k
                    for n, k in signals_of(st).items()}
            count[fam] = {n: count[fam][n] + k for n, k in mine.items()}
        dve_chain, act_chain, pool_chain = sem("dve_chain"), sem("act_chain"), sem("pool_chain")
        rel_s = {n: sem(f"rel_{n}") for n in ("h0", "t0", "t0s", "m1", "h1", "t1", "t1s", "m2", "sb", "sq", "si")}
        use_rel = "att2" in stages

        prev = {}
        before = None
        for st in stages:
            prev[st] = before
            before = st
        OUTS = {}
        for st in stages:
            if st[:4] == "cond":
                OUTS[st] = 2
            elif st[:3] == "ffn":
                OUTS[st] = 0
            elif st[:3] == "att":
                OUTS[st] = 2
            elif st == "self2":
                OUTS[st] = 4
            elif st[:3] == "res":
                OUTS[st] = 2
            else:
                OUTS[st] = 2

        def ready(eng, st):
            if prev[st] is None:
                eng.wait_ge(c_x, 16)
            else:
                eng.wait_ge(S[prev[st]]["out"], OUTS[prev[st]])

        SRC, DST = {}, {}
        at = resid
        for st in stages:
            SRC[st] = at
            if st[:3] == "res":
                DST[st] = resid
            elif st == "self2":
                DST[st] = keep
            elif st == "post2":
                DST[st] = keep
            elif st[:3] == "ffn":
                DST[st] = nxt
            else:
                DST[st] = cur if at is not cur else nxt
            at = DST[st]
        LAST = stages[-1]

        block = ctx.enter_context(nc.Block())

        def weight_users():
            return [st for st in stages if st[:4] == "cond" or st[:3] == "ffn"]

        def free_staging(eng, st, slot):
            users = weight_users()
            k = users.index(st)
            if k:
                u = users[k - 1]
                if u[:3] == "ffn":
                    eng.wait_ge(*S[u].at(f"w_split{slot}", EXPERTS))
                else:
                    eng.wait_ge(*S[u].at("w_split0", 2))

        @block.sync
        def _(sp):
            def load_conditioner(st):
                for slot in range(2):
                    free_staging(sp, st, slot)
                sp.dma_start(w_stage[:, 0:COND_COLS], dram[f"{st}_w"]).then_inc(S[st]["w_dma0"], 16)

            sp.dma_start(small[:, :], dram["small"]).then_inc(c_small, 16)
            sp.dma_start(rows[:, :], dram["rows"].broadcast_to([P, N_ROWS])).then_inc(c_rows, 16)
            sp.dma_start(resid[:, :], dram["xT"]).then_inc(c_x, 16)
            if stages[0][:4] == "cond":
                load_conditioner(stages[0])
            sp.dma_start(sel16[:, :], dram["sel16"]).then_inc(c_sel, 16)
            sp.dma_start(ident16[:, :], dram["ident16"]).then_inc(c_sel, 16)
            sp.dma_start(brow[:, :, :, :].rearrange("p l g k -> p (l g k)"), dram["brow"]).then_inc(c_brow, 16)
            sp.dma_start(mask_u8[:, :], dram["mask"].broadcast_to([P, 2 * TOK])).then_inc(c_mask, 16)
            sp.dma_start(self_w[:, :], dram["self_w"]).then_inc(c_selfw, 16)
            first_att = next((st for st in stages if st[:3] == "att"), None)
            if first_att:
                sp.dma_start(att_w[:, :], dram[f"{first_att}_w"])\
                    .then_inc(c_attw1 if first_att == "att1" else c_attw2, 16)
            if use_rel:
                sp.wait_ge(rel_s["sb"], 2)
                sp.dma_start(relb_dram.ap(), relT[:, :]).then_inc(c_relw, 16)
                sp.wait_ge(c_relw, 16)
                sp.wait_ge(c_brow, 16)
                table = relb_dram.ap().rearrange("(h g) (i k) -> h i g k", h=4, i=SEQ)
                for h in range(4):
                    sp.dma_start(brow[32 * h:32 * h + 32, 1, :, 0:SEQ], table[h]).then_inc(c_relr, 16)
            for st in weight_users():
                s = S[st]
                if st[:4] == "cond":
                    if st != stages[0]:
                        load_conditioner(st)
                    continue
                cols = expert_cols(FFN_KINDS[int(st[3])])[1]
                src = dram[f"{st}_w"]
                for slot in range(2):
                    free_staging(sp, st, slot)
                    sp.dma_start(w_stage[:, slot * STAGE_COLS:slot * STAGE_COLS + cols],
                                 src[slot]).then_inc(s[f"w_dma{slot}"], 16)
                with sp.Fori(1, EXPERTS // 2) as i:
                    for slot in range(2):
                        sp.wait_ge(*s.at(f"w_split{slot}", 2 * i))
                        sp.dma_start(w_stage[:, slot * STAGE_COLS:slot * STAGE_COLS + cols],
                                     src[bass.ds(2 * i + slot, 1)].rearrange("a p c -> (a p) c"))\
                            .then_inc(s[f"w_dma{slot}"], 16)
            for half in range(2):
                sp.wait_ge(S[LAST]["out"], half + 1)
                sp.dma_start(out[:, half * HALF:(half + 1) * HALF], DST[LAST][:, half * HALF:(half + 1) * HALF])\
                    .then_inc(out_done, 16)
            sp.wait_ge(out_done, 32)

        @block.gpsimd
        def _(pool):
            chain = Chain(pool, pool_chain)
            if "moe" in shared:
                for n in AHEAD_OF:
                    pool.sem_inc(shared["moe"][n], AHEAD)

            def attention_masks(layer):
                s = S[f"att{layer}"]
                pool.wait_ge(*s.at("wq_hi", 1))
                pool.tensor_tensor(w_lo[:, 0:TOK], att_w[:, 0:TOK], w_hi[:, 0:TOK], ALU.subtract)\
                    .then_inc(s["wq_split"], 1)
                if layer == 2 and "att1" in stages:
                    pool.memset(kbd[:, :], 0.0).then_inc(s["zeroed"], 1)
                else:
                    chain.step(pool.memset(vbd[:, :], 0.0))
                    pool.memset(kbd[:, :], 0.0).then_inc(s["zeroed"], 1)
                if layer == 1:
                    pool.wait_ge(c_mask, 16)
                    pool.wait_ge(c_brow, 16)
                    pool.wait_ge(c_small, 16)
                if layer == 2:
                    pool.wait_ge(c_relr, 64)
                    if "att1" in stages:
                        pool.wait_ge(*S["att1"].at("biased", 2 * TILES))
                    else:
                        pool.wait_ge(c_mask, 16)
                        pool.wait_ge(c_brow, 16)
                        pool.wait_ge(c_small, 16)
                keys = mask_f[:, :].rearrange("p (b k) -> p b k", k=KEYS)
                chain.step(pool.memset(mask_f[:, :], 0.0))
                src = mask_u8[:, (layer - 1) * TOK:layer * TOK].rearrange("p (b k) -> p b k", k=SEQ)
                chain.step(pool.tensor_scalar(keys[:, :, 0:SEQ], src, -1.0, -MASKED, ALU.add, ALU.mult))
                chain.step(pool.tensor_tensor(brow[:, layer - 1, :, :], brow[:, layer - 1, :, :],
                                              sm("causal").rearrange("p (g k) -> p g k", k=KEYS), ALU.add))
                for t in range(TILES):
                    for g2 in range(2):
                        b = brow[:, layer - 1, 2 * g2:2 * g2 + 2, :].unsqueeze(1).broadcast_to([P, 4, 2, KEYS])
                        m = keys[:, 4 * t:4 * t + 4, :].unsqueeze(2).broadcast_to([P, 4, 2, KEYS])
                        o = bm[:, (2 * t + g2) * 8 * KEYS:(2 * t + g2 + 1) * 8 * KEYS]
                        pool.tensor_tensor(o.rearrange("p (b q k) -> p b q k", b=4, q=2), b, m, ALU.add)\
                            .then_inc(s["bm"], 1)

            def attention(st):
                s = S[st]
                for t in range(-1, TILES):
                    if t + 1 < TILES:
                        pool.wait_ge(*s.at("rowmax", t + 2))
                        s3 = s_sb[:, (t + 1) % 3, :].rearrange("p (a k) -> p a k", k=KEYS)
                        pool.tensor_tensor(s3, s3, red[:, 0, (t + 1) % 2, :].unsqueeze(2).broadcast_to([P, 16, KEYS]),
                                           ALU.subtract).then_inc(s["sub"], 1)
                    if t < 0:
                        continue
                    pool.wait_ge(*s.at("rsum", t + 1))
                    if t >= 2:
                        pool.wait_ge(*s.at("pt", t - 1))
                    for g2 in range(2):
                        o = p_sb[:, t % 2, g2 * 256:(g2 + 1) * 256].rearrange("p (q b k) -> p b q k", q=2, b=4)
                        e = s_sb[:, t % 3, g2 * 8 * KEYS:(g2 + 1) * 8 * KEYS]\
                            .rearrange("p (b q k) -> p b q k", b=4, q=2)
                        w = red[:, 1, t % 2, 8 * g2:8 * g2 + 8].rearrange("p (b q) -> p b q", b=4).unsqueeze(3)\
                            .broadcast_to([P, 4, 2, SEQ])
                        pool.tensor_tensor(o, e[:, :, :, 0:SEQ], w, ALU.mult).then_inc(s["p"], 1)

            def self_attention(st):
                s = S[st]
                for t in range(TILES):
                    pool.wait_ge(*s.at("rsum", t + 1))
                    if t >= 2:
                        pool.wait_ge(*s.at("pt", t - 1))
                    o = p_sb[:, t % 2, :].rearrange("p (g b k) -> p b g k", g=4, b=4)
                    e = s_sb[:, t % 3, 0:512].rearrange("p (b g k) -> p b g k", b=4, g=4)
                    w = red[:, 1, t % 2, :].rearrange("p (b g) -> p b g", b=4).unsqueeze(3)\
                        .broadcast_to([P, 4, 4, SEQ])
                    pool.tensor_tensor(o, e, w, ALU.mult).then_inc(s["p"], 1)

            def ffn(st):
                s = S[st]
                kind = FFN_KINDS[int(st[3])]
                per = 4 * kind["chunks"]
                acc = DST[st]

                def low_half(slot, part, i):
                    pool.wait_ge(*s.at(f"w_hi{slot}", 2 * i + (1 if part == "up" else 2)))
                    lo, hi = part_cols(kind, part)
                    base, at = slot * STAGE_COLS, slot * 1024
                    pool.tensor_tensor(w_lo[:, at + lo:at + hi], w_stage[:, base + lo:base + hi],
                                       w_hi[:, at + lo:at + hi], ALU.subtract).then_inc(s[f"w_split{slot}"], 1)

                def accumulate(y, pair):
                    half = y % 2
                    pool.wait_ge(*s.at("wtd", 4 * pair + y + 1))
                    a = acc[:, half * HALF:(half + 1) * HALF]
                    pool.tensor_tensor(a, a, wtd[:, half, :], ALU.add).then_inc(s["acc"], 1)
                    pool.wait_ge(*s.at("acc", 4 * pair + y + 1))

                def pair(i, first=False, last=False):
                    for k in range(per):
                        for slot, part, nxt in splits_at(kind, k, first, last):
                            low_half(slot, part, i + nxt)
                        if weighed_at(kind, k) is not None:
                            accumulate(weighed_at(kind, k), i)
                        if not first and weighed_at(kind, per + k) is not None:
                            accumulate(weighed_at(kind, per + k), i - 1)

                low_half(0, "up", 0)
                low_half(0, "down", 0)
                ready(pool, st)
                chain.step(pool.memset(acc[:, :], 0.0))
                pair(0, first=True)
                with pool.Fori(1, EXPERTS // 2 - 1) as i:
                    pair(i)
                pair(EXPERTS // 2 - 1, last=True)
                for k in range(per, per + WEIGH - 1):
                    if weighed_at(kind, k) is not None:
                        accumulate(weighed_at(kind, k), EXPERTS // 2 - 1)

            def cond(st):
                s = S[st]
                for k, (lo, hi) in enumerate(COND_PARTS):
                    pool.wait_ge(*s.at("w_hi0", k + 1))
                    pool.tensor_tensor(w_lo[:, lo:hi], w_stage[:, lo:hi], w_hi[:, lo:hi], ALU.subtract)\
                        .then_inc(s["w_split0"], 1)
                wide = big[:, 0:4 * TOK].rearrange("p (e t) -> p e t", e=4)
                for k in range(2, 2 * COND_CHUNKS):
                    chunk, half = k // 2, k % 2
                    pool.wait_ge(*s.at("prod", k + 1))
                    pool.wait_ge(*s.at("spread_sb", 2 * (chunk - 1) + half + 1))
                    h = h32[:, k % RING, :]
                    pool.tensor_tensor(h, h, wide[:, chunk - 1, half * HALF:(half + 1) * HALF], ALU.mult)\
                        .then_inc(s["weighed"], 1)

            for st in stages:
                if st[:3] == "att":
                    attention_masks(int(st[3]))
                    attention(st)
                if st == "self2":
                    s = S[st]
                    if "att2" in stages:
                        pool.wait_ge(*S["att2"].at("wo", 2))
                    chain.step(pool.memset(q2[:, :], 0.0))
                    pool.memset(vself, 0.0).then_inc(s["zeroed"], 1)
                    self_attention(st)
                if st[:3] == "ffn":
                    ffn(st)
                if st[:4] == "cond":
                    cond(st)

        @block.tensor
        def _(pe):
            mm = pe.matmul

            def mm3(out, w, x, start, stop):
                mm(out, w[0], x[0], start=start, stop=False)
                mm(out, w[0], x[1], start=False, stop=False)
                return mm(out, w[1], x[0], start=False, stop=stop)

            def bridge(bank, n):
                for _ in range(n):
                    mm(psum[:, bank, :], ident16[:, :], in_hi[:, 0:HALF], start=True, stop=True)

            def router(st):
                s = S[st]
                src = SRC[st]
                lg = psum[:, 7, 0:64]
                for t in range(TILES):
                    o = lg[:, 8 * t:8 * t + 8]
                    extra = st[:4] == "cond" or st == "ffn0"
                    last = mm(o, src[:, t * P:(t + 1) * P], sm(f"{st}_router"), start=True, stop=not extra)
                    if st[:4] == "cond":
                        if t == 0:
                            pe.wait_ge(*s.at("rep", 1))
                        last = mm(o, nxt[0:64, t * P:(t + 1) * P], sm(f"{st}_wg", p=64), start=False, stop=True)
                    if st == "ffn0":
                        last = mm(o, sm("ones_row", p=1), sm("ffn0_brow", p=1), start=False, stop=True)
                last.then_inc(s["logits"], 1)

            def transpose_weights(st):
                s = S[st]
                pe.wait_ge(c_sel, 32)
                pe.wait_ge(*s.at("w16", 1))
                wT = psum[0:16, 7, :].bitcast(F16)
                for t in range(TILES):
                    last = pe.transpose(wT[:, t * P:(t + 1) * P], w16[:, t, :], ident16[:, :])
                last.then_inc(s["wT"], 1)

            def spread(st, first, n):
                s = S[st]
                off = EXPERTS if st[:4] == "cond" else 0
                if first == 0:
                    pe.wait_ge(*s.at("wTsb", 1))
                for k in range(first, first + n):
                    e, half = k // 2, k % 2
                    if k >= 2:
                        pe.wait_ge(*s.at("spread_sb", k - 1))
                    mm(psum[:, 6 + k % 2, :], sel16[:, (off + e) * P:(off + e + 1) * P],
                       wT16[:, half * HALF:(half + 1) * HALF], start=True, stop=True).then_inc(s["spread"], 1)

            def ffn(st):
                s = S[st]
                kind = FFN_KINDS[int(st[3])]
                C, gated = kind["chunks"], kind["gated"]
                n_up = 2 if gated else 1
                per = 4 * C
                at = interleave(st)

                def up(i, k, between=lambda: None):
                    slot, half, c = k // (2 * C), (k // C) % 2, k % C
                    if k % (2 * C) == 0:
                        pe.wait_ge(*s.at(f"w_split{slot}", 2 * i + 1))
                    x = (in_hi[:, half * HALF:(half + 1) * HALF], in_lo[:, half * HALF:(half + 1) * HALF])
                    if gated:
                        pe.wait_ge(*s.at("prod", per * i + k - 1))
                        banks = [2 * (k % 2), 2 * (k % 2) + 1]
                    else:
                        pe.wait_ge(*s.at("act", per * i + k - 3))
                        banks = [k % 4]
                    for u, bank in enumerate(banks):
                        w0 = slot * 1024 + (u * C + c) * P
                        mm3(psum[:, bank, :], (w_hi[:, w0:w0 + P], w_lo[:, w0:w0 + P]), x, True, True)\
                            .then_inc(s["gate" if gated and u == 0 else "up"], 1)
                        if u < len(banks) - 1:
                            between()

                def down(i, j):
                    slot, half, c = j // (2 * C), (j // C) % 2, j % C
                    if j % (2 * C) == 0:
                        pe.wait_ge(*s.at(f"w_split{slot}", 2 * i + 2))
                    pe.wait_ge(*s.at("hid", per * i + j + 1))
                    if c == 0:
                        pe.wait_ge(*s.at("wtd", 4 * i + j // C - 1))
                    w0 = slot * 1024 + (n_up * C + c) * P
                    mm3(psum[:, 4 + half, :], (w_hi[:, w0:w0 + P], w_lo[:, w0:w0 + P]),
                        (h_hi[:, j % RING, :], h_lo[:, j % RING, :]), c == 0, c == C - 1).then_inc(s["down"], 1)

                router(st)
                pe.wait_ge(*s.at("split", 1))
                for k in range(per):
                    first = at["pieces"] * (k - at["spread"])
                    pieces = iter(range(max(first, 0), min(max(first + at["pieces"], 0), 2 * EXPERTS)))

                    def piece():
                        for n in pieces:
                            spread(st, n, 1)
                            break

                    up(0, k, piece)
                    if k == at["transpose"]:
                        transpose_weights(st)
                    piece()
                    if k >= LAG:
                        down(0, k - LAG)
                    piece()
                with pe.Fori(1, EXPERTS // 2) as i:
                    for k in range(per):
                        up(i, k)
                        if k >= LAG:
                            down(i, k - LAG)
                        else:
                            down(i - 1, per + k - LAG)
                for j in range(per - LAG, per):
                    down(EXPERTS // 2 - 1, j)

            def cond(st, with_table):
                s = S[st]
                router(st)
                if with_table:
                    relative_turn()
                pe.wait_ge(*s.at("split", 1))
                pe.wait_ge(*s.at("w_split0", 1))
                pieces = []
                for k in range(2 * COND_CHUNKS + COND_LAG):
                    if k == 4:
                        pe.wait_ge(*s.at("w_split0", 2))
                    if k < 2 * COND_CHUNKS:
                        chunk, half = k // 2, k % 2
                        if k >= 2:
                            pe.wait_ge(*s.at("prod", k - 1))
                        x = (in_hi[:, half * HALF:(half + 1) * HALF], in_lo[:, half * HALF:(half + 1) * HALF])
                        pieces = list(range(*COND_SPREAD[k])) if k in COND_SPREAD else []
                        for u in range(2):
                            w0 = (3 * chunk + u) * P
                            mm3(psum[:, 2 * (k % 2) + u, :], (w_hi[:, w0:w0 + P], w_lo[:, w0:w0 + P]), x,
                                True, True).then_inc(s[("gate", "up")[u]], 1)
                            if pieces:
                                spread(st, pieces.pop(0), 1)
                    if with_table and k == TABLE_STEP:
                        relative_table()
                    if k == 2:
                        transpose_weights(st)
                    if with_table and k == COND_LAG:
                        pe.wait_ge(rel_s["sb"], 2)
                    if k >= COND_LAG:
                        j = k - COND_LAG
                        chunk, half = j // 2, j % 2
                        pe.wait_ge(*s.at("hid", j + 1))
                        w0 = (3 * chunk + 2) * P
                        mm3(psum[:, 4 + half, :], (w_hi[:, w0:w0 + P], w_lo[:, w0:w0 + P]),
                            (h_hi[:, j % RING, :], h_lo[:, j % RING, :]), chunk == 0, chunk == COND_CHUNKS - 1)\
                            .then_inc(s["down"], 1)
                    for n in pieces:
                        spread(st, n, 1)
                    pieces = []

            def layer_norm(st):
                s = S[st]
                src = SRC[st]
                before = prev[st]
                by_half = before is not None and (before[:3] == "res" or before[:3] == "att")
                if not by_half:
                    ready(pe, st)
                for t in range(TILES):
                    if by_half and t % 4 == 0:
                        pe.wait_ge(S[before]["out"], t // 4 + 1)
                    last = pe.transpose(psum[:, t // 4, (t % 4) * P:(t % 4 + 1) * P], src[:, t * P:(t + 1) * P], ident)
                    if t % 4 == 3:
                        last.then_inc(s["tr"], 1)
                bridge(4, 10)
                for t in (0, 4, 1, 5, 2, 6, 3, 7):
                    pe.wait_ge(*s.at("norm" if t < 4 else "norm_act", t % 4 + 1))
                    last = pe.transpose(psum[:, 2 + t // 4, (t % 4) * P:(t % 4 + 1) * P], tok[:, t, :], ident)
                    if t % 4 == 3:
                        last.then_inc(s["back"], 1)

            def attention(st):
                s = S[st]
                layer = int(st[3])
                src = SRC[st]
                pe.wait_ge(c_attw1 if layer == 1 else c_attw2, 16)
                Wk, Wv = att_w[:, TOK:TOK + P], att_w[:, TOK + P:TOK + P + 64]
                Wo = att_w[:, TOK + P + 64:].rearrange("p (c n) -> p c n", c=8)
                for half in range(2):
                    mm(psum[:, half, :], Wk, src[:, half * HALF:(half + 1) * HALF], start=True, stop=True)\
                        .then_inc(s["k"], 1)
                for t in range(TILES):
                    last = mm(psum[:, 2, t * 64:(t + 1) * 64], src[:, t * P:(t + 1) * P], Wv, start=True, stop=True)
                last.then_inc(s["v"], 1)
                def key_norms():
                    pe.wait_ge(*s.at("sq", 1))
                    for k in range(3):
                        last = mm(psum[:, (0, 1, 7)[k], 0:352], sm("ones_block"), k_square[:, k * 352:(k + 1) * 352],
                                  start=True, stop=True)
                    last.then_inc(s["ssq"], 1)

                def query_norm(k):
                    half, g2, h4 = Q_ORDER[k]
                    pe.wait_ge(*s.at("q2", k + 1))
                    if k == 8:
                        pe.wait_ge(*s.at("k_sb", 1))
                    window = sm("headsel", HEADSEL - (SEQ * h4 + 2 * g2), P)
                    mm(psum[:, (4, 7)[half], :], window, q2[:, (k % 4) * HALF:(k % 4 + 1) * HALF],
                       start=k % 8 == 0, stop=k % 8 == 7).then_inc(s["ss"], 1)

                for k, (half, g2, h4) in enumerate(Q_ORDER):
                    c = 4 * g2 + h4
                    if k >= 3:
                        pe.wait_ge(*s.at("q_sb", k - 2))
                    if k == 0:
                        pe.wait_ge(*s.at("split", 1))
                        pe.wait_ge(*s.at("wq_split", 1))
                    hs = slice(half * HALF, (half + 1) * HALF)
                    mm3(psum[:, Q_BANKS[k % 3], :], (w_hi[:, c * P:(c + 1) * P], w_lo[:, c * P:(c + 1) * P]),
                        (in_hi[:, hs], in_lo[:, hs]), True, True).then_inc(s["q"], 1)
                    if layer == 2 and k == 4:
                        key_norms()
                    if layer == 2 and k >= 2:
                        query_norm(k - 2)
                if layer == 2:
                    query_norm(14)
                    query_norm(15)
                pe.wait_ge(*s.at("q_sb", 16))
                pe.wait_ge(*s.at("kk", 1))
                pe.wait_ge(*s.at("v_sb", 1))

                def scores(t):
                    for g2 in range(2):
                        bank = (2 * t + g2) % 3
                        if 2 * t + g2 >= 3:
                            pe.wait_ge(*s.at("biased", 2 * t + g2 - 2))
                        for b in range(4):
                            n = 4 * t + b
                            last = mm(psum[:, bank, b * 66:(b + 1) * 66],
                                      big[:, (g2 * BATCH + n) * P:(g2 * BATCH + n + 1) * P],
                                      kbd[:, n * 66:(n + 1) * 66], start=True, stop=True)
                    last.then_inc(s["sc"], 1)

                def transposes(t):
                    pe.wait_ge(*s.at("p", 2 * t + 2))
                    if t >= 1:
                        pe.wait_ge(*s.at("pt_sb", t))
                    for g in range(4):
                        last = pe.transpose(psum[:, 7, g * P:(g + 1) * P], p_sb[:, t % 2, g * P:(g + 1) * P],
                                            ident)
                    last.then_inc(s["pt"], 1)

                def contexts(t):
                    pe.wait_ge(*s.at("pt_sb", t + 1))
                    if t >= 2:
                        pe.wait_ge(*s.at("o", 4 * t - 4))
                    for bp in range(2):
                        v0 = t * 256 + bp * P
                        mm(psum[:, 3 + 2 * (t % 2) + bp, :], vbd[:, v0:v0 + P], pT[:, t % 2, :], start=True, stop=True)\
                            .then_inc(s["pv"], 1)

                o = oT[:, :].rearrange("p (n c i) -> p c n i", c=8, i=SEQ)

                def project(half, pairs):
                    for c in pairs:
                        last = mm(psum[:, half, :], Wo[:, c, :], o[:, c, 16 * half:16 * half + 16, :],
                                  start=c == 0, stop=c == 7)
                    if c == 7:
                        last.then_inc(s["wo"], 1)

                scores(0)
                scores(1)
                scores(2)
                bridge(6, 8)
                for t in range(TILES + 1):
                    if 0 < t < TILES - 2:
                        scores(t + 2)
                    if t >= 1:
                        contexts(t - 1)
                    if t < TILES:
                        transposes(t)
                    if t == 6:
                        pe.wait_ge(*s.at("biased", 2 * TILES))
                    if t >= 6:
                        project(0, ((0, 1, 2), (3, 4, 5), (6, 7))[t - 6])
                pe.wait_ge(*s.at("o", 4 * TILES))
                project(1, range(8))

            def self_attention(st):
                s = S[st]
                src = SRC[st]
                pe.wait_ge(c_selfw, 16)
                for half in range(2):
                    for k in range(2):
                        mm(psum[:, 2 * k + half, :], self_w[:, k * P:(k + 1) * P],
                           src[:, half * HALF:(half + 1) * HALF], start=True, stop=True).then_inc(s["qkv"], 1)
                for t in range(TILES):
                    last = mm(psum[:, 4 + t // 4, (t % 4) * P:(t % 4 + 1) * P], src[:, t * P:(t + 1) * P],
                              self_w[:, 2 * P:3 * P], start=True, stop=True)
                last.then_inc(s["qkv"], 1)
                pe.wait_ge(*s.at("q_sb", 1))
                pe.wait_ge(*s.at("k_sb", 1))
                km = q2[:, :].rearrange("p (g t) -> p g t", g=4)

                def scores(t):
                    if t >= 2:
                        pe.wait_ge(*s.at("sub", t - 1))
                    for b in range(4):
                        n = 4 * t + b
                        last = mm(psum[:, t % 2, b * P:(b + 1) * P], big[:, n * P:(n + 1) * P],
                                  km[:, :, n * SEQ:(n + 1) * SEQ], start=True, stop=True)
                    last.then_inc(s["sc"], 1)

                def transposes(t):
                    pe.wait_ge(*s.at("p", t + 1))
                    if t >= 2:
                        pe.wait_ge(*s.at("pt_sb", t - 1))
                    for g in range(4):
                        last = pe.transpose(psum[:, 2 + t % 2, g * P:(g + 1) * P], p_sb[:, t % 2, g * P:(g + 1) * P],
                                            ident)
                    last.then_inc(s["pt"], 1)

                def contexts(t):
                    pe.wait_ge(*s.at("pt_sb", t + 1))
                    if t == 0:
                        pe.wait_ge(*s.at("v_sb", 2))
                    if t >= 2:
                        pe.wait_ge(*s.at("c", t - 1))
                    for g in range(4):
                        v0 = (t * 4 + g) * P
                        last = mm(psum[:, 4 + t % 2, g * P:(g + 1) * P], pT[:, t % 2, g * P:(g + 1) * P],
                                  vself[:, v0:v0 + P], start=True, stop=True)
                    last.then_inc(s["pv"], 1)

                def context_transpose(t):
                    pe.wait_ge(*s.at("c", t + 1))
                    if t >= 2:
                        pe.wait_ge(*s.at("ct_sb", t - 1))
                    pe.transpose(psum[:, 6 + t % 2, 0:P], tok[:, t, :], ident).then_inc(s["ct"], 1)

                scores(0)
                scores(1)
                scores(2)
                bridge(7, 6)
                for t in range(TILES + 3):
                    if 0 < t < TILES - 2:
                        scores(t + 2)
                    if t < TILES:
                        transposes(t)
                    if 1 <= t <= TILES:
                        contexts(t - 1)
                    if t >= 3:
                        context_transpose(t - 3)
                bridge(0, 4)
                pe.wait_ge(*s.at("ct_sb", TILES))
                ctxT = oT[:, 0:TOK].rearrange("p (t h i) -> p h t i", h=4, i=SEQ)
                for b in range(4):
                    r = slice(32 * b, 32 * b + 32)
                    for h in range(4):
                        last = mm(psum[:, b, 0:256], self_w[r, (3 + h) * P:(4 + h) * P], ctxT[r, h, :, :],
                                  start=h == 0, stop=h == 3)
                    last.then_inc(s["wo"], 1)

            def relative_hidden():
                pe.wait_ge(rel_s["h0"], 1)
                pe.transpose(psum[:, 0, 0:63], rel[0:63, 0, :], sm("ident", 0, 63, 63)).then_inc(rel_s["t0"], 1)
                pe.wait_ge(rel_s["t0s"], 1)
                mm(psum[0:63, 1, 0:P], rel[:, 1, 0:63], sm("relw1"), start=True, stop=True).then_inc(rel_s["m1"], 1)

            def relative_turn():
                pe.wait_ge(rel_s["h1"], 1)
                pe.transpose(psum[:, 6, 0:63], rel[0:63, 2, :], sm("ident", 0, 63, 63)).then_inc(rel_s["t1"], 1)

            def relative_table():
                pe.wait_ge(rel_s["t1s"], 1)
                for part in range(2):
                    for i in range(16):
                        q = 16 * part + i
                        last = mm(psum[0:16, 4 + part, i * SEQ:(i + 1) * SEQ], sm("relw2"),
                                  rel[:, 3, 31 - q:63 - q], start=True, stop=True)
                last.then_inc(rel_s["m2"], 1)

            k_square = oT[:, 2 * TOK:2 * TOK + BATCH * KEYS]
            pe.wait_ge(c_small, 16)
            if use_rel:
                relative_hidden()
            for st in stages:
                if st[:3] == "res":
                    continue
                if family(st) != "norm":
                    ready(pe, st)
                if use_rel and st == stages[0] and st[:4] != "cond":
                    relative_turn()
                    relative_table()
                    pe.wait_ge(rel_s["sb"], 2)
                if st[:4] == "cond":
                    cond(st, use_rel and st == stages[0])
                elif st[:3] == "ffn":
                    ffn(st)
                elif st[:3] == "att":
                    attention(st)
                elif st == "self2":
                    self_attention(st)
                else:
                    layer_norm(st)

        @block.vector
        def _(dve):
            chain = Chain(dve, dve_chain)
            stt, tt, ts = dve.scalar_tensor_tensor, dve.tensor_tensor, dve.tensor_scalar

            def r8(k):
                return rt[:, k, :].rearrange("p (t e) -> p t e", e=8)

            def router_top(st):
                s = S[st]
                dve.wait_ge(*s.at("logits", 1))
                chain.step(ts(rt[:, 0, :], psum[:, 7, 0:64], ROUTERS[st]["scale"], None, ALU.mult))
                for t in range(TILES):
                    chain.done(dve.max(r8(1)[:, t, :], r8(0)[:, t, :]))
                chain.wait()
                tt(r8(2), r8(0), r8(1)[:, :, 0:1].broadcast_to([P, 8, 8]), ALU.subtract).then_inc(s["lg_sb"], 1)

            def router_mask(st):
                lg, top, m0, m1, fi = r8(0), r8(1), r8(3), r8(4), r8(6)
                for t in range(TILES):
                    chain.done(dve.max_index(rt_idx[:, 8 * t:8 * t + 8], top[:, t, :], lg[:, t, :]))
                chain.wait()
                chain.step(dve.tensor_copy(rt[:, 6, :], rt_idx[:, :]))
                iota = sm("iota").unsqueeze(1).broadcast_to([P, 8, 8])
                chain.done(tt(m0, iota, fi[:, :, 0:1].broadcast_to([P, 8, 8]), ALU.is_equal))
                if ROUTERS[st]["keep"] == 2:
                    chain.step(tt(m1, iota, fi[:, :, 1:2].broadcast_to([P, 8, 8]), ALU.is_equal))
                    chain.step(tt(m0, m0, m1, ALU.add))
                chain.wait()

            def router_weights(st):
                s, r = S[st], ROUTERS[st]
                ex, m0, em = r8(7), r8(3), r8(5)
                dve.wait_ge(*s.at("ex", 1))
                chain.done(dve.reduce_sum(rt[:, 8, 0:8], ex, AX_X))
                chain.step(tt(em, ex, m0, ALU.mult))
                if r["norm"]:
                    chain.step(dve.reduce_sum(rt[:, 8, 8:16], em, AX_X))
                    chain.step(stt(rt[:, 8, 16:24], rt[:, 8, 0:8], r["eps"], rt[:, 8, 8:16], ALU.mult, ALU.add))
                    chain.step(dve.reciprocal(rt[:, 8, 24:32], rt[:, 8, 16:24]))
                else:
                    chain.step(dve.reciprocal(rt[:, 8, 24:32], rt[:, 8, 0:8]))
                chain.step(tt(r8(9), em, rt[:, 8, 24:32].unsqueeze(2).broadcast_to([P, 8, 8]), ALU.mult))
                chain.step(dve.tensor_copy(w16[:, :, 0:8], r8(9)))
                tt(w16[:, :, 8:16], r8(9), w16[:, :, 0:8], ALU.subtract).then_inc(s["w16"], 1)

            def router_copy(st):
                s = S[st]
                dve.wait_ge(*s.at("wT", 1))
                dve.tensor_copy(wT16[:, :], psum[0:16, 7, :].bitcast(F16)).then_inc(s["wTsb"], 1)

            def split_input(st):
                s = S[st]
                chain.step(dve.tensor_copy(in_hi[:, :], SRC[st][:, :]))
                tt(in_lo[:, :], SRC[st][:, :], in_hi[:, :], ALU.subtract).then_inc(s["split"], 1)

            def ffn(st):
                s = S[st]
                kind = FFN_KINDS[int(st[3])]
                C, gated = kind["chunks"], kind["gated"]
                per = 4 * C
                at = interleave(st)
                wide = big[:, :].rearrange("p (e t) -> p e t", e=8)
                links = 0 if gated else per

                def hidden(i, k):
                    r = k % RING
                    dve.wait_ge(*s.at("act", per * i + k + 1))
                    dve.wait_ge(*s.at("down", per * i + k - RING + 1))
                    chain.step(dve.tensor_copy(h_hi[:, r, :], h32[:, r, :]))
                    tt(h_lo[:, r, :], h32[:, r, :], h_hi[:, r, :], ALU.subtract).then_inc(s["hid"], 1)

                def product(i, k):
                    slot, c, r = k // (2 * C), k % C, k % RING
                    dve.wait_ge(*s.at("act", per * i + k + 1))
                    dve.wait_ge(*s.at("up", per * i + k + 1))
                    dve.wait_ge(*s.at("hid", per * i + k - RING + 1))
                    ub = w_bias[:, slot * 12 + 1 + c:slot * 12 + 2 + c]
                    stt(h32[:, r, :], psum[:, 2 * (k % 2) + 1, :], ub, gate32[:, k % 2, :],
                        ALU.add, ALU.mult).then_inc(s["prod"], 1)

                def low_of_product(i, k):
                    r = k % RING
                    dve.wait_ge(*s.at("high", per * i + k + 1))
                    stt(h_lo[:, r, :], h32[:, r, :], 1.0 / WSCALE, h_hi[:, r, :], ALU.mult,
                        ALU.subtract).then_inc(s["hid"], 1)

                def weigh(i, y):
                    slot, half = y // 2, y % 2
                    dve.wait_ge(*s.at("down", per * i + C * (y + 1)))
                    dve.wait_ge(*s.at("acc", 4 * i + y - 1))
                    w = wide[:, bass.ds(2 * i + slot, 1), half * HALF:(half + 1) * HALF].rearrange("p a t -> p (a t)")
                    stt(wtd[:, half, :], psum[:, 4 + half, :], w_bias[:, slot * 12:slot * 12 + 1], w,
                        ALU.add, ALU.mult).then_inc(s["wtd"], 1)

                def step(i, k, first=False):
                    if gated:
                        product(i, k)
                        if not first or k:
                            low_of_product(i, k - 1)
                    else:
                        hidden(i, k)
                    if first and k == at["copy"]:
                        router_copy(st)
                    y = weighed_at(kind, k)
                    if y is not None:
                        if first:
                            dve.wait_ge(*s.at("spread_sb", y + 1))
                        weigh(i, y)
                    y = weighed_at(kind, per + k)
                    if y is not None and not first:
                        weigh(i - 1, y)

                split_input(st)
                router_top(st)
                router_mask(st)
                router_weights(st)
                for k in range(per):
                    step(0, k, first=True)
                dve.wait_ge(*s.at("spread_sb", 2 * EXPERTS))
                base = chain.n
                with dve.Fori(1, EXPERTS // 2) as i:
                    chain.n = base + (i - 1) * links
                    for k in range(per):
                        step(i, k)
                chain.n = base + links * (EXPERTS // 2 - 1)
                if gated:
                    low_of_product(EXPERTS // 2 - 1, per - 1)
                last_pair = EXPERTS // 2 - 1
                acc, res = DST[st], S[f"res{st[3]}"]
                lo, hi = slice(0, HALF), slice(HALF, TOK)
                if st == "ffn2":
                    chain.step(tt(resid[:, :], resid[:, :], keep[:, :], ALU.add))
                dve.wait_ge(*s.at("acc", 4 * last_pair + 2))
                chain.done(tt(resid[:, hi], resid[:, hi], acc[:, hi], ALU.add))
                for k in range(per, per + WEIGH):
                    if weighed_at(kind, k) is not None:
                        weigh(last_pair, weighed_at(kind, k))
                dve.wait_ge(*s.at("acc", 2 * EXPERTS - 1))
                tt(resid[:, lo], resid[:, lo], acc[:, lo], ALU.add).then_inc(res["out"], 1)
                dve.wait_ge(*s.at("wtd", 2 * EXPERTS))
                chain.wait()
                tt(resid[:, hi], resid[:, hi], wtd[:, 1, :], ALU.add).then_inc(res["out"], 1)

            def cond_input(st):
                s = S[st]
                dve.tensor_copy(nxt[0:64, :].rearrange("p (b i) -> p b i", i=SEQ),
                                sm("condT", p=64).unsqueeze(2).broadcast_to([64, BATCH, SEQ])).then_inc(s["rep"], 1)
                split_input(st)

            def cond(st, prepared):
                s = S[st]
                if not prepared:
                    cond_input(st)
                router_top(st)
                router_mask(st)
                router_weights(st)
                for k in range(2 * COND_CHUNKS + 2):
                    if k < 2 * COND_CHUNKS:
                        r = k % RING
                        dve.wait_ge(*s.at("act", k + 1))
                        if k >= RING:
                            dve.wait_ge(*s.at("hid", k - RING + 1))
                        g = gate32[:, k % 2, :]
                        chain.step(stt(h32[:, r, :], g, 0.01, g, ALU.mult, ALU.max))
                        dve.wait_ge(*s.at("up", k + 1))
                        stt(h32[:, r, :], psum[:, 2 * (k % 2) + 1, :], 1.0 / WSCALE, h32[:, r, :],
                            ALU.mult, ALU.mult).then_inc(s["prod"], 1)
                    if k == 2:
                        router_copy(st)
                    if k >= 2:
                        r = (k - 2) % RING
                        dve.wait_ge(*s.at("high", k - 1))
                        tt(h_lo[:, r, :], h32[:, r, :], h_hi[:, r, :], ALU.subtract).then_inc(s["hid"], 1)

            def layer_norm(st):
                s = S[st]
                for t in range(TILES):
                    if t % 4 == 0:
                        dve.wait_ge(*s.at("tr", t // 4 + 1))
                    chain.done(dve.bn_stats(st6[:, t, :], psum[:, t // 4, (t % 4) * P:(t % 4 + 1) * P]))
                chain.wait()
                for t in range(TILES):
                    last = dve.bn_aggr(mv[:, t, :], st6[:, t, :])
                    chain.done(last)
                chain.wait()
                dve.sem_inc(s["stats"], 1)
                dve.wait_ge(*s.at("sq", 1))
                chain.step(dve.reciprocal(rstd[:, :], sq8[:, :]))
                stt(nmr[:, :], mv[:, :, 0], -1.0, rstd[:, :], ALU.mult, ALU.mult).then_inc(s["inv"], 1)
                for t in range(TILES // 2):
                    ts(tok[:, t, :], psum[:, t // 4, (t % 4) * P:(t % 4 + 1) * P], mv[:, t, 0:1], rstd[:, t:t + 1],
                       ALU.subtract, ALU.mult).then_inc(s["norm"], 1)
                dve.wait_ge(*s.at("back", 2))
                beta = sm(f"{st}_b") if st[:2] == "ln" else None
                ts(DST[st][:, HALF:TOK], psum[:, 3, :], sm(f"{st}_g"), beta, ALU.mult,
                   *([ALU.add] if beta is not None else [])).then_inc(s["out"], 1)

            def attention(st):
                s = S[st]
                layer = int(st[3])
                kv = kbd[:, :].rearrange("p (b q k) -> p b q k", q=2, k=KEYS)
                nk = sm("null_key")
                split_input(st)
                dve.wait_ge(*s.at("zeroed", 1))
                dve.wait_ge(*s.at("k", 2))
                if layer == 1:
                    for p in range(2):
                        r = slice(64 * p, 64 * p + 64)
                        for half in range(2):
                            chain.done(dve.tensor_copy(
                                kv[r, 16 * half:16 * half + 16, p, 0:SEQ],
                                psum[r, half, :].rearrange("p (b k) -> p b k", k=SEQ)))
                        chain.done(dve.tensor_copy(kv[r, :, p, SEQ], nk[r, :].broadcast_to([64, BATCH])))
                    chain.wait()
                    dve.sem_inc(s["kk"], 1)
                else:
                    flat = oT[:, 0:BATCH * KEYS]
                    k33 = flat.rearrange("p (b k) -> p b k", k=KEYS)
                    for half in range(2):
                        chain.done(dve.tensor_copy(k33[:, 16 * half:16 * half + 16, 0:SEQ],
                                                   psum[:, half, :].rearrange("p (b k) -> p b k", k=SEQ)))
                    chain.step(dve.tensor_copy(k33[:, :, SEQ], nk.broadcast_to([P, BATCH])))
                    tt(oT[:, 2 * TOK:2 * TOK + BATCH * KEYS], flat, flat, ALU.mult).then_inc(s["sq"], 1)
                    dve.wait_ge(*s.at("k_sb", 1))
                    nrm = oT[:, 4 * TOK:4 * TOK + BATCH * KEYS]
                    chain.step(ts(nrm, nrm, 1e-12, None, ALU.max))
                    chain.step(dve.reciprocal(nrm, nrm))
                    chain.step(tt(flat, flat, nrm, ALU.mult))
                    chain.step(ts(flat, flat, sm("qs2"), sm("ks2"), ALU.mult, ALU.mult))
                    for p in range(2):
                        r = slice(64 * p, 64 * p + 64)
                        chain.done(dve.tensor_copy(kv[r, :, p, :], k33[r, :, :]))
                    chain.wait()
                    dve.sem_inc(s["kk"], 1)
                dve.wait_ge(*s.at("v", 1))
                vb = vbd[:, :].rearrange("p (t b d) -> p t b d", b=4, d=64)
                for b in range(4):
                    r = slice(32 * b, 32 * b + 32)
                    chain.done(tt(vb[r, :, b, :], psum[r, 2, :].rearrange("p (t d) -> p t d", d=64),
                                  rw("null_value_row")[r, :].unsqueeze(1).broadcast_to([32, TILES, 64]), ALU.subtract))
                chain.wait()
                dve.sem_inc(s["v_sb"], 1)
                rqv = rq[:, :].rearrange("p (g b q) -> p g b q", g=2, q=2)

                if layer == 2:
                    for half in range(2):
                        dve.wait_ge(*s.at("ss", 8 * half + 8))
                        dve.transpose(q2[:, (4 + half) * HALF:(5 + half) * HALF], psum[:, (4, 7)[half], :])\
                            .then_inc(s["ss_rows"], 1)

                def query_scales(half):
                    dve.wait_ge(*s.at("rq", half + 1))
                    r = rq[:, :].rearrange("p (g h x) -> p g h x", g=2, h=2)[:, :, half, :]
                    chain.step(ts(r, r, 1e-12, None, ALU.max))
                    chain.step(dve.reciprocal(r, r))
                    chain.step(ts(r, r, 8.0, None, ALU.mult))

                dve.wait_ge(*s.at("bm", 2 * TILES))
                for t in range(-1, TILES):
                    if t + 1 < TILES:
                        n = t + 1
                        if layer == 2 and n % 4 == 0:
                            query_scales(n // 4)
                        dve.wait_ge(*s.at("sc", n + 1))
                        if n >= 3:
                            dve.wait_ge(*s.at("p", 2 * (n - 3) + 2))
                        for g2 in range(2):
                            sl = s_sb[:, n % 3, g2 * 8 * KEYS:(g2 + 1) * 8 * KEYS]
                            table = bm[:, (2 * n + g2) * 8 * KEYS:(2 * n + g2 + 1) * 8 * KEYS]
                            src = psum[:, (2 * n + g2) % 3, 0:8 * KEYS]
                            if layer == 2:
                                w = rqv[:, g2, 4 * n:4 * n + 4, :].rearrange("p b q -> p (b q)").unsqueeze(2)\
                                    .broadcast_to([P, 8, KEYS])
                                chain.step(tt(sl.rearrange("p (a k) -> p a k", k=KEYS),
                                              src.rearrange("p (a k) -> p a k", k=KEYS), w, ALU.mult))
                                src = sl
                            tt(sl, src, table, ALU.add).then_inc(s["biased"], 1)
                        dve.wait_ge(*s.at("biased", 2 * n + 2))
                        s3 = s_sb[:, n % 3, :].rearrange("p (a k) -> p a k", k=KEYS)
                        dve.reduce_max(red[:, 0, n % 2, :], s3, AX_X).then_inc(s["rowmax"], 1)
                    if 0 <= t < TILES:
                        dve.wait_ge(*s.at("ex", t + 1))
                        if t >= 2:
                            dve.wait_ge(*s.at("p", 2 * (t - 2) + 2))
                        s3 = s_sb[:, t % 3, :].rearrange("p (a k) -> p a k", k=KEYS)
                        total = red[:, 1, t % 2, :]
                        chain.step(dve.reduce_sum(total, s3, AX_X))
                        dve.reciprocal(total, total).then_inc(s["rsum"], 1)

            def self_attention(st):
                s = S[st]
                qm = big[:, 0:4 * TOK].rearrange("p (b h i) -> p h b i", h=4, i=SEQ)
                for half in range(2):
                    dve.wait_ge(*s.at("qkv", 2 * half + 1))
                    for h in range(4):
                        chain.done(ts(qm[:, h, 16 * half:16 * half + 16, :],
                                      psum[:, half, :].rearrange("p (b i) -> p b i", i=SEQ),
                                      sm("bq"), sm("headmask", h, 1), ALU.add, ALU.mult))
                chain.wait()
                dve.sem_inc(s["q_sb"], 1)

                bv = rw("bv").rearrange("p (g h d) -> p g h d", g=4, h=4)
                for t in range(-1, TILES + 2):
                    if t + 1 < TILES:
                        n = t + 1
                        dve.wait_ge(*s.at("sc", n + 1))
                        if n >= 3:
                            dve.wait_ge(*s.at("p", n - 2))
                        s3 = s_sb[:, n % 3, 0:512].rearrange("p (a k) -> p a k", k=SEQ)
                        src = psum[:, n % 2, :].rearrange("p (a k) -> p a k", k=SEQ)
                        chain.step(dve.reduce_max(red[:, 0, n % 2, :], src, AX_X))
                        tt(s3, src, red[:, 0, n % 2, :].unsqueeze(2).broadcast_to([P, 16, SEQ]), ALU.subtract)\
                            .then_inc(s["sub"], 1)
                    if 0 <= t < TILES:
                        dve.wait_ge(*s.at("ex", t + 1))
                        if t >= 2:
                            dve.wait_ge(*s.at("p", t - 1))
                        s3 = s_sb[:, t % 3, 0:512].rearrange("p (a k) -> p a k", k=SEQ)
                        total = red[:, 1, t % 2, :]
                        chain.step(dve.reduce_sum(total, s3, AX_X))
                        dve.reciprocal(total, total).then_inc(s["rsum"], 1)
                    if t >= 2:
                        m = t - 2
                        dve.wait_ge(*s.at("pv", m + 1))
                        for h in range(4):
                            r = slice(32 * h, 32 * h + 32)
                            c = psum[r, 4 + m % 2, :]\
                                .rearrange("p (g b h d) -> p b g h d", g=4, b=4, h=4)[:, :, :, h, :]
                            bias = bv[r, :, h, :].unsqueeze(1).broadcast_to([32, 4, 4, 8])
                            chain.done(tt(tok[r, m, :].rearrange("p (b g d) -> p b g d", b=4, g=4), c, bias, ALU.add))
                        chain.wait()
                        dve.sem_inc(s["c"], 1)
                x = keep[:, :].rearrange("p (t b i) -> p t b i", b=4, i=SEQ)
                for b in range(4):
                    dve.wait_ge(*s.at("wo", b + 1))
                    stt(x[:, :, b, :], psum[:, b, 0:256].rearrange("p (t i) -> p t i", i=SEQ), sm("bo"),
                        x[:, :, b, :], ALU.add, ALU.add).then_inc(s["out"], 1)

            def relative_layer(k):
                n = 63
                a, m, q, r0 = rel[0:n, 4, :], mv[0:n, 0, :], sq8[0:n, 0:1], rstd[0:n, 0:1]
                g_name, b_name = (("relg0", "relb0"), ("relg1", "relb1"))[k]
                if k == 0:
                    chain.step(stt(a, rw("relw0", n), sm("posm", p=n), rw("relb0", n), ALU.mult, ALU.add))
                else:
                    dve.wait_ge(rel_s["m1"], 1)
                    chain.step(tt(a, psum[0:n, 1, 0:P], rw("relb1", n), ALU.add))
                chain.step(dve.bn_stats(st6[0:n, 0, :], a))
                chain.step(dve.bn_aggr(m, st6[0:n, 0, :]))
                dve.sem_inc(rel_s["sq"], 1)
                dve.wait_ge(rel_s["sq"], 2 * k + 2)
                chain.step(dve.reciprocal(r0, q))
                chain.step(ts(a, a, m[:, 0:1], r0, ALU.subtract, ALU.mult))
                tt(a, a, rw(g_name, n), ALU.mult).then_inc(rel_s["si"], 1)
                if k == 0:
                    dve.wait_ge(rel_s["t0"], 1)
                    dve.tensor_copy(rel[:, 1, 0:n], psum[:, 0, 0:n]).then_inc(rel_s["t0s"], 1)
                else:
                    dve.wait_ge(rel_s["t1"], 1)
                    dve.tensor_copy(rel[:, 3, 0:n], psum[:, 6, 0:n]).then_inc(rel_s["t1s"], 1)

            dve.wait_ge(c_small, 16)
            dve.wait_ge(c_rows, 16)
            prepared = use_rel and stages[0][:4] == "cond"
            if use_rel:
                relative_layer(0)
                if prepared:
                    ready(dve, stages[0])
                    cond_input(stages[0])
                relative_layer(1)
            for st in stages:
                if st[:3] == "res":
                    continue
                ready(dve, st)
                s = S[st]
                if st[:4] == "cond":
                    cond(st, prepared and st == stages[0])
                elif st[:3] == "ffn":
                    ffn(st)
                elif st[:3] == "att":
                    attention(st)
                elif st == "self2":
                    self_attention(st)
                else:
                    layer_norm(st)

        @block.scalar
        def _(act):
            chain = Chain(act, act_chain)
            fn = act.activation

            def preload(func):
                chain.step(fn(table_probe[:, :], sm("eps"), func))

            def router(st):
                s = S[st]
                preload(ACT.Exp)
                act.wait_ge(*s.at("lg_sb", 1))
                fn(rt[:, 7, :], rt[:, 2, :], ACT.Exp).then_inc(s["ex"], 1)

            def spread(st, first, n):
                s = S[st]
                scale = 1.0 if st[:4] == "cond" else 1.0 / WSCALE
                for k in range(first, first + n):
                    act.wait_ge(*s.at("spread", k + 1))
                    fn(big[:, k * HALF:(k + 1) * HALF], psum[:, 6 + k % 2, :], ACT.Copy, scale=scale)\
                        .then_inc(s["spread_sb"], 1)

            def halves_free(st):
                users = [u for u in weight_users() if stages.index(u) < stages.index(st)]
                if users:
                    u = users[-1]
                    act.wait_ge(*S[u].at("down", ffn_steps(u)))
                    if u[:3] == "ffn":
                        act.wait_ge(*S[u].at("wtd", 2 * EXPERTS))

            def high_half(st, slot, part, i):
                s = S[st]
                kind = FFN_KINDS[int(st[3])]
                n, cols = expert_cols(kind)
                base, bias = slot * STAGE_COLS, slot * 12
                lo, hi = part_cols(kind, part)
                if part == "up":
                    act.wait_ge(*s.at(f"w_dma{slot}", 16 * (i + 1)))
                    if kind["gated"]:
                        c = kind["chunks"]
                        chain.done(fn(w_bias[:, bias + 1:bias + 1 + c], w_stage[:, base + n + 1:base + n + 1 + c],
                                      ACT.Copy, scale=WSCALE))
                        chain.done(fn(w_bias[:, bias + 1 + c:bias + 1 + 2 * c],
                                      w_stage[:, base + n + 1 + c:base + n + 1 + 2 * c], ACT.Copy))
                    else:
                        chain.done(fn(w_bias[:, bias + 1:bias + cols - n], w_stage[:, base + n + 1:base + cols],
                                      ACT.Copy))
                else:
                    chain.done(fn(w_bias[:, bias:bias + 1], w_stage[:, base + n:base + n + 1], ACT.Copy, scale=WSCALE))
                chain.step(fn(w_stage[:, base + lo:base + hi], w_stage[:, base + lo:base + hi], ACT.Copy, scale=WSCALE))
                fn(w_hi[:, slot * 1024 + lo:slot * 1024 + hi], w_stage[:, base + lo:base + hi], ACT.Copy)\
                    .then_inc(s[f"w_hi{slot}"], 1)

            def ffn(st):
                s = S[st]
                kind = FFN_KINDS[int(st[3])]
                C, gated = kind["chunks"], kind["gated"]
                per = 4 * C
                pairs = EXPERTS // 2

                def split_part(slot, part, i, nxt):
                    if part == "up":
                        act.wait_ge(*s.at("up", per * i + 2 * C * nxt))
                        act.wait_ge(*s.at("act", per * i + 2 * C * nxt))
                        if gated:
                            act.wait_ge(*s.at("prod", per * i + 2 * C * nxt))
                    else:
                        ahead = nxt if slot == 0 and nxt else slot - 1
                        act.wait_ge(*s.at("down", per * i + 2 * C * ahead))
                        act.wait_ge(*s.at("wtd", 4 * i + 2 * ahead))
                    high_half(st, slot, part, i + nxt)

                def high_of_product(i, k):
                    r = k % RING
                    act.wait_ge(*s.at("prod", per * i + k + 1))
                    act.wait_ge(*s.at("down", per * i + k - RING + 1))
                    fn(h_hi[:, r, :], h32[:, r, :], ACT.Copy, scale=1.0 / WSCALE).then_inc(s["high"], 1)

                def pair(i, first=False, last=False):
                    done = 0
                    for k in range(per):
                        slot, c = k // (2 * C), k % C
                        act.wait_ge(*s.at("gate" if gated else "up", per * i + k + 1))
                        b = slot * 12 + 1 + c + (C if gated else 0)
                        if gated:
                            act.wait_ge(*s.at("prod", per * i + k - 1))
                            dst, bank = gate32[:, k % 2, :], 2 * (k % 2)
                        else:
                            act.wait_ge(*s.at("hid", per * i + k - RING + 1))
                            dst, bank = h32[:, k % RING, :], k % 4
                        fn(dst, psum[:, bank, :], kind["func"], bias=w_bias[:, b:b + 1], scale=1.0 / WSCALE)\
                            .then_inc(s["act"], 1)
                        if first and k >= at["spread"] and done < 2 * EXPERTS:
                            n = min(at["pieces"], 2 * EXPERTS - done)
                            spread(st, done, n)
                            done += n
                        if gated and (not first or k):
                            high_of_product(i, k - 1)
                        for split_slot, part, nxt in splits_at(kind, k, first, last):
                            split_part(split_slot, part, i, nxt)

                at = interleave(st)
                links = sum(3 if gated and part == "up" else 2 for _, _, part, _ in splits(kind))
                router(st)
                pair(0, first=True)
                base_n = chain.n
                with act.Fori(1, pairs - 1) as i:
                    chain.n = base_n + (i - 1) * links
                    pair(i)
                chain.n = base_n + (pairs - 2) * links
                pair(pairs - 1, last=True)
                if gated:
                    high_of_product(pairs - 1, per - 1)

            def cond(st, with_table):
                s = S[st]
                router(st)
                for k in range(2 * COND_CHUNKS + 2):
                    if k < 2 * COND_CHUNKS:
                        act.wait_ge(*s.at("gate", k + 1))
                        if k >= 2:
                            act.wait_ge(*s.at("prod", k - 1))
                        fn(gate32[:, k % 2, :], psum[:, 2 * (k % 2), :], ACT.Copy, scale=1.0 / WSCALE)\
                            .then_inc(s["act"], 1)
                    if with_table and k == TABLE_STEP:
                        relative_table()
                    if k in COND_SPREAD:
                        first, end = COND_SPREAD[k]
                        spread(st, first, end - first)
                    if k >= 2:
                        j = k - 2
                        if j < 2:
                            act.wait_ge(*s.at("prod", j + 1))
                        else:
                            act.wait_ge(*s.at("weighed", j - 1))
                        if j >= RING:
                            act.wait_ge(*s.at("down", j - RING + 1))
                        fn(h_hi[:, j % RING, :], h32[:, j % RING, :], ACT.Copy).then_inc(s["high"], 1)
                for half in range(2):
                    act.wait_ge(*s.at("down", 2 * COND_CHUNKS - 1 + half))
                    fn(DST[st][:, half * HALF:(half + 1) * HALF], psum[:, 4 + half, :], ACT.Copy,
                       scale=1.0 / WSCALE).then_inc(s["out"], 1)

            def layer_norm(st):
                s = S[st]
                preload(ACT.Sqrt)
                act.wait_ge(*s.at("stats", 1))
                fn(sq8[:, :], mv[:, :, 1], ACT.Sqrt, bias=sm("eps")).then_inc(s["sq"], 1)
                act.wait_ge(*s.at("inv", 1))
                for t in range(TILES // 2, TILES):
                    fn(tok[:, t, :], psum[:, t // 4, (t % 4) * P:(t % 4 + 1) * P], ACT.Identity,
                       bias=nmr[:, t:t + 1], scale=rstd[:, t:t + 1]).then_inc(s["norm_act"], 1)
                act.wait_ge(*s.at("back", 1))
                kw = dict(bias=sm(f"{st}_b")) if st[:2] == "ln" else {}
                fn(DST[st][:, 0:HALF], psum[:, 2, :], ACT.Identity, scale=sm(f"{st}_g"), **kw).then_inc(s["out"], 1)

            def attention(st):
                s = S[st]
                layer = int(st[3])
                q = big[:, :].rearrange("p (g b h i) -> p g h b i", g=2, h=4, i=SEQ)

                def query_roots(half):
                    act.wait_ge(*s.at("ss_rows", half + 1))
                    r = rq[:, :].rearrange("p (g b q) -> p g q b", g=2, q=2)[:, :, :, 16 * half:16 * half + 16]
                    rows = q2[:, (4 + half) * HALF:(5 + half) * HALF].rearrange("p (b x) -> p x b", x=SEQ)
                    fn(r, rows[:, 0:4, :].rearrange("p (g q) b -> p g q b", g=2), ACT.Sqrt).then_inc(s["rq"], 1)

                for k, (half, g2, h4) in enumerate(Q_ORDER):
                    act.wait_ge(*s.at("q", k + 1))
                    if layer == 2:
                        if k >= 4:
                            act.wait_ge(*s.at("ss", k - 3))
                        fn(q2[:, (k % 4) * HALF:(k % 4 + 1) * HALF], psum[:, Q_BANKS[k % 3], :], ACT.Square,
                           scale=1.0 / WSCALE)\
                            .then_inc(s["q2"], 1)
                    fn(q[:, g2, h4, 16 * half:16 * half + 16, :],
                       psum[:, Q_BANKS[k % 3], :].rearrange("p (b i) -> p b i", i=SEQ), ACT.Copy,
                       scale=(0.125 if layer == 1 else 1.0) / WSCALE).then_inc(s["q_sb"], 1)
                    if layer == 2 and k == 6:
                        act.wait_ge(*s.at("ssq", 1))
                        for n in range(3):
                            chain.done(fn(oT[:, 4 * TOK + n * 352:4 * TOK + (n + 1) * 352],
                                          psum[:, (0, 1, 7)[n], 0:352], ACT.Sqrt))
                        chain.wait()
                        act.sem_inc(s["k_sb"], 1)
                if layer == 2:
                    query_roots(0)
                    query_roots(1)
                preload(ACT.Exp)
                for t in range(-1, TILES + 1):
                    if t + 1 < TILES:
                        act.wait_ge(*s.at("sub", t + 2))
                        e = s_sb[:, (t + 1) % 3, :]
                        fn(e, e, ACT.Exp).then_inc(s["ex"], 1)
                    if 0 <= t < TILES:
                        act.wait_ge(*s.at("pt", t + 1))
                        if t >= 2:
                            act.wait_ge(*s.at("pv", 2 * t - 2))
                        fn(pT[:, t % 2, :], psum[:, 7, :], ACT.Copy).then_inc(s["pt_sb"], 1)
                    if t >= 1:
                        act.wait_ge(*s.at("pv", 2 * t))
                        o = oT[:, :].rearrange("p (t m b g x) -> p t m b g x", t=TILES, m=2, b=2, g=2)
                        for b in range(2):
                            for par in range(2):
                                r, to = slice(64 * b, 64 * b + 64), slice(64 * par, 64 * par + 64)
                                b0 = 3 + 2 * ((t - 1) % 2)
                                src = psum[r, b0:b0 + 2, :]\
                                    .rearrange("p m (g q x) -> p m g q x", g=2, q=2)[:, :, :, par, :]
                                fn(o[to, t - 1, :, b, :, :], src, ACT.Identity, bias=sm("null_value")[r, :])\
                                    .then_inc(s["o"], 1)
                for half in range(2):
                    act.wait_ge(*s.at("wo", half + 1))
                    fn(DST[st][:, half * HALF:(half + 1) * HALF], psum[:, half, :], ACT.Copy).then_inc(s["out"], 1)
                if layer == 1 and "att2" in stages:
                    act.wait_ge(*s.at("wo", 2))
                    act.dma_start(att_w[:, :], dram["att2_w"]).then_inc(c_attw2, 16)

            def self_attention(st):
                s = S[st]
                km = q2[:, :].rearrange("p (g t) -> p g t", g=4)
                act.wait_ge(*s.at("zeroed", 1))
                for half in range(2):
                    act.wait_ge(*s.at("qkv", 2 * half + 2))
                    for g in range(4):
                        r = slice(32 * g, 32 * g + 32)
                        chain.done(fn(km[r, g, half * HALF:(half + 1) * HALF], psum[r, 2 + half, :], ACT.Identity,
                                      bias=sm("bk")[r, :]))
                chain.wait()
                act.sem_inc(s["k_sb"], 1)
                preload(ACT.Exp)

                def values(half):
                    act.wait_ge(*s.at("qkv", 5))
                    vb = vself.rearrange("p (t g b d) -> p t g b d", g=4, b=4, d=32)
                    for b in range(4):
                        r = slice(32 * b, 32 * b + 32)
                        src = psum[r, 4 + half, :].rearrange("p (t g d) -> p t g d", g=4, d=32)
                        chain.done(fn(vb[r, 4 * half:4 * half + 4, :, b, :], src, ACT.Copy))
                    chain.wait()
                    act.sem_inc(s["v_sb"], 1)

                for t in range(-1, TILES + 3):
                    if t + 1 < TILES:
                        act.wait_ge(*s.at("sub", t + 2))
                        e = s_sb[:, (t + 1) % 3, 0:512]
                        fn(e, e, ACT.Exp, scale=float(8.0 ** -0.5)).then_inc(s["ex"], 1)
                    if t < 1:
                        values(t + 1)
                    if 0 <= t < TILES:
                        act.wait_ge(*s.at("pt", t + 1))
                        if t >= 2:
                            act.wait_ge(*s.at("pv", t - 1))
                        fn(pT[:, t % 2, :], psum[:, 2 + t % 2, :], ACT.Copy).then_inc(s["pt_sb"], 1)
                    if t >= 3:
                        m = t - 3
                        act.wait_ge(*s.at("ct", m + 1))
                        fn(oT[:, m * P:(m + 1) * P], psum[:, 6 + m % 2, 0:P], ACT.Copy).then_inc(s["ct_sb"], 1)

            def relative_layer(k):
                n = 63
                preload(ACT.Sqrt)
                act.wait_ge(rel_s["sq"], 2 * k + 1)
                fn(sq8[0:n, 0:1], mv[0:n, 0, 1:2], ACT.Sqrt, bias=sm("eps", p=n)).then_inc(rel_s["sq"], 1)
                preload(ACT.Silu)
                act.wait_ge(rel_s["si"], k + 1)
                fn(rel[0:n, 2 * k, :], rel[0:n, 4, :], ACT.Silu).then_inc(rel_s["h1" if k else "h0"], 1)

            def relative_table():
                act.wait_ge(rel_s["m2"], 1)
                for part in range(2):
                    fn(relT[:, part * HALF:(part + 1) * HALF], psum[0:16, 4 + part, :], ACT.Identity,
                       bias=sm("relb2", p=16)).then_inc(rel_s["sb"], 1)

            def first_split(st, k):
                if st[:4] == "cond":
                    act.wait_ge(*S[st].at("w_dma0", 16))
                    lo, hi = COND_PARTS[k]
                    chain.step(fn(w_stage[:, lo:hi], w_stage[:, lo:hi], ACT.Copy, scale=WSCALE))
                    fn(w_hi[:, lo:hi], w_stage[:, lo:hi], ACT.Copy).then_inc(S[st]["w_hi0"], 1)
                else:
                    high_half(st, 0, ("up", "down")[k], 0)

            act.wait_ge(c_small, 16)
            if use_rel:
                relative_layer(0)
                if family(stages[0]) != "moe":
                    relative_layer(1)
                    relative_table()
            for st in stages:
                if st[:3] == "res":
                    continue
                if st in ("pre1", "pre2"):
                    a = S[f"att{st[3]}"]
                    halves_free(st)
                    act.wait_ge(c_attw1 if st == "pre1" else c_attw2, 16)
                    chain.step(fn(att_w[:, 0:TOK], att_w[:, 0:TOK], ACT.Copy, scale=WSCALE))
                    fn(w_hi[:, 0:TOK], att_w[:, 0:TOK], ACT.Copy).then_inc(a["wq_hi"], 1)
                if family(st) == "moe":
                    halves_free(st)
                    with_rel = use_rel and st == stages[0]
                    first_split(st, 0)
                    if with_rel:
                        relative_layer(1)
                    first_split(st, 1)
                    if with_rel and st[:4] != "cond":
                        relative_table()
                ready(act, st)
                if st[:4] == "cond":
                    cond(st, use_rel and st == stages[0])
                elif st[:3] == "ffn":
                    ffn(st)
                elif st[:3] == "att":
                    attention(st)
                elif st == "self2":
                    self_attention(st)
                else:
                    layer_norm(st)


def constants():
    c = {}
    c["ident"] = np.eye(P)
    c["iota"] = np.tile(np.arange(8.0), (P, 1))
    c["eps"] = np.full((P, 1), LN_EPS)
    c["headmask"] = ((np.arange(P)[:, None] % 32) // 8 == np.arange(4)[None, :])
    c["headsel"] = np.arange(HEADSEL + P)[None, :] == HEADSEL + np.arange(P)[:, None] // 64
    c["ones_block"] = (np.arange(P)[:, None] // 64 == np.arange(P)[None, :] // 64)
    future = np.arange(SEQ)[None, :] > (np.arange(P) % SEQ)[:, None]
    causal = np.zeros((P, 4, KEYS))
    causal[:, :, 0:SEQ] = np.where(future, MASKED, 0.0)[:, None, :]
    c["causal"] = causal.reshape(P, 4 * KEYS)
    pos = np.zeros((P, 1))
    pos[0:63, 0] = 31.0 - np.arange(63)
    c["posm"] = pos
    c["ones_row"] = np.ones((P, P))
    return c


def lay_out(i):
    f = np.float32

    def a(name):
        return np.asarray(i[name])

    def col(v):
        return v.reshape(-1, 1)

    def full(v, n=1):
        v = v.reshape(-1, n) if v.ndim == 1 else v
        o = np.zeros((P, v.shape[1]), f)
        o[0:v.shape[0]] = v
        return o

    s = constants()
    cond = a("cond_64")
    twice = lambda v: col(np.concatenate([v, v]))
    for layer in (0, 3):
        s[f"cond{layer}_router"] = a(f"L{layer}_cond_wt").T
        s[f"cond{layer}_wg"] = full(a(f"L{layer}_cond_wg").T)
    s["ffn0_router"] = a("L0_ffn_w_gate")
    s["ffn1_router"] = a("L1_ffn_gate_w").T
    s["ffn2_router"] = a("L2_ffn_w_gate")
    s["ffn3_router"] = a("L3_ffn_router_w").T
    s["condT"] = full(cond.T)
    s["ffn0_brow"] = np.tile(a("L0_ffn_b_gate"), (P, 1))
    s["pre1_g"], s["post1_g"] = col(a("L1_cond_g_in")), col(a("L1_cond_g_out"))
    s["pre2_g"], s["post2_g"] = col(a("L2_cond_g_norm")), col(a("L2_cond_g_out"))
    for n in (1, 2):
        s[f"ln{n}_g"], s[f"ln{n}_b"] = col(a(f"L2_ffn_ln{n}_w")), col(a(f"L2_ffn_ln{n}_b"))
    s["null_key"], s["null_value"] = twice(cond[0]), twice(cond[1])
    s["qs2"], s["ks2"] = twice(a("L2_cond_q_scale")), twice(a("L2_cond_k_scale"))
    bqkv = a("L2_ffn_b_qkv")
    s["bq"], s["bk"], s["bo"] = col(bqkv[0:P]), col(bqkv[P:2 * P]), col(a("L2_ffn_b_o"))
    s["relw1"] = a("L2_cond_w1")
    heads = np.array([8 * g2 + 2 * h4 + p for h4 in range(4) for g2 in range(2) for p in range(2)])
    s["relw2"] = a("L2_cond_w2")[:, heads]
    s["relb2"] = full(a("L2_cond_b2")[heads])
    small = np.zeros((P, N_SMALL), f)
    for name, (at, n) in SMALL.items():
        small[:, at:at + n] = s[name]

    r = {"relw0": a("L2_cond_w0").reshape(-1), "relb0": a("L2_cond_b0"), "relg0": a("L2_cond_g0"),
         "relb1": a("L2_cond_b1"), "relg1": a("L2_cond_g1"), "null_value_row": cond[1], "bv": bqkv[2 * P:]}
    rows = np.concatenate([r[n] for n in ROWS]).reshape(1, N_ROWS)

    d = {"small": small, "rows": rows}
    d["xT"] = a("x").reshape(TOK, P).T
    d["ident16"] = np.eye(P, dtype=np.float16)
    sel = np.zeros((16, 12, P), np.float16)
    for e in range(EXPERTS):
        sel[[e, e + 8], e, :] = 1
        sel[[e, e + 8], 8 + e // 2, 64 * (e % 2):64 * (e % 2) + 64] = 1
    d["sel16"] = sel.reshape(16, 12 * P)
    d["mask"] = np.stack([a("mask_BxS_bk0"), a("mask_BxS_bf1")]).reshape(1, 2 * TOK)
    brow = np.zeros((4, SEQ, 2, 4, KEYS), f)
    hh = heads.reshape(4, 4)
    brow[:, :, 0, :, 0:SEQ] = a("fside_16xSxS_0")[hh].transpose(0, 2, 1, 3)
    for layer in (1, 2):
        brow[:, :, layer - 1, :, SEQ] = a(f"L{layer}_cond_null_attn_bias")[hh][:, None, :]
    d["brow"] = brow.reshape(P, 2 * 4 * KEYS)
    for layer in (0, 3):
        L = f"L{layer}_cond_"
        w = np.zeros((P, COND_CHUNKS, 3, P), f)
        w[:, 0, 0], w[:, 0, 1], w[:, 0, 2] = a(L + "sw_gate"), a(L + "sw_up"), a(L + "sw_down")
        w[:, 1:, 0] = a(L + "w_gate").transpose(1, 0, 2).reshape(P, 4, P)
        w[:, 1:, 1] = a(L + "w_up").transpose(1, 0, 2).reshape(P, 4, P)
        w[:, 1:, 2] = a(L + "w_down").reshape(4, P, P).transpose(1, 0, 2)
        d[f"cond{layer}_w"] = w.reshape(P, COND_COLS)

    def expert_blocks(ups, down, biases, bdown):
        F = down.shape[1]
        c = F // P
        parts = list(ups) + [down.reshape(EXPERTS, c, P, P).transpose(0, 2, 1, 3).reshape(EXPERTS, P, c * P)]
        parts.append(bdown[:, :, None])
        parts += [b.reshape(EXPERTS, c, P).transpose(0, 2, 1) for b in biases]
        return np.concatenate(parts, axis=2)

    d["ffn0_w"] = expert_blocks([a("L0_ffn_W1")], a("L0_ffn_W2"), [a("L0_ffn_b1")], a("L0_ffn_b2"))
    d["ffn1_w"] = expert_blocks([a("L1_ffn_w1").transpose(1, 2, 0)], a("L1_ffn_w2").transpose(1, 2, 0),
                                [a("L1_ffn_b1")], a("L1_ffn_b2"))
    d["ffn2_w"] = expert_blocks([a("L2_ffn_w1")], a("L2_ffn_w2"), [a("L2_ffn_b1")], a("L2_ffn_b2"))
    d["ffn3_w"] = expert_blocks([a("L3_ffn_gate_w"), a("L3_ffn_up_w")], a("L3_ffn_down_w"),
                                [a("L3_ffn_up_b"), a("L3_ffn_gate_b")], a("L3_ffn_down_b"))
    for layer, wo in ((1, "Wo"), (2, "Wout")):
        L = f"L{layer}_cond_"
        kv = a(L + "Wkv")
        o = a(L + wo).reshape(8, P, P).transpose(1, 0, 2).reshape(P, 8 * P)
        d[f"att{layer}_w"] = np.concatenate(
            [a(L + "Wq"), kv[:, 0:64], kv[:, 0:64], kv[:, 64:], o], axis=1)
    wo = a("L2_ffn_w_o").reshape(4, 4, 8, P).transpose(0, 2, 1, 3).reshape(32, 4 * P)
    d["self_w"] = np.concatenate([a("L2_ffn_w_qkv"), np.concatenate([wo] * 4)], axis=1)
    return {k: np.ascontiguousarray(v) for k, v in d.items()}


def make(nc, arrays, stages=None):
    dram = {}
    for name, v in arrays.items():
        dram[name] = nc.dram_tensor(f"in_{name}", v.shape, mybir.dt.from_np(v.dtype), kind="ExternalInput").ap()
    out = nc.dram_tensor("out_xT", (P, TOK), F32, kind="ExternalOutput").ap()
    build_program(nc, dram, out, stages)


def kernel(**inputs):
    import concourse.bacc as bacc
    from concourse.bass_utils import run_bass_kernel_spmd

    arrays = lay_out(inputs)
    nc = bacc.Bacc("TRN2", target_bir_lowering=False, num_devices=1)
    make(nc, arrays)
    r = run_bass_kernel_spmd(nc, [{f"in_{k}": v for k, v in arrays.items()}], core_ids=[0])
    return np.ascontiguousarray(np.asarray(r.results[0]["out_xT"]).T).reshape(BATCH, SEQ, P)
```
